# Optimizing a Trainium2 kernel written in Bass

```python
import numpy as np
import jax
import jax.numpy as jnp

def _softmax(x, axis=-1):
    return jax.nn.softmax(x, axis=axis)

def _gelu(x):
    return jax.nn.gelu(x, approximate=True)

def _silu(x):
    return jax.nn.silu(x)

def _sigmoid(x):
    return jax.nn.sigmoid(x)

def _layernorm(x, axis=-1, eps=1e-05):
    m = jnp.mean(x, axis=axis, keepdims=True)
    v = jnp.var(x, axis=axis, keepdims=True)
    return (x - m) / jnp.sqrt(v + eps)

def _scatter_add(tgt, idx, src, axis=0):
    return tgt.at[idx].add(src)

def _segment_sum(src, seg, n):
    return jax.ops.segment_sum(src, seg, n)
kernel_name = 'mk_sandwich_d1_jaxref_r8_d74506'

def setup_inputs(seed: int=0):
    np.random.seed(seed)
    _w = jnp.asarray

    def _L0_attn_setup():
        import jax, jax.numpy as jnp
        import numpy as np
        B, L, D, H = (2, 256, 128, 16)
        C = D // H
        SCALE = 1.0 / np.sqrt(D).astype(np.float32)
        key = jax.random.key(seed)
        ks = jax.random.split(key, 5)
        return {'x': jax.random.normal(ks[0], (B, L, D), dtype=jnp.float32), 'w_qkv': jax.random.normal(ks[1], (3 * D, D), dtype=jnp.float32) * (1.0 / np.sqrt(D)), 'b_qkv': jax.random.normal(ks[2], (3 * D,), dtype=jnp.float32) * 0.02, 'w_o': jax.random.normal(ks[3], (D, D), dtype=jnp.float32) * (1.0 / np.sqrt(D)), 'b_o': jax.random.normal(ks[4], (D,), dtype=jnp.float32) * 0.02}
    _L0_attn_in = _L0_attn_setup()

    def _L0_ffn_setup():
        import jax, jax.numpy as jnp
        import numpy as np
        D = 128
        H = 4
        DF = 512
        E = 8
        EPS = 1e-05

        def _layer_norm(x, g, b):
            mu = jnp.mean(x, axis=-1, keepdims=True)
            var = jnp.mean(jnp.square(x - mu), axis=-1, keepdims=True)
            return (x - mu) * jax.lax.rsqrt(var + EPS) * g + b

        def _mha(x, Wqkv, bqkv, Wo, bo):
            S, B, _ = x.shape
            hd = D // H
            qkv = x @ Wqkv.T + bqkv
            q, k, v = jnp.split(qkv, 3, axis=-1)
            to_heads = lambda t: t.reshape(S, B, H, hd).transpose(1, 2, 0, 3)
            q, k, v = (to_heads(q), to_heads(k), to_heads(v))
            scores = jnp.einsum('bhqd,bhkd->bhqk', q, k) * (1.0 / np.sqrt(hd))
            att = jax.nn.softmax(scores, axis=-1)
            o = jnp.einsum('bhqk,bhkd->bhqd', att, v)
            o = o.transpose(2, 0, 1, 3).reshape(S, B, D)
            return o @ Wo.T + bo

        def _moe(x, Wg, W1, b1, W2, b2):
            S, B, _ = x.shape
            xf = x.reshape(S * B, D)
            logits = xf @ Wg.T
            idx = jnp.argmax(logits, axis=-1)
            out = jnp.zeros_like(xf)
            for e in range(E):
                m = (idx == e)[:, None].astype(xf.dtype)
                h = jax.nn.relu(xf @ W1[e] + b1[e])
                out = out + m * (h @ W2[e] + b2[e])
            return out.reshape(S, B, D)
        key = jax.random.key(seed)
        ks = jax.random.split(key, 16)
        S, B = (64, 8)
        s = lambda k, shape, fan: jax.random.normal(k, shape, jnp.float32) * (1.0 / np.sqrt(fan))
        return {'x': jax.random.normal(ks[0], (S, B, D), jnp.float32), 'Wqkv': s(ks[1], (3 * D, D), D), 'bqkv': jnp.zeros((3 * D,), jnp.float32), 'Wo': s(ks[2], (D, D), D), 'bo': jnp.zeros((D,), jnp.float32), 'g1': jnp.ones((D,), jnp.float32), 'be1': jnp.zeros((D,), jnp.float32), 'g2': jnp.ones((D,), jnp.float32), 'be2': jnp.zeros((D,), jnp.float32), 'Wg': s(ks[3], (E, D), D), 'W1': s(ks[4], (E, D, DF), D), 'b1': jnp.zeros((E, DF), jnp.float32), 'W2': s(ks[5], (E, DF, D), DF), 'b2': jnp.zeros((E, D), jnp.float32)}
    _L0_ffn_in = _L0_ffn_setup()
    _d = {'L0_attn_x': _L0_attn_in['x'], 'L0_attn_w_qkv': _L0_attn_in['w_qkv'], 'L0_attn_b_qkv': _L0_attn_in['b_qkv'], 'L0_attn_w_o': _L0_attn_in['w_o'], 'L0_attn_b_o': _L0_attn_in['b_o'], 'L0_ffn_Wqkv': _L0_ffn_in['Wqkv'], 'L0_ffn_bqkv': _L0_ffn_in['bqkv'], 'L0_ffn_Wo': _L0_ffn_in['Wo'], 'L0_ffn_bo': _L0_ffn_in['bo'], 'L0_ffn_g1': _L0_ffn_in['g1'], 'L0_ffn_be1': _L0_ffn_in['be1'], 'L0_ffn_g2': _L0_ffn_in['g2'], 'L0_ffn_be2': _L0_ffn_in['be2'], 'L0_ffn_Wg': _L0_ffn_in['Wg'], 'L0_ffn_W1': _L0_ffn_in['W1'], 'L0_ffn_b1': _L0_ffn_in['b1'], 'L0_ffn_W2': _L0_ffn_in['W2'], 'L0_ffn_b2': _L0_ffn_in['b2']}
    _x0 = _d['L0_attn_x']
    _d['L0_attn_x'] = jax.random.normal(jax.random.fold_in(jax.random.key(seed), 1), (16, 256, 128), dtype=_x0.dtype)
    del _x0
    return _d

def reference(L0_attn_x, L0_attn_w_qkv, L0_attn_b_qkv, L0_attn_w_o, L0_attn_b_o, L0_ffn_Wqkv, L0_ffn_bqkv, L0_ffn_Wo, L0_ffn_bo, L0_ffn_g1, L0_ffn_be1, L0_ffn_g2, L0_ffn_be2, L0_ffn_Wg, L0_ffn_W1, L0_ffn_b1, L0_ffn_W2, L0_ffn_b2):

    def _L0_attn_ref(x, w_qkv, b_qkv, w_o, b_o):
        import jax, jax.numpy as jnp
        import numpy as np
        B, L, D, H = (2, 256, 128, 16)
        C = D // H
        SCALE = 1.0 / np.sqrt(D).astype(np.float32)
        b, l, d = x.shape
        h, c = (H, d // H)
        qkv = jnp.einsum('bld,ed->ble', x, w_qkv) + b_qkv
        q, k, v = jnp.split(qkv, 3, axis=-1)
        q = q.reshape(b, l, h, c)
        k = k.reshape(b, l, h, c)
        v = v.reshape(b, l, h, c)
        attn = jax.nn.softmax(jnp.einsum('blhc,bmhc->bhlm', q, k) * SCALE, axis=-1)
        heads = jnp.einsum('bhlm,bmhc->blhc', attn, v).reshape(b, l, d)
        return jnp.einsum('bld,ed->ble', heads, w_o) + b_o + x

    def _L0_ffn_ref(x, Wqkv, bqkv, Wo, bo, g1, be1, g2, be2, Wg, W1, b1, W2, b2):
        import jax, jax.numpy as jnp
        import numpy as np
        D = 128
        H = 4
        DF = 512
        E = 8
        EPS = 1e-05

        def _layer_norm(x, g, b):
            mu = jnp.mean(x, axis=-1, keepdims=True)
            var = jnp.mean(jnp.square(x - mu), axis=-1, keepdims=True)
            return (x - mu) * jax.lax.rsqrt(var + EPS) * g + b

        def _mha(x, Wqkv, bqkv, Wo, bo):
            S, B, _ = x.shape
            hd = D // H
            qkv = x @ Wqkv.T + bqkv
            q, k, v = jnp.split(qkv, 3, axis=-1)
            to_heads = lambda t: t.reshape(S, B, H, hd).transpose(1, 2, 0, 3)
            q, k, v = (to_heads(q), to_heads(k), to_heads(v))
            scores = jnp.einsum('bhqd,bhkd->bhqk', q, k) * (1.0 / np.sqrt(hd))
            att = jax.nn.softmax(scores, axis=-1)
            o = jnp.einsum('bhqk,bhkd->bhqd', att, v)
            o = o.transpose(2, 0, 1, 3).reshape(S, B, D)
            return o @ Wo.T + bo

        def _moe(x, Wg, W1, b1, W2, b2):
            S, B, _ = x.shape
            xf = x.reshape(S * B, D)
            logits = xf @ Wg.T
            idx = jnp.argmax(logits, axis=-1)
            out = jnp.zeros_like(xf)
            for e in range(E):
                m = (idx == e)[:, None].astype(xf.dtype)
                h = jax.nn.relu(xf @ W1[e] + b1[e])
                out = out + m * (h @ W2[e] + b2[e])
            return out.reshape(S, B, D)
        y = _layer_norm(x + _mha(x, Wqkv, bqkv, Wo, bo), g1, be1)
        z = _layer_norm(y + _moe(y, Wg, W1, b1, W2, b2), g2, be2)
        return z
    x = L0_attn_x
    x = x + _layernorm(_L0_attn_ref(_layernorm(x, axis=-1), L0_attn_w_qkv, L0_attn_b_qkv, L0_attn_w_o, L0_attn_b_o), axis=-1)
    x = x + _layernorm(_L0_ffn_ref(_layernorm(x, axis=-1), L0_ffn_Wqkv, L0_ffn_bqkv, L0_ffn_Wo, L0_ffn_bo, L0_ffn_g1, L0_ffn_be1, L0_ffn_g2, L0_ffn_be2, L0_ffn_Wg, L0_ffn_W1, L0_ffn_b1, L0_ffn_W2, L0_ffn_b2), axis=-1)
    return x

_drawn_inputs = setup_inputs


def setup_inputs(seed=0):
    import zlib

    import numpy as np

    out = dict(_drawn_inputs(seed))
    spreads = {'L0_ffn_bqkv': (0.0, 0.1),
     'L0_ffn_bo': (0.0, 0.1),
     'L0_ffn_g1': (1.0, 0.2),
     'L0_ffn_be1': (0.0, 0.1),
     'L0_ffn_g2': (1.0, 0.2),
     'L0_ffn_be2': (0.0, 0.1),
     'L0_ffn_b1': (0.0, 0.417),
     'L0_ffn_b2': (0.0, 0.296)}
    factors = {}
    for name, (base, spread) in spreads.items():
        noise = np.random.default_rng([zlib.crc32(name.encode()), seed]).standard_normal(out[name].shape)
        drawn = base * np.exp(spread * noise) if base else spread * noise
        out[name] = jnp.asarray(drawn.astype(out[name].dtype))
    for name, factor in factors.items():
        out[name] = (out[name] * factor).astype(out[name].dtype)
    return out
```

```python
from contextlib import ExitStack

import concourse.bass as bass
from concourse import mybir

F32 = mybir.dt.float32
BF16 = mybir.dt.bfloat16
I32 = mybir.dt.int32
ALU = mybir.AluOpType
ACT = mybir.ActivationFunctionType
AX = mybir.AxisListType

P = 128
B1, L1 = 16, 256
H1, C1 = 16, 8
SCALE1 = 1.0 / float(P) ** 0.5
EPS = 1e-5
NT = B1 * L1 // P
Q_PART = (0, 0, 1, 1, 0, 2)
K_PART = (0, 1, 0, 1, 2, 0)
NPROD = len(Q_PART)
MAX_ROW = 96
HALF = 8
AHEAD = 4
LAST = B1 - 1


def count(value):
    return max(value, 0) if isinstance(value, int) else value


def first_layer(nc, x, w_qkv, b_qkv, w_o, b_o, ident, identh, minus_half, xs):
    with ExitStack() as ctx:
        def sb(name, shape, dt=F32):
            return ctx.enter_context(nc.sbuf_tensor(name, shape, dt))

        def pb(name, shape, dt=F32):
            return ctx.enter_context(nc.psum_tensor(name, shape, dt))

        def sem(name):
            return ctx.enter_context(nc.semaphore(name))

        w_nat = sb("w_nat", [P, 4, P])
        wT = sb("wT", [P, 4, P])
        b_col = sb("b_col", [P, 2])
        bv_col = sb("bv_col", [P, 1])
        one_pair = sb("one_pair", [P, 1])
        bo_row = sb("bo_row", [P, P])
        x_all = sb("x_all", [P, NT, P])
        xnb_all = sb("xnb_all", [P, NT, P])
        xin = sb("xin", [P, 2, 2, P])
        xn = sb("xn", [P, 2, P])
        st = [sb(f"st{k}", [P, 2, 6]) for k in range(3)]
        mv = [sb(f"mv{k}", [P, 2, 2]) for k in range(3)]
        nm = [sb(f"nm{k}", [P, 2]) for k in range(3)]
        ve = [sb(f"ve{k}", [P, 2]) for k in range(3)]
        rs = [sb(f"rs{k}", [P, 2]) for k in range(3)]
        xnT = sb("xnT", [P, L1])
        parts = sb("parts", [P, 2, 3, 2, 2, L1], BF16)
        rest = sb("rest", [P, 2, L1])
        qs = sb("qs", [P, H1, 4, L1], BF16)
        ks = sb("ks", [P, H1, 4, L1], BF16)
        v32 = sb("v32", [P, 4, 2, H1, 32])
        nmax = sb("nmax", [P, 2, H1])
        nmr = sb("nmr", [P, 2, HALF])
        mparts = sb("mparts", [P, 2, 3, HALF], BF16)
        mT = sb("mT", [24, L1], BF16)
        pr = sb("pr", [P, 4, 2, 2, L1])
        osb = sb("osb", [P, 2, 512])
        rden = sb("rden", [P, 2, 8])
        on = sb("on", [P, 2, P])
        onT = sb("onT", [P, L1])
        r1 = sb("r1", [P, 2, P])
        nr = sb("nr", [P, 2, P])

        psA = pb("psA", [P, 2, 512])
        psB = pb("psB", [P, 4, 512])
        psO = pb("psO", [P, 512])
        misc = pb("misc", [P, 512])
        misch = misc[:, :].bitcast(BF16)

        names = ["passed", "ld_w", "ld_b", "ld_x", "consts", "consts_p", "zeroed", "dve_set", "x_in0", "x_in1",
                 "stats0", "stats1", "aggr0", "aggr1", "ln0_step", "ln1_step", "xn_ok", "xnb_ok", "misc_full",
                 "misc_free", "p1_ok", "p2_ok", "p3_ok", "stack0", "stack1", "a_full", "a_free", "split_step",
                 "mp_ok", "mrow0", "mrow1", "b_full", "b_free", "av_done", "o_ev", "rden_ok", "r_ok", "x1_ok",
                 "stored", "v_ok"]
        S = {n: sem(n) for n in names}

        x_t = x.rearrange("b (p c) d -> b p c d", p=P)

        BEFORE, EACH = 13, 8

        def has(k, i):
            done, here, ahead = 1 <= i <= LAST + 1, i <= LAST, i + AHEAD <= LAST
            return (done, here, i + 3 <= LAST or 2 <= i <= LAST + 2, ahead, done, i + 1 <= LAST, ahead, done)[k]

        def use_no(k, i):
            if isinstance(i, int):
                return BEFORE + sum(has(kk, ii) for ii in range(i) for kk in range(EACH)) + sum(
                    has(kk, i) for kk in range(k))
            return i * EACH + (use_no(k, 2) - 2 * EACH)

        def xT_use(b):
            return 1 + 3 * b if isinstance(b, int) and b < AHEAD else use_no(3, b - AHEAD)

        def v_use(b):
            return 2 + 3 * b if isinstance(b, int) and b < 3 else use_no(2, b - 3)

        def qk_use(b):
            if isinstance(b, int) and b < AHEAD:
                return 3 + 3 * b if b < 3 else 11
            return use_no(6, b - AHEAD)

        def max_use(b, hf):
            if hf == 0 and isinstance(b, int) and b == 0:
                return 12
            return use_no(1, b) if hf else use_no(5, b - 1)

        def out_use(b, hf):
            return use_no(4 * hf, b + 1)

        def fits(i, d):
            return not isinstance(i, int) or 0 <= i + d <= LAST

        def stack_count(b, m):
            return (b - m) * (4 * NPROD * 2) + 16 * 2 * NPROD

        def pipeline(eng, iteration):
            iteration(0, 0)
            iteration(1, 1)
            with eng.Fori(0, 2) as four:
                for r in range(2, 6):
                    iteration(four * 4 + r, r % 4)
            for i in range(10, LAST + 3):
                iteration(i, i % 4)

        block = ctx.enter_context(nc.Block())

        @block.tensor
        def _(pe):
            T = nc.tensor
            pe.wait_ge(S["ld_w"], 32)
            pe.wait_ge(S["consts_p"], 1)
            for k in range(4):
                last = T.transpose(misc[:, k * P:(k + 1) * P], w_nat[:, k, :], ident[:, :])
            last.then_inc(S["misc_full"], 1)

            def prep_x(b):
                pe.wait_ge(S["misc_free"], count(xT_use(b)))
                pe.wait_ge(S["xn_ok"], count(b + 1))
                for c in range(2):
                    last = T.transpose(misc[:, c * P:(c + 1) * P], xn[:, c, :], ident[:, :])
                last.then_inc(S["misc_full"], 1)

            def prep_qk(b):
                pe.wait_ge(S["misc_free"], count(qk_use(b)))
                for k in range(2):
                    last = T.matmul(misc[:, k * L1:(k + 1) * L1], wT[:, k, :], xnT[:, :], start=True, stop=True)
                last.then_inc(S["misc_full"], 1)

            def token_major(lhs, k, at):
                for c in range(2):
                    last = T.matmul(misc[:, at + c * P:at + (c + 1) * P], lhs[:, c * P:(c + 1) * P], wT[:, k, :],
                                    start=True, stop=True)
                return last

            def scores_for_max(b, m, g):
                if g == 0:
                    pe.wait_ge(S[f"stack{m // 2}"], count(stack_count(b, m)))
                for c in range(2):
                    pe.wait_ge(S["a_free"], count(16 * b + 2 * g + c - 1))
                    for j in range(2):
                        h = 2 * g + j
                        last = T.matmul(psA[:, c, j * L1:(j + 1) * L1], qs[0:MAX_ROW, h, m, c * P:(c + 1) * P],
                                        ks[0:MAX_ROW, h, m, :], start=True, stop=True)
                    last.then_inc(S["a_full"], 1)

            def scores(b, m, g):
                if g % 4 == 0:
                    pe.wait_ge(S[f"mrow{g // 4}"], count(16 * (b + 1)))
                pe.wait_ge(S["b_free"], count(8 * b + g - 1))
                for j in range(2):
                    h = 2 * g + j
                    for c in range(2):
                        last = T.matmul(psB[:, 2 * (g % 2) + j, c * L1:(c + 1) * L1], ks[:, h, m, c * P:(c + 1) * P],
                                        qs[:, h, m, :], start=True, stop=True)
                last.then_inc(S["b_full"], 1)

            def attend(b, m, q):
                pe.wait_ge(S["b_free"], count(8 * b + 2 * q + 2))
                if q % 2 == 0:
                    pe.wait_ge(S["o_ev"], count(2 * b + q // 2))
                for c in range(2):
                    for j in range(4):
                        g = 2 * q + j // 2
                        last = T.matmul(psO[32 * j:32 * j + 32, (q % 2) * L1:(q % 2 + 1) * L1],
                                        v32[:, m, c, 4 * q + j, :], pr[:, g % 4, j % 2, c, :],
                                        start=(c == 0), stop=(c == 1))
                last.then_inc(S["av_done"], 1)

            def max_rows(b, hf):
                pe.wait_ge(S["misc_free"], count(max_use(b, hf)))
                pe.wait_ge(S["mp_ok"], count(2 * b + hf + 1))
                for c in range(2):
                    last = T.transpose(misch[0:24, c * P:(c + 1) * P],
                                       mparts[:, c, :, :].rearrange("p a h -> p (a h)"), identh[:, :])
                last.then_inc(S["misc_full"], 1)

            def heads_to_tokens(b, hf):
                pe.wait_ge(S["misc_free"], count(out_use(b, hf)))
                pe.wait_ge(S["o_ev"], count(2 * b + hf + 1))
                for c in range(2):
                    for q in range(2):
                        last = T.transpose(misc[:, (2 * c + q) * P:(2 * c + q + 1) * P],
                                           osb[:, hf, q * L1 + c * P:q * L1 + (c + 1) * P], ident[:, :])
                last.then_inc(S["misc_full"], 1)

            def heads_T(i):
                pe.wait_ge(S["misc_free"], count(use_no(7, i)))
                for c in range(2):
                    last = T.transpose(misc[:, c * P:(c + 1) * P], on[:, c, :], ident[:, :])
                last.then_inc(S["misc_full"], 1)

            def iteration(i, m):
                here, next_, done, ahead = fits(i, 0), fits(i, 1), fits(i, -1), fits(i, AHEAD)
                for g in range(8):
                    if here:
                        scores(i, m, g)
                    if next_:
                        scores_for_max(i + 1, (m + 1) % 4, g)
                    if here and g in (2, 4, 6):
                        attend(i, m, g // 2 - 1)
                    if g == 0 and done:
                        attend(i - 1, (m - 1) % 4, 3)
                        heads_to_tokens(i - 1, 0)
                    if g == 1 and here:
                        max_rows(i, 1)
                    if g == 2 and (fits(i, 3) or fits(i, -2)):
                        pe.wait_ge(S["misc_free"], count(use_no(2, i)))
                        if fits(i, 3):
                            last = token_major(xnT, 2, 0)
                        if fits(i, -2):
                            last = token_major(onT, 3, 2 * P)
                        last.then_inc(S["misc_full"], 1)
                    if g == 3 and ahead:
                        prep_x(i + AHEAD)
                    if g == 4 and done:
                        heads_to_tokens(i - 1, 1)
                    if g == 5 and next_:
                        max_rows(i + 1, 0)
                    if g == 6 and ahead:
                        prep_qk(i + AHEAD)
                    if g == 7 and done:
                        heads_T(i)

            for b in range(AHEAD):
                prep_x(b)
                if b < 3:
                    pe.wait_ge(S["misc_free"], count(v_use(b)))
                    token_major(xnT, 2, 0).then_inc(S["misc_full"], 1)
                prep_qk(b)
            pe.wait_ge(S["zeroed"], 3)
            for g in range(8):
                scores_for_max(0, 0, g)
                if g == 5:
                    max_rows(0, 0)
            pipeline(pe, iteration)

        @block.vector
        def _(dve):
            V = nc.vector
            dve.wait_ge(S["misc_full"], 1)
            V.tensor_copy(wT[:, 0:2, :].rearrange("p k (c h) -> p k h c", c=C1),
                          misc[:, 0:2 * P].rearrange("p (k h c) -> p k h c", k=2, c=C1))
            V.tensor_copy(wT[:, 2:4, :].rearrange("p a d -> p (a d)"), misc[:, 2 * P:4 * P]).then_inc(S["misc_free"], 1)

            def ln_stats(kind, b, src):
                for c in range(2):
                    V.bn_stats(st[kind][:, c, :], src[:, c, :]).then_inc(S[f"stats{kind}"], 1)
                for c in range(2):
                    dve.wait_ge(S[f"stats{kind}"], count(2 * b + c + 1))
                    dve.sem_inc(S["passed"])
                    last = V.bn_aggr(mv[kind][:, c, :], st[kind][:, c, :])
                last.then_inc(S[f"aggr{kind}"], 1)

            def stats_x(b, m):
                dve.wait_ge(S[f"x_in{m % 2}"], count((b - m % 2) * 8 + 16))
                dve.wait_ge(S["xn_ok"], count(b))
                ln_stats(0, b, xin[:, m % 2, :, :])

            def split_qk(b, m):
                dve.wait_ge(S["misc_full"], count(qk_use(b) + 1))
                dve.wait_ge(S["p1_ok"], count(2 * b + 2))
                dve.wait_ge(S["p3_ok"], count(b))
                for k in range(2):
                    last = V.scalar_tensor_tensor(out=rest[:, k, :], in0=misc[:, k * L1:(k + 1) * L1],
                                                  scalar=b_col[:, k:k + 1], in1=parts[:, m // 2, 0, k, m % 2, :],
                                                  op0=ALU.add, op1=ALU.subtract)
                last.then_inc(S["misc_free"], 1)
                dve.wait_ge(S["misc_free"], count(qk_use(b) + 1))
                V.tensor_copy(parts[:, m // 2, 1, :, m % 2, :], rest[:, :, :]).then_inc(S["p2_ok"], 1)

            def residual(i):
                dve.wait_ge(S["misc_full"], count(use_no(2, i) + 1))
                if fits(i, 3):
                    dve.wait_ge(S["v_ok"], count(i - 1))
                dve.wait_ge(S["xnb_ok"], count(i - 1))
                dve.wait_ge(S["x1_ok"], count(i - 2))
                V.tensor_tensor(out=r1[:, :, :], in0=misc[:, 2 * P:4 * P].rearrange("p (c d) -> p c d", c=2),
                                in1=xnb_all[:, bass.ds((i - 2) * 2, 2), :], op=ALU.add).then_inc(S["misc_free"], 1)
                dve.wait_ge(S["misc_free"], count(use_no(2, i) + 1))
                ln_stats(1, i - 2, r1)

            def maxima(b, g):
                for c in range(2):
                    dve.wait_ge(S["a_full"], count(16 * b + 2 * g + c + 1))
                    if g % 4 == 0 and c == 0:
                        dve.wait_ge(S["mp_ok"], count(2 * b + g // 4 - 1))
                    V.tensor_reduce(nmax[:, c, 2 * g:2 * g + 2], psA[:, c, :].rearrange("p (h m) -> p h m", h=2),
                                    AX.X, ALU.max, negate=True).then_inc(S["a_free"], 1)

            def normalise(b, hf):
                dve.wait_ge(S["misc_full"], count(out_use(b, hf) + 1))
                o = misc[:, :].rearrange("p (c k r) -> p c k r", c=2, r=32)
                V.reciprocal(rden[:, :, :], o[:, :, :, C1]).then_inc(S["rden_ok"], 1)
                dve.wait_ge(S["rden_ok"], count(2 * b + hf + 1))
                V.tensor_tensor(out=on[:, :, hf * 64:(hf + 1) * 64].rearrange("p c (k e) -> p c k e", e=C1),
                                in0=o[:, :, :, 0:C1],
                                in1=rden[:, :, :].unsqueeze(3).broadcast_to([P, 2, 8, C1]),
                                op=ALU.mult).then_inc(S["misc_free"], 1)

            def iteration(i, m):
                next_, done = fits(i, 1), fits(i, -1)
                for g in range(8):
                    if next_:
                        maxima(i + 1, g)
                    if g == 0 and done:
                        normalise(i - 1, 0)
                    if g == 1 and fits(i, AHEAD):
                        stats_x(i + AHEAD, m)
                    if g == 3 and fits(i, -2):
                        residual(i)
                    if g == 4 and done:
                        normalise(i - 1, 1)
                    if g == 7 and fits(i, AHEAD):
                        split_qk(i + AHEAD, m)

            for b in range(AHEAD):
                stats_x(b, b)
                if b == 1:
                    V.memset(ks[0:MAX_ROW, :, :, :].rearrange("p h b l -> p (h b l)").bitcast(F32),
                             0.0).then_inc(S["zeroed"], 1)
                if b >= 1:
                    split_qk(b - 1, b - 1)
            split_qk(3, 3)
            for g in range(8):
                maxima(0, g)
            pipeline(dve, iteration)

        @block.scalar
        def _(act):
            A = nc.scalar

            def first_parts(b, m):
                act.wait_ge(S["misc_full"], count(qk_use(b) + 1))
                act.wait_ge(S[f"stack{m // 2}"], count(stack_count(b - 4, m)))
                for k in range(2):
                    A.activation(parts[:, m // 2, 0, k, m % 2, :], misc[:, k * L1:(k + 1) * L1], ACT.Identity,
                                 bias=b_col[:, k:k + 1]).then_inc(S["p1_ok"], 1)

            def copy_out(dst, src, n):
                act.wait_ge(S["misc_full"], count(n + 1))
                A.activation(dst, src, ACT.Copy).then_inc(S["misc_free"], 1)

            def max_rows(b, hf):
                act.wait_ge(S[f"mrow{hf}"], count(16 * b))
                act.wait_ge(S[f"mrow{1 - hf}"], count(16 * (b + hf)))
                copy_out(mT[:, :], misch[0:24, 0:L1], max_use(b, hf))

            def out_rows(b, hf):
                act.wait_ge(S["av_done"], count(4 * b + 2 * hf + 2))
                act.wait_ge(S["misc_full"], count(out_use(b - 1, hf) + 1 if not isinstance(b, int) or b >= 1 else 0))
                A.activation(osb[:, hf, :], psO[:, :], ACT.Copy).then_inc(S["o_ev"], 1)

            def v_in(b, m, only):
                act.wait_ge(S["misc_full"], count(v_use(b) + 1))
                A.activation(v32[:, m, :, :, 0:C1], misc[:, 0:2 * P].rearrange("p (a h c) -> p a h c", a=2, c=C1),
                             ACT.Copy).then_inc(S["misc_free" if only else "v_ok"], 1)

            def iteration(i, m):
                here, next_, done, ahead = fits(i, 0), fits(i, 1), fits(i, -1), fits(i, AHEAD)
                for g in range(8):
                    if here:
                        act.wait_ge(S["b_full"], count(8 * i + g + 1))
                        act.wait_ge(S["av_done"], count(4 * i + (g - 4) // 2 + 1))
                        A.activation(pr[:, g % 4, :, :, :].rearrange("p j c l -> p (j c l)"),
                                     psB[:, 2 * (g % 2):2 * (g % 2) + 2, :].rearrange("p a n -> p (a n)"),
                                     ACT.Exp, scale=SCALE1).then_inc(S["b_free"], 1)
                    if g == 0 and done:
                        out_rows(i - 1, 1)
                    if g == 1 and here:
                        max_rows(i, 1)
                    if g == 2 and fits(i, 3):
                        v_in(i + 3, (m + 3) % 4, isinstance(i, int) and i < 2)
                    if g == 3 and ahead:
                        copy_out(xnT[:, :], misc[:, 0:L1], xT_use(i + AHEAD))
                    if g == 4 and here:
                        out_rows(i, 0)
                    if g == 5 and next_:
                        max_rows(i + 1, 0)
                    if g == 6 and ahead:
                        first_parts(i + AHEAD, m)
                    if g == 7 and done:
                        act.wait_ge(S["misc_full"], count(use_no(7, i) + 1))
                        A.activation(onT[:, :], misc[:, 0:L1], ACT.Identity, bias=bv_col[:, :]
                                     ).then_inc(S["misc_free"], 1)

            act.wait_ge(S["consts"], 1)
            A.activation(ks[MAX_ROW:P, :, :, :].rearrange("p h b l -> p (h b l)").bitcast(F32),
                         one_pair[MAX_ROW:P, :].broadcast_to([P - MAX_ROW, H1 * 2 * L1]),
                         ACT.Copy).then_inc(S["zeroed"], 1)
            act.wait_ge(S["ld_b"], 64)
            for b in range(AHEAD):
                copy_out(xnT[:, :], misc[:, 0:L1], xT_use(b))
                if b < 3:
                    v_in(b, b, True)
                first_parts(b, b)
            max_rows(0, 0)
            pipeline(act, iteration)

        @block.gpsimd
        def _(pool):
            G = nc.gpsimd
            G.memset(minus_half[:, :], -0.5)
            G.memset(one_pair[:, :].bitcast(BF16), 1.0)
            G.memset(ident[:, :], 0.0).then_inc(S["consts"], 1)
            pool.wait_ge(S["consts"], 1)
            G.affine_select(out=ident[:, :], in_=ident[:, :], compare_op=ALU.not_equal, fill=1.0, base=0,
                            pattern=[[-1, P]], channel_multiplier=1).then_inc(S["consts"], 1)
            pool.wait_ge(S["consts"], 2)
            pool.sem_inc(S["passed"])
            G.tensor_copy(identh[:, :], ident[:, :]).then_inc(S["consts_p"], 1)

            def ln_scale(kind, b):
                step, before = f"ln{kind}_step", (3 + kind) * b
                pool.wait_ge(S[f"aggr{kind}"], count(b + 1))
                pool.sem_inc(S["passed"])
                G.tensor_scalar(ve[kind][:, :], mv[kind][:, :, 1], EPS, None, ALU.add).then_inc(S[step], 1)
                G.tensor_scalar(nm[kind][:, :], mv[kind][:, :, 0], -1.0, None, ALU.mult).then_inc(S[step], 1)
                pool.wait_ge(S[step], count(before + 1))
                G.tensor_tensor(rs[kind][:, :], ve[kind][:, :], minus_half[:, :], ALU.pow).then_inc(S[step], 1)
                pool.wait_ge(S[step], count(before + 3))
                pool.sem_inc(S["passed"])

            def norm_x(b, m):
                ln_scale(0, b)
                if not isinstance(b, int) or b >= 1:
                    pool.wait_ge(S["misc_full"], count(xT_use(b - 1) + 1))
                    pool.sem_inc(S["passed"])
                for c in range(2):
                    last = G.tensor_scalar(xn[:, c, :], xin[:, m % 2, c, :], nm[0][:, c:c + 1], rs[0][:, c:c + 1],
                                           ALU.add, ALU.mult)
                last.then_inc(S["xn_ok"], 1)
                pool.wait_ge(S["xn_ok"], count(b + 1))
                G.tensor_tensor(xnb_all[:, bass.ds(b * 2, 2), :], xn[:, :, :],
                                bo_row[:, :].unsqueeze(1).broadcast_to([P, 2, P]), ALU.add).then_inc(S["xnb_ok"], 1)

            def last_parts(b, m):
                pool.wait_ge(S["p2_ok"], count(b + 1))
                G.tensor_tensor(parts[:, m // 2, 2, :, m % 2, :], rest[:, :, :], parts[:, m // 2, 1, :, m % 2, :],
                                ALU.subtract).then_inc(S["p3_ok"], 1)

            def split_max(b, hf):
                src = nmax[:, :, hf * HALF:(hf + 1) * HALF]
                n = 3 * (2 * b + hf)
                pool.wait_ge(S["a_free"], count(16 * b + 8 * hf + 8))
                if not isinstance(b, int) or b + hf > 0:
                    pool.wait_ge(S["misc_full"], count((max_use(b, 0) if hf else max_use(b - 1, 1)) + 1))
                    pool.sem_inc(S["passed"])
                G.tensor_copy(mparts[:, :, 0, :], src).then_inc(S["split_step"], 1)
                pool.wait_ge(S["split_step"], count(n + 1))
                G.tensor_tensor(nmr[:, :, :], src, mparts[:, :, 0, :], ALU.subtract).then_inc(S["split_step"], 1)
                pool.wait_ge(S["split_step"], count(n + 2))
                pool.sem_inc(S["passed"])
                G.tensor_copy(mparts[:, :, 1, :], nmr[:, :, :]).then_inc(S["split_step"], 1)
                pool.wait_ge(S["split_step"], count(n + 3))
                G.tensor_tensor(mparts[:, :, 2, :], nmr[:, :, :], mparts[:, :, 1, :],
                                ALU.subtract).then_inc(S["mp_ok"], 1)

            def add_attention(b):
                ln_scale(1, b)
                for c in range(2):
                    last = G.tensor_scalar(nr[:, c, :], r1[:, c, :], nm[1][:, c:c + 1], rs[1][:, c:c + 1],
                                           ALU.add, ALU.mult)
                last.then_inc(S["ln1_step"], 1)
                pool.wait_ge(S["ln1_step"], count(4 * b + 4))
                G.tensor_tensor(x_all[:, bass.ds(b * 2, 2), :], nr[:, :, :], x_all[:, bass.ds(b * 2, 2), :],
                                ALU.add).then_inc(S["x1_ok"], 1)

            def iteration(i, m):
                if fits(i, 0):
                    split_max(i, 1)
                if fits(i, AHEAD):
                    norm_x(i + AHEAD, m)
                if fits(i, 1):
                    split_max(i + 1, 0)
                if fits(i, AHEAD):
                    last_parts(i + AHEAD, m)
                if fits(i, -2):
                    add_attention(i - 2)

            G.memset(v32[:, :, :, :, C1 + 1:32], 0.0)
            G.memset(v32[:, :, :, :, C1:C1 + 1], 1.0)
            pool.wait_ge(S["ld_b"], 64)
            pool.wait_ge(S["ld_x"], 16)
            norm_x(0, 0)
            for b in range(1, AHEAD):
                norm_x(b, b)
                if b == 1:
                    G.memset(qs[:, :, :, :].rearrange("p h b l -> p (h b l)").bitcast(F32),
                             0.0).then_inc(S["zeroed"], 1)
                last_parts(b - 1, b - 1)
            last_parts(3, 3)
            split_max(0, 0)
            pipeline(pool, iteration)

        @block.sync
        def _(sp):
            def load_x(b, m):
                sp.wait_ge(S["xn_ok"], count(b - 1))
                sp.dma_start(xin[:, m % 2, :, :], x_t[b]).then_inc(S[f"x_in{m % 2}"], 16)

            def stack(b, m):
                sp.wait_ge(S["p3_ok"], count(b + 2))
                if not isinstance(b, int) or b >= 4:
                    sp.wait_ge(S["b_full"], count(8 * (b - 2)))
                for dst, k, which in ((qs, 0, Q_PART), (ks, 1, K_PART)):
                    for j, part in enumerate(which):
                        sp.dma_start(dst[C1 * j:C1 * (j + 1), :, m:m + 2, :].rearrange("c h b l -> c h (b l)"),
                                     parts[:, m // 2, part, k, :, :].rearrange("p b l -> p (b l)")
                                     ).then_inc(S[f"stack{m // 2}"], 16)

            def max_rows(b, m, hf):
                sp.wait_ge(S["misc_free"], count(max_use(b, hf) + 1))
                sp.dma_start(qs[MAX_ROW:MAX_ROW + 3, hf * HALF:(hf + 1) * HALF, m, :],
                             mT[:, :]).then_inc(S[f"mrow{hf}"], 16)

            def iteration(i, m):
                if fits(i, AHEAD):
                    load_x(i + AHEAD, m)
                if fits(i, 0):
                    max_rows(i, m, 1)
                if m % 2 == 0 and fits(i, 2):
                    stack(i + 2, (m + 2) % 4)
                if fits(i, 1):
                    max_rows(i + 1, (m + 1) % 4, 0)
                if not isinstance(i, int):
                    pass
                elif i >= 10:
                    for b in range((0 if i == 10 else i - 3), i - 2):
                        x1_over(b)

            def x1_over(b):
                sp.wait_ge(S["x1_ok"], count(b + 1))
                sp.dma_start(xs[(L1 // 32) * b:(L1 // 32) * (b + 1), :, :].rearrange("p j d -> p (j d)"),
                             x_all[:, 2 * b:2 * b + 2, :].rearrange("p c d -> p (c d)")).then_inc(S["stored"], 16)

            load_x(0, 0)
            load_x(1, 1)
            sp.dma_start(w_nat[:, 0:3, :], w_qkv.rearrange("(k p) d -> p k d", p=P)).then_inc(S["ld_w"], 16)
            sp.dma_start(w_nat[:, 3, :], w_o).then_inc(S["ld_w"], 16)
            for k in range(2):
                sp.dma_start(b_col[:, k:k + 1], b_qkv[k * P:(k + 1) * P].rearrange("(h c o) -> c h o", c=C1, o=1),
                             allow_slow_non_contiguous=True).then_inc(S["ld_b"], 16)
            sp.dma_start(bv_col[:, :], b_qkv[2 * P:3 * P].rearrange("(p o) -> p o", o=1),
                         allow_slow_non_contiguous=True).then_inc(S["ld_b"], 16)
            sp.dma_start(bo_row[:, :], b_o.partition_broadcast(P)).then_inc(S["ld_b"], 16)
            sp.dma_start(x_all[:, :, :].rearrange("p (b c) d -> p b c d", c=2),
                         x.rearrange("b (p c) d -> p b c d", p=P)).then_inc(S["ld_x"], 16)
            load_x(2, 2)
            load_x(3, 3)
            sp.wait_ge(S["zeroed"], 3)
            stack(0, 0)
            max_rows(0, 0, 0)
            pipeline(sp, iteration)
            x1_over(LAST)
            sp.wait_ge(S["stored"], count(16 * B1))


H2, C2 = 4, 32
S2 = B1
SCALE2 = 1.0 / float(C2) ** 0.5
NSTEP = NT // 2
NE, DF = 8, 512


def second_attention(nc, w, ident, identh, minus_half, xs, y_all, logits):
    Wqkv, bqkv, Wo, bo, g1, be1, Wg = w
    with ExitStack() as ctx:
        def sb(name, shape, dt=F32):
            return ctx.enter_context(nc.sbuf_tensor(name, shape, dt))

        def pb(name):
            return ctx.enter_context(nc.psum_tensor(name, [P, 512], F32))

        u_nat = sb("u_nat", [P, 4, P])
        wg_nat = sb("wg_nat", [NE, P])
        uT = sb("uT", [P, 4, P])
        wgT = sb("wgT", [P, NE])
        u_col = sb("u_col", [P, 3])
        rows = sb("rows", [P, 3, P])
        same = sb("same", [P, 8])
        mask = sb("mask", [P, P], BF16)
        x2n = sb("x2n", [P, 2, 2, P])
        st_x, st_y = sb("st_x", [P, 2, 6]), sb("st_y", [P, 2, 6])
        mv_x, mv_y = sb("mv_x", [P, 2, 2]), sb("mv_y", [P, 2, 2])
        ve_x, ve_y = sb("ve_x", [P, 2]), sb("ve_y", [P, 2])
        nm_x, nm_y = sb("nm_x", [P, 2]), sb("nm_y", [P, 2])
        rs_x, rs_y = sb("rs_x", [P, 2]), sb("rs_y", [P, 2])
        xy = sb("xy", [P, 2, 512])
        qT2 = sb("qT2", [P, 2, H2, L1])
        kT2 = sb("kT2", [P, 2, L1])
        v2 = sb("v2", [P, 4, 2, P])
        nmax2 = sb("nmax2", [P, 2, H2])
        nbias = sb("nbias", [P, 2, H2])
        den = sb("den", [P, 2, 2, H2])
        rden2 = sb("rden2", [P, 2, H2])
        prob = sb("prob", [P, 2, 2, H2, P])
        probT = sb("probT", [P, 2, 512])
        attT = sb("attT", [P, L1])
        r2 = sb("r2", [P, 2, P])
        yn = sb("yn", [P, 2, P])
        yg = sb("yg", [P, 2, P])
        yout = sb("yout", [P, 2, 2, P])
        xs_flat = xs[:, :, :].rearrange("p j d -> p (j d)")
        psXY, psQK, psVO, psAL = pb("psXY"), pb("psQK"), pb("psVO"), pb("psAL")
        psS = [pb("psS0"), pb("psS1")]
        psP = [pb("psP0"), pb("psP1")]

        names = ["passed", "in_w", "in_b", "wT_full", "wT_ok", "same_ok", "q_zero", "mask_ok", "xst", "xagg", "xstep", "xrs_ok", "xn2_ok",
                 "xnb2_ok", "xy_full", "xy_read", "qk_full", "q_ok", "k_ok", "vo_full", "v2_ok", "r2_ok", "s_full",
                 "m_step", "max_ok", "p_ok", "rd_ok", "pn_ok", "pt_full", "pt_ok", "al_full", "att_ok", "lg_ok",
                 "yst", "yagg", "ystep", "yln_step", "y_ok", "y_kept"]
        S = {n: ctx.enter_context(nc.semaphore("l2_" + n)) for n in names}

        def has(t, lag):
            return not isinstance(t, int) or 0 <= t - lag < NSTEP

        def pipeline(iteration):
            def run(eng):
                for t in range(8):
                    iteration(t, t)
                with eng.Fori(0, 2) as four:
                    for r in range(4):
                        iteration(four * 4 + (8 + r), r)
                for t in range(16, NSTEP + 8):
                    iteration(t, t % 4)
            return run

        block = ctx.enter_context(nc.Block())

        @block.tensor
        def _(pe):
            T = nc.tensor
            pe.wait_ge(S["in_w"], 48)
            for k in range(4):
                last = T.transpose(psS[0][:, k * P:(k + 1) * P], u_nat[:, k, :], ident[:, :])
            last = T.transpose(psS[1][:, 0:NE], wg_nat[:, :], ident[0:NE, 0:NE])
            last.then_inc(S["wT_full"], 1)
            pe.wait_ge(S["wT_ok"], 2)
            pe.wait_ge(S["mask_ok"], 1)

            def iteration(t, m):
                if has(t, 2):
                    i, n = t - 2, (m - 2) % 2
                    pe.wait_ge(S["q_ok"], count(i + 1))
                    pe.wait_ge(S["k_ok"], count(i + 1))
                    for c in range(2):
                        pe.wait_ge(S["p_ok"], count(8 * (i - 1) + 4 * c + 4))
                        for h in range(H2):
                            at = psS[c][:, h * P:(h + 1) * P]
                            T.matmul(at, identh[:, :], mask[:, :], start=True, stop=False)
                            last = T.matmul(at, qT2[:, n, h, c * P:(c + 1) * P],
                                            kT2[:, n, c * P:(c + 1) * P], start=False, stop=True)
                        last.then_inc(S["s_full"], 1)
                if has(t, 1):
                    pe.wait_ge(S["xy_read"], count(t))
                    pe.wait_ge(S["q_ok"], count(t - 1))
                    pe.wait_ge(S["k_ok"], count(t - 1))
                    for k in range(2):
                        last = T.matmul(psQK[:, k * L1:(k + 1) * L1], uT[:, k, :], xy[:, (m - 1) % 2, 0:L1],
                                        start=True, stop=True)
                    last.then_inc(S["qk_full"], 1)
                if has(t, 1) or has(t, 5):
                    pe.wait_ge(S["v2_ok"], count(min(t - 1, NSTEP) if isinstance(t, int) else t - 1))
                    pe.wait_ge(S["r2_ok"], count(t - 5))
                    if has(t, 1):
                        for c in range(2):
                            last = T.matmul(psVO[:, c * P:(c + 1) * P], xy[:, (m - 1) % 2, c * P:(c + 1) * P],
                                            uT[:, 2, :], start=True, stop=True)
                    if has(t, 5):
                        pe.wait_ge(S["att_ok"], count(t - 4))
                        for c in range(2):
                            last = T.matmul(psVO[:, (2 + c) * P:(3 + c) * P], attT[:, c * P:(c + 1) * P],
                                            uT[:, 3, :], start=True, stop=True)
                    last.then_inc(S["vo_full"], 1)
                if has(t, 4) or has(t, 8):
                    pe.wait_ge(S["att_ok"], count(min(t - 4, NSTEP) if isinstance(t, int) else t - 4))
                    pe.wait_ge(S["lg_ok"], count(t - 8))
                    if has(t, 4):
                        pe.wait_ge(S["pt_ok"], count(2 * (t - 4) + 2))
                        pe.wait_ge(S["v2_ok"], count(t - 3))
                        for c in range(2):
                            for h in range(H2):
                                last = T.matmul(psAL[C2 * h:C2 * h + C2, c * P:(c + 1) * P],
                                                v2[:, m % 4, c, C2 * h:C2 * h + C2],
                                                probT[:, c, h * P:(h + 1) * P], start=True, stop=True,
                                                tile_position=(0, C2 * h))
                    if has(t, 8):
                        pe.wait_ge(S["xy_read"], count(t))
                        for c in range(2):
                            last = T.matmul(psAL[:, L1 + NE * c:L1 + NE * (c + 1)],
                                            xy[:, (m - 1) % 2, (2 + c) * P:(3 + c) * P], wgT[:, :], start=True,
                                            stop=True)
                    last.then_inc(S["al_full"], 1)
                if has(t, 0) or has(t, 7):
                    pe.wait_ge(S["xy_read"], count(t))
                    if has(t, 0):
                        pe.wait_ge(S["xn2_ok"], count(t + 1))
                        for c in range(2):
                            last = T.transpose(psXY[:, c * P:(c + 1) * P], x2n[:, m % 2, c, :], ident[:, :])
                    if has(t, 7):
                        pe.wait_ge(S["y_ok"], count(t - 6))
                        for c in range(2):
                            last = T.transpose(psXY[:, (2 + c) * P:(3 + c) * P], yout[:, (m - 7) % 2, c, :], ident[:, :])
                    last.then_inc(S["xy_full"], 1)
                if has(t, 3):
                    i = t - 3
                    for c in range(2):
                        pe.wait_ge(S["pn_ok"], count(2 * i + c + 1))
                        pe.wait_ge(S["pt_ok"], count(2 * (i - 1) + c + 1))
                        for h in range(H2):
                            last = T.transpose(psP[c][:, h * P:(h + 1) * P], prob[:, (m - 3) % 2, c, h, :],
                                               ident[:, :])
                        last.then_inc(S["pt_full"], 1)

            pipeline(iteration)(pe)

        @block.vector
        def _(dve):
            V = nc.vector
            V.tensor_reduce(same[:, :], ident[:, :].rearrange("p (s r) -> p r s", r=8), AX.X,
                            ALU.add).then_inc(S["same_ok"], 1)
            dve.wait_ge(S["same_ok"], 1)
            V.tensor_scalar(mask[:, :].rearrange("p (s r) -> p s r", r=8),
                            same[:, :].unsqueeze(1).broadcast_to([P, S2, 8]), -1.0, 1e30, ALU.add,
                            ALU.mult).then_inc(S["mask_ok"], 1)
            dve.wait_ge(S["wT_full"], 1)
            V.tensor_copy(uT[:, :, :].rearrange("p k d -> p (k d)"), psS[0][:, :]).then_inc(S["wT_ok"], 1)
            V.tensor_copy(wgT[:, :], psS[1][:, 0:NE]).then_inc(S["wT_ok"], 1)
            dve.wait_ge(S["in_b"], 96)

            def norm_x(i, n):
                dve.wait_ge(S["xn2_ok"], count(i))
                for c in range(2):
                    V.bn_stats(st_x[:, c, :], xs_flat[:, bass.ds(i * L1 + c * P, P)]).then_inc(S["xst"], 1)
                for c in range(2):
                    dve.wait_ge(S["xst"], count(2 * i + c + 1))
                    dve.sem_inc(S["passed"])
                    last = V.bn_aggr(mv_x[:, c, :], st_x[:, c, :])
                last.then_inc(S["xagg"], 1)

            def apply_x(i, n):
                dve.wait_ge(S["xrs_ok"], count(i + 1))
                dve.wait_ge(S["xnb2_ok"], count(i - 1))
                dve.wait_ge(S["xy_full"], count(i - 1))
                for c in range(2):
                    last = V.tensor_scalar(x2n[:, n, c, :], xs_flat[:, bass.ds(i * L1 + c * P, P)], nm_x[:, c:c + 1], rs_x[:, c:c + 1],
                                           ALU.add, ALU.mult)
                last.then_inc(S["xn2_ok"], 1)

            def iteration(t, m):
                if has(t, 0):
                    norm_x(t, m % 2)
                if has(t, 2):
                    i = t - 2
                    for c in range(2):
                        dve.wait_ge(S["s_full"], count(2 * i + c + 1))
                        V.tensor_reduce(nmax2[:, c, :], psS[c][:, :].rearrange("p (h k) -> p h k", h=H2), AX.X,
                                        ALU.max, negate=True).then_inc(S["m_step"], 1)
                        dve.wait_ge(S["m_step"], count(2 * i + c + 1))
                        dve.wait_ge(S["p_ok"], count(8 * (i - 1) + 4 * c + 4))
                        V.tensor_scalar(nbias[:, c, :], nmax2[:, c, :], SCALE2, None,
                                        ALU.mult).then_inc(S["max_ok"], 1)
                if has(t, 0):
                    apply_x(t, m % 2)
                if has(t, 3):
                    i, n = t - 3, (m - 3) % 2
                    for c in range(2):
                        dve.wait_ge(S["p_ok"], count(8 * i + 4 * c + 4))
                        dve.wait_ge(S["pn_ok"], count(2 * (i - 1) + c + 1))
                        V.reciprocal(rden2[:, c, :], den[:, n, c, :]).then_inc(S["rd_ok"], 1)
                        dve.wait_ge(S["rd_ok"], count(2 * i + c + 1))
                        V.tensor_tensor(out=prob[:, n, c, :, :], in0=prob[:, n, c, :, :],
                                        in1=rden2[:, c, :].unsqueeze(2).broadcast_to([P, H2, P]),
                                        op=ALU.mult).then_inc(S["pn_ok"], 1)
                if has(t, 1):
                    dve.wait_ge(S["qk_full"], count(t))
                    dve.wait_ge(S["s_full"], count(2 * (t - 1) - 2))
                    V.tensor_scalar(kT2[:, (m - 1) % 2, :], psQK[:, L1:2 * L1], u_col[:, 1:2], None,
                                    ALU.add).then_inc(S["k_ok"], 1)
                if has(t, 5):
                    dve.wait_ge(S["vo_full"], count(t))
                    dve.wait_ge(S["v2_ok"], count(min(t, NSTEP) if isinstance(t, int) else t))
                    dve.wait_ge(S["y_ok"], count(t - 5))
                    dve.wait_ge(S["xnb2_ok"], count(t - 4))
                    V.tensor_tensor(out=r2[:, :, :], in0=psVO[:, L1:2 * L1].rearrange("p (c d) -> p c d", c=2),
                                    in1=y_all[:, bass.ds((t - 5) * 2, 2), :], op=ALU.add).then_inc(S["r2_ok"], 1)
                    dve.wait_ge(S["r2_ok"], count(t - 4))
                    for c in range(2):
                        V.bn_stats(st_y[:, c, :], r2[:, c, :]).then_inc(S["yst"], 1)
                    for c in range(2):
                        dve.wait_ge(S["yst"], count(2 * (t - 5) + c + 1))
                        dve.sem_inc(S["passed"])
                        last = V.bn_aggr(mv_y[:, c, :], st_y[:, c, :])
                    last.then_inc(S["yagg"], 1)
                if has(t, 8):
                    dve.wait_ge(S["al_full"], count(t - 3))
                    dve.wait_ge(S["att_ok"], count(min(t - 3, NSTEP) if isinstance(t, int) else t - 3))
                    V.tensor_copy(logits[:, bass.ds((t - 8) * 2, 2), :],
                                  psAL[:, L1:L1 + 2 * NE].rearrange("p (c e) -> p c e", c=2)).then_inc(S["lg_ok"], 1)

            pipeline(iteration)(dve)

        @block.scalar
        def _(act):
            A = nc.scalar
            act.wait_ge(S["in_b"], 96)
            act.wait_ge(S["q_zero"], 1)

            def iteration(t, m):
                if has(t, 4):
                    i = t - 4
                    for c in range(2):
                        act.wait_ge(S["pt_full"], count(2 * i + c + 1))
                        act.wait_ge(S["al_full"], count(i))
                        A.activation(probT[:, c, :], psP[c][:, :], ACT.Copy).then_inc(S["pt_ok"], 1)
                if has(t, 2):
                    i, n = t - 2, m % 2
                    for c in range(2):
                        act.wait_ge(S["max_ok"], count(2 * i + c + 1))
                        act.wait_ge(S["pt_full"], count(2 * (i - 2) + c + 1))
                        for h in range(H2):
                            A.activation(prob[:, n, c, h, :], psS[c][:, h * P:(h + 1) * P], ACT.Exp,
                                         bias=nbias[:, c, h:h + 1], scale=SCALE2,
                                         accum_out=den[:, n, c, h:h + 1]).then_inc(S["p_ok"], 1)
                if has(t, 0) or has(t, 7):
                    act.wait_ge(S["xy_full"], count(t + 1))
                    act.wait_ge(S["vo_full"], count(min(t - 1, NSTEP) if isinstance(t, int) else t - 1))
                    act.wait_ge(S["al_full"], count(t - 4))
                    lo, hi = (0 if has(t, 0) else L1), (2 * L1 if has(t, 7) else L1)
                    A.activation(xy[:, m % 2, lo:hi], psXY[:, lo:hi], ACT.Copy).then_inc(S["xy_read"], 1)
                if has(t, 1):
                    act.wait_ge(S["qk_full"], count(t))
                    act.wait_ge(S["s_full"], count(2 * (t - 1) - 2))
                    act.wait_ge(S["k_ok"], count(t))
                    for h in range(H2):
                        mine = slice(C2 * h, C2 * h + C2)
                        last = A.activation(qT2[mine, (m - 1) % 2, h, :], psQK[mine, 0:L1], ACT.Identity,
                                            bias=u_col[mine, 0:1])
                    last.then_inc(S["q_ok"], 1)
                    act.wait_ge(S["vo_full"], count(t))
                    act.wait_ge(S["al_full"], count(t - 4))
                    A.activation(v2[:, (m - 1) % 4, :, :].rearrange("p c d -> p (c d)"), psVO[:, 0:L1],
                                 ACT.Copy).then_inc(S["v2_ok"], 1)
                if has(t, 4):
                    act.wait_ge(S["al_full"], count(t - 3))
                    act.wait_ge(S["vo_full"], count(t))
                    A.activation(attT[:, :], psAL[:, 0:L1], ACT.Identity, bias=u_col[:, 2:3]
                                 ).then_inc(S["att_ok"], 1)

            pipeline(iteration)(act)

        @block.gpsimd
        def _(pool):
            G = nc.gpsimd
            G.memset(qT2[:, :, :, :], 0.0).then_inc(S["q_zero"], 1)
            pool.wait_ge(S["in_b"], 96)

            def scale_of(agg, step, i, mv, ve, nm, rs):
                pool.wait_ge(S[agg], count(i + 1))
                pool.sem_inc(S["passed"])
                G.tensor_scalar(ve[:, :], mv[:, :, 1], EPS, None, ALU.add).then_inc(S[step], 1)
                G.tensor_scalar(nm[:, :], mv[:, :, 0], -1.0, None, ALU.mult).then_inc(S[step], 1)
                pool.wait_ge(S[step], count(2 * i + 2))
                return G.tensor_tensor(rs[:, :], ve[:, :], minus_half[:, :], ALU.pow)

            def ready_x(i, n):
                scale_of("xagg", "xstep", i, mv_x, ve_x, nm_x, rs_x).then_inc(S["xrs_ok"], 1)

            def add_bo(i, n):
                pool.wait_ge(S["xn2_ok"], count(i + 1))
                G.tensor_tensor(y_all[:, bass.ds(i * 2, 2), :], x2n[:, n, :, :],
                                rows[:, 0:1, :].broadcast_to([P, 2, P]), ALU.add).then_inc(S["xnb2_ok"], 1)

            def iteration(t, m):
                if has(t, 0):
                    ready_x(t, m % 2)
                if has(t, 5):
                    i = t - 5
                    scale_of("yagg", "ystep", i, mv_y, ve_y, nm_y, rs_y).then_inc(S["yln_step"], 1)
                    pool.wait_ge(S["yln_step"], count(3 * i + 1))
                    pool.sem_inc(S["passed"])
                    for c in range(2):
                        last = G.tensor_scalar(yn[:, c, :], r2[:, c, :], nm_y[:, c:c + 1], rs_y[:, c:c + 1], ALU.add,
                                               ALU.mult)
                    last.then_inc(S["yln_step"], 1)
                    pool.wait_ge(S["yln_step"], count(3 * i + 2))
                    G.tensor_tensor(yg[:, :, :], yn[:, :, :], rows[:, 1:2, :].broadcast_to([P, 2, P]),
                                    ALU.mult).then_inc(S["yln_step"], 1)
                    pool.wait_ge(S["yln_step"], count(3 * i + 3))
                    pool.wait_ge(S["xy_full"], count(t + 1))
                    G.tensor_tensor(yout[:, (m - 5) % 2, :, :], yg[:, :, :], rows[:, 2:3, :].broadcast_to([P, 2, P]),
                                    ALU.add).then_inc(S["y_ok"], 1)
                    pool.wait_ge(S["y_ok"], count(i + 1))
                    pool.sem_inc(S["passed"])
                    G.tensor_copy(y_all[:, bass.ds(i * 2, 2), :], yout[:, (m - 5) % 2, :, :]).then_inc(S["y_kept"], 1)
                if has(t, 0):
                    add_bo(t, m % 2)

            pipeline(iteration)(pool)

        @block.sync
        def _(sp):
            sp.dma_start(u_nat[:, 0:3, :], Wqkv.rearrange("(k p) d -> p k d", p=P)).then_inc(S["in_w"], 16)
            sp.dma_start(u_nat[:, 3, :], Wo).then_inc(S["in_w"], 16)
            sp.dma_start(wg_nat[:, :], Wg).then_inc(S["in_w"], 16)
            for k in range(3):
                sp.dma_start(u_col[:, k:k + 1], bqkv[k * P:(k + 1) * P].rearrange("(p o) -> p o", o=1),
                             allow_slow_non_contiguous=True).then_inc(S["in_b"], 16)
            for k, row in enumerate((bo, g1, be1)):
                sp.dma_start(rows[:, k, :], row.partition_broadcast(P)).then_inc(S["in_b"], 16)


def experts(nc, w, ident, minus_half, xs, y_all, logits, out):
    W1, b1, W2, b2, g2, be2 = w
    NF = DF // P
    NG = NT // 4
    with ExitStack() as ctx:
        def sb(name, shape, dt=F32):
            return ctx.enter_context(nc.sbuf_tensor(name, shape, dt))

        def pb(name, n):
            return [ctx.enter_context(nc.psum_tensor(f"{name}{k}", [P, 512], F32)) for k in range(n)]

        w1 = sb("w1", [P, NE, DF])
        w2 = sb("w2", [P, NE, NF, P])
        b1_nat = sb("b1_nat", [NE * NF, P])
        b1_col = sb("b1_col", [P, NE * NF])
        b2_row = sb("b2_row", [1, NE, P])
        rows = sb("rows3", [P, 2, P])
        ones = sb("ones", [1, P])
        rank = sb("rank", [P, NE])
        best = sb("best", [P, NT])
        hit = sb("hit", [P, NT, NE])
        mine = sb("mine", [P, NT, NE])
        tmp = sb("tmp", [P, NT, NE])
        yT = sb("yT", [P, 2, 512])
        hT = sb("hT", [P, 2, NF, 512])
        acc = sb("acc", [P, 4, P])
        st_z, mv_z = sb("st_z", [P, 4, 6]), sb("mv_z", [P, 4, 2])
        ve_z, nm_z, rs_z = sb("ve_z", [P, 4]), sb("nm_z", [P, 4]), sb("rs_z", [P, 4])
        mh4 = sb("mh4", [P, 4])
        zn = sb("zn", [P, 4, P])
        zg = sb("zg", [P, 4, P])
        zo = sb("zo", [P, 4, P])
        psT = pb("psT", 1)[0]
        psH, psM = pb("psH", 2), pb("psM", 2)
        names = ["passed", "ld1", "ld2", "ldb", "consts", "route", "b1_full", "b1_ok", "t_full", "t_ok", "h_full", "h_ok",
                 "m_full", "m_ok", "acc_ok", "zst", "zagg", "zstep", "z_ok", "done", "out_ok"]
        S = {n: ctx.enter_context(nc.semaphore("ex_" + n)) for n in names}

        y_flat = y_all[:, :, :].rearrange("p j d -> p (j d)")
        m_flat = mine[:, :, :].rearrange("p j e -> p (j e)")
        block = ctx.enter_context(nc.Block())

        @block.tensor
        def _(pe):
            T = nc.tensor
            pe.wait_ge(S["ldb"], 64)
            T.transpose(psT[:, 0:NE * NF], b1_nat[:, :], ident[0:NE * NF, 0:NE * NF]).then_inc(S["b1_full"], 1)
            pe.wait_ge(S["b1_ok"], 1)
            pe.wait_ge(S["ld1"], 16)
            pe.wait_ge(S["ld2"], 16)
            pe.wait_ge(S["consts"], 1)

            def group(g, n):
                pe.wait_ge(S["t_ok"], count(g))
                pe.wait_ge(S["acc_ok"], count(g + 1))
                for c in range(4):
                    last = T.transpose(psT[:, c * P:(c + 1) * P], acc[:, c, :], ident[:, :])
                last.then_inc(S["t_full"], 1)
                pe.wait_ge(S["t_ok"], count(g + 1))
                for e in range(NE + 1):
                    if e < NE:
                        for f in range(NF):
                            u = e * NF + f
                            pe.wait_ge(S["h_ok"], count((g * NE * NF + u) - 1))
                            T.matmul(psH[u % 2][:, :], w1[:, e, f * P:(f + 1) * P], yT[:, n, :], start=True,
                                     stop=True).then_inc(S["h_full"], 1)
                    if e > 0:
                        d = e - 1
                        pe.wait_ge(S["m_ok"], count(g * NE + d - 1))
                        pe.wait_ge(S["h_ok"], count(g * NE * NF + (d + 1) * NF))
                        for c in range(4):
                            for f in range(NF):
                                T.matmul(psM[d % 2][:, c * P:(c + 1) * P], hT[:, d % 2, f, c * P:(c + 1) * P],
                                         w2[:, d, f, :], start=(f == 0), stop=False)
                            last = T.matmul(psM[d % 2][:, c * P:(c + 1) * P], ones[:, :], b2_row[:, d, :],
                                            start=False, stop=True)
                        last.then_inc(S["m_full"], 1)

            group(0, 0)
            group(1, 1)
            with pe.Fori(0, NG // 2 - 1) as k:
                group(k * 2 + 2, 0)
                group(k * 2 + 3, 1)

        @block.vector
        def _(dve):
            V = nc.vector

            def step(ins, n):
                ins.then_inc(S["route"], 1)
                dve.wait_ge(S["route"], count(n))
            step(V.tensor_reduce(best[:, :], logits[:, :, :], AX.X, ALU.max), 1)
            step(V.tensor_tensor(hit[:, :, :], logits[:, :, :], best[:, :].unsqueeze(2).broadcast_to([P, NT, NE]),
                                 ALU.is_ge), 2)
            dve.wait_ge(S["consts"], 1)
            step(V.tensor_tensor(tmp[:, :, :], hit[:, :, :], rank[:, :].unsqueeze(1).broadcast_to([P, NT, NE]),
                                 ALU.mult), 3)
            step(V.tensor_reduce(best[:, :], tmp[:, :, :], AX.X, ALU.max), 4)
            step(V.tensor_tensor(mine[:, :, :], tmp[:, :, :], best[:, :].unsqueeze(2).broadcast_to([P, NT, NE]),
                                 ALU.is_equal), 5)
            dve.wait_ge(S["b1_full"], 1)
            V.tensor_copy(b1_col[:, :], psT[:, 0:NE * NF]).then_inc(S["b1_ok"], 1)

            def group(g, n):
                dve.wait_ge(S["z_ok"], count(2 * g))
                V.tensor_copy(acc[:, :, :], y_all[:, bass.ds(g * 4, 4), :]).then_inc(S["acc_ok"], 1)
                dve.wait_ge(S["acc_ok"], count(g + 1))
                dve.wait_ge(S["t_full"], count(g + 1))
                for e in range(NE):
                    dve.wait_ge(S["m_full"], count(g * NE + e + 1))
                    if e > 0:
                        dve.wait_ge(S["m_ok"], count(g * NE + e))
                    for c in range(4):
                        last = V.scalar_tensor_tensor(out=acc[:, c, :], in0=psM[e % 2][:, c * P:(c + 1) * P],
                                                      scalar=m_flat[:, bass.ds(g * 32 + c * NE + e, 1)],
                                                      in1=acc[:, c, :], op0=ALU.mult, op1=ALU.add)
                    last.then_inc(S["m_ok"], 1)
                dve.wait_ge(S["m_ok"], count(g * NE + NE))
                for c in range(4):
                    V.bn_stats(st_z[:, c, :], acc[:, c, :]).then_inc(S["zst"], 1)
                for c in range(4):
                    dve.wait_ge(S["zst"], count(8 * g + c + 1))
                    dve.sem_inc(S["passed"])
                    last = V.bn_aggr(mv_z[:, c, :], st_z[:, c, :])
                last.then_inc(S["zagg"], 1)
                dve.wait_ge(S["zstep"], count(8 * g + 5))
                for c in range(4):
                    V.bn_stats(st_z[:, c, :], zo[:, c, :]).then_inc(S["zst"], 1)
                for c in range(4):
                    dve.wait_ge(S["zst"], count(8 * g + 4 + c + 1))
                    dve.sem_inc(S["passed"])
                    last = V.bn_aggr(mv_z[:, c, :], st_z[:, c, :])
                last.then_inc(S["zagg"], 1)

            group(0, 0)
            group(1, 1)
            with dve.Fori(0, NG // 2 - 1) as k:
                group(k * 2 + 2, 0)
                group(k * 2 + 3, 1)

        @block.scalar
        def _(act):
            A = nc.scalar
            act.wait_ge(S["b1_ok"], 1)

            def group(g, n):
                act.wait_ge(S["t_full"], count(g + 1))
                act.wait_ge(S["h_full"], count(g * NE * NF - NE * NF))
                A.activation(yT[:, n, :], psT[:, :], ACT.Copy).then_inc(S["t_ok"], 1)
                for e in range(NE):
                    for f in range(NF):
                        u = e * NF + f
                        act.wait_ge(S["h_full"], count(g * NE * NF + u + 1))
                        act.wait_ge(S["m_full"], count(g * NE + e - 1))
                        A.activation(hT[:, e % 2, f, :], psH[u % 2][:, :], ACT.Relu,
                                     bias=b1_col[:, u:u + 1]).then_inc(S["h_ok"], 1)

            group(0, 0)
            group(1, 1)
            with act.Fori(0, NG // 2 - 1) as k:
                group(k * 2 + 2, 0)
                group(k * 2 + 3, 1)

        @block.gpsimd
        def _(pool):
            G = nc.gpsimd
            G.memset(mh4[:, :], -0.5)
            G.memset(ones[:, :], 1.0)
            for e in range(NE):
                last = G.memset(rank[:, e:e + 1], float(NE - e))
            last.then_inc(S["consts"], 1)
            pool.wait_ge(S["ldb"], 64)

            def group(g, n):
                def scale(n):
                    pool.wait_ge(S["zagg"], count(2 * g + n + 1))
                    pool.sem_inc(S["passed"])
                    G.tensor_scalar(ve_z[:, :], mv_z[:, :, 1], EPS, None, ALU.add).then_inc(S["zstep"], 1)
                    G.tensor_scalar(nm_z[:, :], mv_z[:, :, 0], -1.0, None, ALU.mult).then_inc(S["zstep"], 1)
                    pool.wait_ge(S["zstep"], count(8 * g + 5 * n + 2))
                    G.tensor_tensor(rs_z[:, :], ve_z[:, :], mh4[:, :], ALU.pow).then_inc(S["zstep"], 1)
                    pool.wait_ge(S["zstep"], count(8 * g + 5 * n + 3))
                    pool.sem_inc(S["passed"])

                def apply(dst, src):
                    for c in range(4):
                        last = G.tensor_scalar(dst[:, c, :], src[:, c, :], nm_z[:, c:c + 1], rs_z[:, c:c + 1],
                                               ALU.add, ALU.mult)
                    return last

                scale(0)
                apply(zn, acc).then_inc(S["z_ok"], 1)
                pool.wait_ge(S["z_ok"], count(2 * g + 1))
                G.tensor_tensor(zg[:, :, :], zn[:, :, :], rows[:, 0:1, :].broadcast_to([P, 4, P]),
                                ALU.mult).then_inc(S["zstep"], 1)
                pool.wait_ge(S["zstep"], count(8 * g + 4))
                G.tensor_tensor(zo[:, :, :], zg[:, :, :], rows[:, 1:2, :].broadcast_to([P, 4, P]),
                                ALU.add).then_inc(S["zstep"], 1)
                scale(1)
                apply(zn, zo).then_inc(S["z_ok"], 1)
                pool.wait_ge(S["z_ok"], count(2 * g + 2))
                G.tensor_tensor(xs[:, bass.ds(g * 4, 4), :], xs[:, bass.ds(g * 4, 4), :], zn[:, :, :],
                                ALU.add).then_inc(S["done"], 1)

            group(0, 0)
            group(1, 1)
            with pool.Fori(0, NG // 2 - 1) as k:
                group(k * 2 + 2, 0)
                group(k * 2 + 3, 1)

        @block.sync
        def _(sp):
            sp.dma_start(b1_nat[:, :], b1.rearrange("e (f p) -> (e f) p", p=P)).then_inc(S["ldb"], 16)
            sp.dma_start(b2_row[:, :, :], b2.rearrange("(o e) d -> o e d", o=1)).then_inc(S["ldb"], 16)
            for k, row in enumerate((g2, be2)):
                sp.dma_start(rows[:, k, :], row.partition_broadcast(P)).then_inc(S["ldb"], 16)
            sp.dma_start(w1[:, :, :], W1.rearrange("e d f -> d e f")).then_inc(S["ld1"], 16)
            sp.dma_start(w2[:, :, :, :].rearrange("p e f d -> p (e f) d"), W2.rearrange("e (f p) d -> p (e f) d", p=P)
                         ).then_inc(S["ld2"], 16)
            out_t = out.rearrange("(q r) l d -> q (r l d)", q=B1).rearrange("q (b n) -> (q b) n", b=8)
            for g in range(NG):
                sp.wait_ge(S["done"], count(g + 1))
                sp.dma_start(out_t[:, 4 * g * P:4 * (g + 1) * P],
                             xs[:, 4 * g:4 * g + 4, :].rearrange("p c d -> p (c d)")).then_inc(S["out_ok"], 16)
            sp.wait_ge(S["out_ok"], count(16 * NG))

def build_program(nc, a, out):
    with ExitStack() as ctx:
        ident = ctx.enter_context(nc.sbuf_tensor("ident", [P, P], F32))
        identh = ctx.enter_context(nc.sbuf_tensor("identh", [P, P], BF16))
        minus_half = ctx.enter_context(nc.sbuf_tensor("minus_half", [P, 2], F32))
        xs = ctx.enter_context(nc.sbuf_tensor("xs", [P, NT, P], F32))
        first_layer(nc, a["x"], a["w_qkv"], a["b_qkv"], a["w_o"], a["b_o"], ident, identh, minus_half, xs)
        y_all = ctx.enter_context(nc.sbuf_tensor("y_all", [P, NT, P], F32))
        logits = ctx.enter_context(nc.sbuf_tensor("logits", [P, NT, NE], F32))
        second_attention(nc, [a[k] for k in ("Wqkv", "bqkv", "Wo", "bo", "g1", "be1", "Wg")], ident, identh,
                         minus_half, xs, y_all, logits)
        experts(nc, [a[k] for k in ("W1", "b1", "W2", "b2", "g2", "be2")], ident, minus_half, xs, y_all, logits, out)


def kernel(L0_attn_x, L0_attn_w_qkv, L0_attn_b_qkv, L0_attn_w_o, L0_attn_b_o, L0_ffn_Wqkv, L0_ffn_bqkv, L0_ffn_Wo,
           L0_ffn_bo, L0_ffn_g1, L0_ffn_be1, L0_ffn_g2, L0_ffn_be2, L0_ffn_Wg, L0_ffn_W1, L0_ffn_b1, L0_ffn_W2,
           L0_ffn_b2):
    import numpy as np
    import concourse.bacc as bacc
    from concourse.bass_utils import run_bass_kernel_spmd

    given = {"x": L0_attn_x, "w_qkv": L0_attn_w_qkv, "b_qkv": L0_attn_b_qkv, "w_o": L0_attn_w_o, "b_o": L0_attn_b_o,
             "Wqkv": L0_ffn_Wqkv, "bqkv": L0_ffn_bqkv, "Wo": L0_ffn_Wo, "bo": L0_ffn_bo, "g1": L0_ffn_g1,
             "be1": L0_ffn_be1, "g2": L0_ffn_g2, "be2": L0_ffn_be2, "Wg": L0_ffn_Wg, "W1": L0_ffn_W1,
             "b1": L0_ffn_b1, "W2": L0_ffn_W2, "b2": L0_ffn_b2}
    nc = bacc.Bacc("TRN2", target_bir_lowering=False, num_devices=1)
    arrays, args = {}, {}
    for name, array in given.items():
        arrays[name] = np.ascontiguousarray(array)
        args[name] = nc.dram_tensor(name, arrays[name].shape, mybir.dt.from_np(arrays[name].dtype),
                                    kind="ExternalInput").ap()
    out = nc.dram_tensor("out", (B1, L1, P), F32, kind="ExternalOutput").ap()
    build_program(nc, args, out)
    r = run_bass_kernel_spmd(nc, [arrays], core_ids=[0])
    return r.results[0]["out"]
```

```python
from contextlib import ExitStack

import concourse.bass as bass
from concourse import mybir

F32 = mybir.dt.float32
BF16 = mybir.dt.bfloat16
I32 = mybir.dt.int32
ALU = mybir.AluOpType
ACT = mybir.ActivationFunctionType
AX = mybir.AxisListType

P = 128
B1, L1 = 16, 256
H1, C1 = 16, 8
SCALE1 = 1.0 / float(P) ** 0.5
EPS = 1e-5
NT = B1 * L1 // P
Q_PART = (0, 0, 1, 1, 0, 2)
K_PART = (0, 1, 0, 1, 2, 0)
NPROD = len(Q_PART)
MAX_ROW = 96
HALF = 8
AHEAD = 4
LAST = B1 - 1


def count(value):
    return max(value, 0) if isinstance(value, int) else value


def first_layer(nc, x, w_qkv, b_qkv, w_o, b_o, ident, identh, minus_half, xs):
    with ExitStack() as ctx:
        def sb(name, shape, dt=F32):
            return ctx.enter_context(nc.sbuf_tensor(name, shape, dt))

        def pb(name, shape, dt=F32):
            return ctx.enter_context(nc.psum_tensor(name, shape, dt))

        def sem(name):
            return ctx.enter_context(nc.semaphore(name))

        w_nat = sb("w_nat", [P, 4, P])
        wT = sb("wT", [P, 4, P])
        b_col = sb("b_col", [P, 2])
        bv_col = sb("bv_col", [P, 1])
        one_pair = sb("one_pair", [P, 1])
        bo_row = sb("bo_row", [P, P])
        x_all = sb("x_all", [P, NT, P])
        xnb_all = sb("xnb_all", [P, NT, P])
        xin = sb("xin", [P, 2, 2, P])
        xn = sb("xn", [P, 2, P])
        st = [sb(f"st{k}", [P, 2, 6]) for k in range(3)]
        mv = [sb(f"mv{k}", [P, 2, 2]) for k in range(3)]
        nm = [sb(f"nm{k}", [P, 2]) for k in range(3)]
        ve = [sb(f"ve{k}", [P, 2]) for k in range(3)]
        rs = [sb(f"rs{k}", [P, 2]) for k in range(3)]
        xnT = sb("xnT", [P, L1])
        parts = sb("parts", [P, 2, 3, 2, 2, L1], BF16)
        rest = sb("rest", [P, 2, L1])
        qs = sb("qs", [P, H1, 4, L1], BF16)
        ks = sb("ks", [P, H1, 4, L1], BF16)
        v32 = sb("v32", [P, 4, 2, H1, 32])
        nmax = sb("nmax", [P, 2, H1])
        nmr = sb("nmr", [P, 2, HALF])
        mparts = sb("mparts", [P, 2, 3, HALF], BF16)
        mT = sb("mT", [24, L1], BF16)
        pr = sb("pr", [P, 4, 2, 2, L1])
        osb = sb("osb", [P, 2, 512])
        rden = sb("rden", [P, 2, 8])
        on = sb("on", [P, 2, P])
        onT = sb("onT", [P, L1])
        r1 = sb("r1", [P, 2, P])
        nr = sb("nr", [P, 2, P])

        psA = pb("psA", [P, 2, 512])
        psB = pb("psB", [P, 4, 512])
        psO = pb("psO", [P, 512])
        misc = pb("misc", [P, 512])
        misch = misc[:, :].bitcast(BF16)

        names = ["passed", "ld_w", "ld_b", "ld_x", "consts", "consts_p", "zeroed", "dve_set", "x_in0", "x_in1",
                 "stats0", "stats1", "aggr0", "aggr1", "ln0_step", "ln1_step", "xn_ok", "xnb_ok", "misc_full",
                 "misc_free", "p1_ok", "p2_ok", "p3_ok", "stack0", "stack1", "a_full", "a_free", "split_step",
                 "mp_ok", "mrow0", "mrow1", "b_full", "b_free", "av_done", "o_ev", "rden_ok", "r_ok", "x1_ok",
                 "stored", "v_ok"]
        S = {n: sem(n) for n in names}

        x_t = x.rearrange("b (p c) d -> b p c d", p=P)

        BEFORE, EACH = 13, 8

        def has(k, i):
            done, here, ahead = 1 <= i <= LAST + 1, i <= LAST, i + AHEAD <= LAST
            return (done, here, i + 3 <= LAST or 2 <= i <= LAST + 2, ahead, done, i + 1 <= LAST, ahead, done)[k]

        def use_no(k, i):
            if isinstance(i, int):
                return BEFORE + sum(has(kk, ii) for ii in range(i) for kk in range(EACH)) + sum(
                    has(kk, i) for kk in range(k))
            return i * EACH + (use_no(k, 2) - 2 * EACH)

        def xT_use(b):
            return 1 + 3 * b if isinstance(b, int) and b < AHEAD else use_no(3, b - AHEAD)

        def v_use(b):
            return 2 + 3 * b if isinstance(b, int) and b < 3 else use_no(2, b - 3)

        def qk_use(b):
            if isinstance(b, int) and b < AHEAD:
                return 3 + 3 * b if b < 3 else 11
            return use_no(6, b - AHEAD)

        def max_use(b, hf):
            if hf == 0 and isinstance(b, int) and b == 0:
                return 12
            return use_no(1, b) if hf else use_no(5, b - 1)

        def out_use(b, hf):
            return use_no(4 * hf, b + 1)

        def fits(i, d):
            return not isinstance(i, int) or 0 <= i + d <= LAST

        def stack_count(b, m):
            return (b - m) * (4 * NPROD * 2) + 16 * 2 * NPROD

        def pipeline(eng, iteration):
            iteration(0, 0)
            iteration(1, 1)
            with eng.Fori(0, 2) as four:
                for r in range(2, 6):
                    iteration(four * 4 + r, r % 4)
            for i in range(10, LAST + 3):
                iteration(i, i % 4)

        block = ctx.enter_context(nc.Block())

        @block.tensor
        def _(pe):
            T = nc.tensor
            pe.wait_ge(S["ld_w"], 32)
            pe.wait_ge(S["consts_p"], 1)
            for k in range(4):
                last = T.transpose(misc[:, k * P:(k + 1) * P], w_nat[:, k, :], ident[:, :])
            last.then_inc(S["misc_full"], 1)

            def prep_x(b):
                pe.wait_ge(S["misc_free"], count(xT_use(b)))
                pe.wait_ge(S["xn_ok"], count(b + 1))
                for c in range(2):
                    last = T.transpose(misc[:, c * P:(c + 1) * P], xn[:, c, :], ident[:, :])
                last.then_inc(S["misc_full"], 1)

            def prep_qk(b):
                pe.wait_ge(S["misc_free"], count(qk_use(b)))
                for k in range(2):
                    last = T.matmul(misc[:, k * L1:(k + 1) * L1], wT[:, k, :], xnT[:, :], start=True, stop=True)
                last.then_inc(S["misc_full"], 1)

            def token_major(lhs, k, at):
                for c in range(2):
                    last = T.matmul(misc[:, at + c * P:at + (c + 1) * P], lhs[:, c * P:(c + 1) * P], wT[:, k, :],
                                    start=True, stop=True)
                return last

            def scores_for_max(b, m, g):
                if g == 0:
                    pe.wait_ge(S[f"stack{m // 2}"], count(stack_count(b, m)))
                for c in range(2):
                    pe.wait_ge(S["a_free"], count(16 * b + 2 * g + c - 1))
                    for j in range(2):
                        h = 2 * g + j
                        last = T.matmul(psA[:, c, j * L1:(j + 1) * L1], qs[0:MAX_ROW, h, m, c * P:(c + 1) * P],
                                        ks[0:MAX_ROW, h, m, :], start=True, stop=True)
                    last.then_inc(S["a_full"], 1)

            def scores(b, m, g):
                if g % 4 == 0:
                    pe.wait_ge(S[f"mrow{g // 4}"], count(16 * (b + 1)))
                pe.wait_ge(S["b_free"], count(8 * b + g - 1))
                for j in range(2):
                    h = 2 * g + j
                    for c in range(2):
                        last = T.matmul(psB[:, 2 * (g % 2) + j, c * L1:(c + 1) * L1], ks[:, h, m, c * P:(c + 1) * P],
                                        qs[:, h, m, :], start=True, stop=True)
                last.then_inc(S["b_full"], 1)

            def attend(b, m, q):
                pe.wait_ge(S["b_free"], count(8 * b + 2 * q + 2))
                if q % 2 == 0:
                    pe.wait_ge(S["o_ev"], count(2 * b + q // 2))
                for c in range(2):
                    for j in range(4):
                        g = 2 * q + j // 2
                        last = T.matmul(psO[32 * j:32 * j + 32, (q % 2) * L1:(q % 2 + 1) * L1],
                                        v32[:, m, c, 4 * q + j, :], pr[:, g % 4, j % 2, c, :],
                                        start=(c == 0), stop=(c == 1))
                last.then_inc(S["av_done"], 1)

            def max_rows(b, hf):
                pe.wait_ge(S["misc_free"], count(max_use(b, hf)))
                pe.wait_ge(S["mp_ok"], count(2 * b + hf + 1))
                for c in range(2):
                    last = T.transpose(misch[0:24, c * P:(c + 1) * P],
                                       mparts[:, c, :, :].rearrange("p a h -> p (a h)"), identh[:, :])
                last.then_inc(S["misc_full"], 1)

            def heads_to_tokens(b, hf):
                pe.wait_ge(S["misc_free"], count(out_use(b, hf)))
                pe.wait_ge(S["o_ev"], count(2 * b + hf + 1))
                for c in range(2):
                    for q in range(2):
                        last = T.transpose(misc[:, (2 * c + q) * P:(2 * c + q + 1) * P],
                                           osb[:, hf, q * L1 + c * P:q * L1 + (c + 1) * P], ident[:, :])
                last.then_inc(S["misc_full"], 1)

            def heads_T(i):
                pe.wait_ge(S["misc_free"], count(use_no(7, i)))
                for c in range(2):
                    last = T.transpose(misc[:, c * P:(c + 1) * P], on[:, c, :], ident[:, :])
                last.then_inc(S["misc_full"], 1)

            def iteration(i, m):
                here, next_, done, ahead = fits(i, 0), fits(i, 1), fits(i, -1), fits(i, AHEAD)
                for g in range(8):
                    if here:
                        scores(i, m, g)
                    if next_:
                        scores_for_max(i + 1, (m + 1) % 4, g)
                    if here and g in (2, 4, 6):
                        attend(i, m, g // 2 - 1)
                    if g == 0 and done:
                        attend(i - 1, (m - 1) % 4, 3)
                        heads_to_tokens(i - 1, 0)
                    if g == 1 and here:
                        max_rows(i, 1)
                    if g == 2 and (fits(i, 3) or fits(i, -2)):
                        pe.wait_ge(S["misc_free"], count(use_no(2, i)))
                        if fits(i, 3):
                            last = token_major(xnT, 2, 0)
                        if fits(i, -2):
                            last = token_major(onT, 3, 2 * P)
                        last.then_inc(S["misc_full"], 1)
                    if g == 3 and ahead:
                        prep_x(i + AHEAD)
                    if g == 4 and done:
                        heads_to_tokens(i - 1, 1)
                    if g == 5 and next_:
                        max_rows(i + 1, 0)
                    if g == 6 and ahead:
                        prep_qk(i + AHEAD)
                    if g == 7 and done:
                        heads_T(i)

            for b in range(AHEAD):
                prep_x(b)
                if b < 3:
                    pe.wait_ge(S["misc_free"], count(v_use(b)))
                    token_major(xnT, 2, 0).then_inc(S["misc_full"], 1)
                prep_qk(b)
            pe.wait_ge(S["zeroed"], 3)
            for g in range(8):
                scores_for_max(0, 0, g)
                if g == 5:
                    max_rows(0, 0)
            pipeline(pe, iteration)

        @block.vector
        def _(dve):
            V = nc.vector
            dve.wait_ge(S["misc_full"], 1)
            V.tensor_copy(wT[:, 0:2, :].rearrange("p k (c h) -> p k h c", c=C1),
                          misc[:, 0:2 * P].rearrange("p (k h c) -> p k h c", k=2, c=C1))
            V.tensor_copy(wT[:, 2:4, :].rearrange("p a d -> p (a d)"), misc[:, 2 * P:4 * P]).then_inc(S["misc_free"], 1)

            def ln_stats(kind, b, src):
                for c in range(2):
                    V.bn_stats(st[kind][:, c, :], src[:, c, :]).then_inc(S[f"stats{kind}"], 1)
                for c in range(2):
                    dve.wait_ge(S[f"stats{kind}"], count(2 * b + c + 1))
                    dve.sem_inc(S["passed"])
                    last = V.bn_aggr(mv[kind][:, c, :], st[kind][:, c, :])
                last.then_inc(S[f"aggr{kind}"], 1)

            def stats_x(b, m):
                dve.wait_ge(S[f"x_in{m % 2}"], count((b - m % 2) * 8 + 16))
                dve.wait_ge(S["xn_ok"], count(b))
                ln_stats(0, b, xin[:, m % 2, :, :])

            def split_qk(b, m):
                dve.wait_ge(S["misc_full"], count(qk_use(b) + 1))
                dve.wait_ge(S["p1_ok"], count(2 * b + 2))
                dve.wait_ge(S["p3_ok"], count(b))
                for k in range(2):
                    last = V.scalar_tensor_tensor(out=rest[:, k, :], in0=misc[:, k * L1:(k + 1) * L1],
                                                  scalar=b_col[:, k:k + 1], in1=parts[:, m // 2, 0, k, m % 2, :],
                                                  op0=ALU.add, op1=ALU.subtract)
                last.then_inc(S["misc_free"], 1)
                dve.wait_ge(S["misc_free"], count(qk_use(b) + 1))
                V.tensor_copy(parts[:, m // 2, 1, :, m % 2, :], rest[:, :, :]).then_inc(S["p2_ok"], 1)

            def residual(i):
                dve.wait_ge(S["misc_full"], count(use_no(2, i) + 1))
                if fits(i, 3):
                    dve.wait_ge(S["v_ok"], count(i - 1))
                dve.wait_ge(S["xnb_ok"], count(i - 1))
                dve.wait_ge(S["x1_ok"], count(i - 2))
                V.tensor_tensor(out=r1[:, :, :], in0=misc[:, 2 * P:4 * P].rearrange("p (c d) -> p c d", c=2),
                                in1=xnb_all[:, bass.ds((i - 2) * 2, 2), :], op=ALU.add).then_inc(S["misc_free"], 1)
                dve.wait_ge(S["misc_free"], count(use_no(2, i) + 1))
                ln_stats(1, i - 2, r1)

            def maxima(b, g):
                for c in range(2):
                    dve.wait_ge(S["a_full"], count(16 * b + 2 * g + c + 1))
                    if g % 4 == 0 and c == 0:
                        dve.wait_ge(S["mp_ok"], count(2 * b + g // 4 - 1))
                    V.tensor_reduce(nmax[:, c, 2 * g:2 * g + 2], psA[:, c, :].rearrange("p (h m) -> p h m", h=2),
                                    AX.X, ALU.max, negate=True).then_inc(S["a_free"], 1)

            def normalise(b, hf):
                dve.wait_ge(S["misc_full"], count(out_use(b, hf) + 1))
                o = misc[:, :].rearrange("p (c k r) -> p c k r", c=2, r=32)
                V.reciprocal(rden[:, :, :], o[:, :, :, C1]).then_inc(S["rden_ok"], 1)
                dve.wait_ge(S["rden_ok"], count(2 * b + hf + 1))
                V.tensor_tensor(out=on[:, :, hf * 64:(hf + 1) * 64].rearrange("p c (k e) -> p c k e", e=C1),
                                in0=o[:, :, :, 0:C1],
                                in1=rden[:, :, :].unsqueeze(3).broadcast_to([P, 2, 8, C1]),
                                op=ALU.mult).then_inc(S["misc_free"], 1)

            def iteration(i, m):
                next_, done = fits(i, 1), fits(i, -1)
                for g in range(8):
                    if next_:
                        maxima(i + 1, g)
                    if g == 0 and done:
                        normalise(i - 1, 0)
                    if g == 1 and fits(i, AHEAD):
                        stats_x(i + AHEAD, m)
                    if g == 3 and fits(i, -2):
                        residual(i)
                    if g == 4 and done:
                        normalise(i - 1, 1)
                    if g == 7 and fits(i, AHEAD):
                        split_qk(i + AHEAD, m)

            for b in range(AHEAD):
                stats_x(b, b)
                if b == 1:
                    V.memset(ks[0:MAX_ROW, :, :, :].rearrange("p h b l -> p (h b l)").bitcast(F32),
                             0.0).then_inc(S["zeroed"], 1)
                if b >= 1:
                    split_qk(b - 1, b - 1)
            split_qk(3, 3)
            for g in range(8):
                maxima(0, g)
            pipeline(dve, iteration)

        @block.scalar
        def _(act):
            A = nc.scalar

            def first_parts(b, m):
                act.wait_ge(S["misc_full"], count(qk_use(b) + 1))
                act.wait_ge(S[f"stack{m // 2}"], count(stack_count(b - 4, m)))
                for k in range(2):
                    A.activation(parts[:, m // 2, 0, k, m % 2, :], misc[:, k * L1:(k + 1) * L1], ACT.Identity,
                                 bias=b_col[:, k:k + 1]).then_inc(S["p1_ok"], 1)

            def copy_out(dst, src, n):
                act.wait_ge(S["misc_full"], count(n + 1))
                A.activation(dst, src, ACT.Copy).then_inc(S["misc_free"], 1)

            def max_rows(b, hf):
                act.wait_ge(S[f"mrow{hf}"], count(16 * b))
                act.wait_ge(S[f"mrow{1 - hf}"], count(16 * (b + hf)))
                copy_out(mT[:, :], misch[0:24, 0:L1], max_use(b, hf))

            def out_rows(b, hf):
                act.wait_ge(S["av_done"], count(4 * b + 2 * hf + 2))
                act.wait_ge(S["misc_full"], count(out_use(b - 1, hf) + 1 if not isinstance(b, int) or b >= 1 else 0))
                A.activation(osb[:, hf, :], psO[:, :], ACT.Copy).then_inc(S["o_ev"], 1)

            def v_in(b, m, only):
                act.wait_ge(S["misc_full"], count(v_use(b) + 1))
                A.activation(v32[:, m, :, :, 0:C1], misc[:, 0:2 * P].rearrange("p (a h c) -> p a h c", a=2, c=C1),
                             ACT.Copy).then_inc(S["misc_free" if only else "v_ok"], 1)

            def iteration(i, m):
                here, next_, done, ahead = fits(i, 0), fits(i, 1), fits(i, -1), fits(i, AHEAD)
                for g in range(8):
                    if here:
                        act.wait_ge(S["b_full"], count(8 * i + g + 1))
                        act.wait_ge(S["av_done"], count(4 * i + (g - 4) // 2 + 1))
                        A.activation(pr[:, g % 4, :, :, :].rearrange("p j c l -> p (j c l)"),
                                     psB[:, 2 * (g % 2):2 * (g % 2) + 2, :].rearrange("p a n -> p (a n)"),
                                     ACT.Exp, scale=SCALE1).then_inc(S["b_free"], 1)
                    if g == 0 and done:
                        out_rows(i - 1, 1)
                    if g == 1 and here:
                        max_rows(i, 1)
                    if g == 2 and fits(i, 3):
                        v_in(i + 3, (m + 3) % 4, isinstance(i, int) and i < 2)
                    if g == 3 and ahead:
                        copy_out(xnT[:, :], misc[:, 0:L1], xT_use(i + AHEAD))
                    if g == 4 and here:
                        out_rows(i, 0)
                    if g == 5 and next_:
                        max_rows(i + 1, 0)
                    if g == 6 and ahead:
                        first_parts(i + AHEAD, m)
                    if g == 7 and done:
                        act.wait_ge(S["misc_full"], count(use_no(7, i) + 1))
                        A.activation(onT[:, :], misc[:, 0:L1], ACT.Identity, bias=bv_col[:, :]
                                     ).then_inc(S["misc_free"], 1)

            act.wait_ge(S["consts"], 1)
            A.activation(ks[MAX_ROW:P, :, :, :].rearrange("p h b l -> p (h b l)").bitcast(F32),
                         one_pair[MAX_ROW:P, :].broadcast_to([P - MAX_ROW, H1 * 2 * L1]),
                         ACT.Copy).then_inc(S["zeroed"], 1)
            act.wait_ge(S["ld_b"], 64)
            for b in range(AHEAD):
                copy_out(xnT[:, :], misc[:, 0:L1], xT_use(b))
                if b < 3:
                    v_in(b, b, True)
                first_parts(b, b)
            max_rows(0, 0)
            pipeline(act, iteration)

        @block.gpsimd
        def _(pool):
            G = nc.gpsimd
            G.memset(minus_half[:, :], -0.5)
            G.memset(one_pair[:, :].bitcast(BF16), 1.0)
            G.memset(ident[:, :], 0.0).then_inc(S["consts"], 1)
            pool.wait_ge(S["consts"], 1)
            G.affine_select(out=ident[:, :], in_=ident[:, :], compare_op=ALU.not_equal, fill=1.0, base=0,
                            pattern=[[-1, P]], channel_multiplier=1).then_inc(S["consts"], 1)
            pool.wait_ge(S["consts"], 2)
            pool.sem_inc(S["passed"])
            G.tensor_copy(identh[:, :], ident[:, :]).then_inc(S["consts_p"], 1)

            def ln_scale(kind, b):
                step, before = f"ln{kind}_step", (3 + kind) * b
                pool.wait_ge(S[f"aggr{kind}"], count(b + 1))
                pool.sem_inc(S["passed"])
                G.tensor_scalar(ve[kind][:, :], mv[kind][:, :, 1], EPS, None, ALU.add).then_inc(S[step], 1)
                G.tensor_scalar(nm[kind][:, :], mv[kind][:, :, 0], -1.0, None, ALU.mult).then_inc(S[step], 1)
                pool.wait_ge(S[step], count(before + 1))
                G.tensor_tensor(rs[kind][:, :], ve[kind][:, :], minus_half[:, :], ALU.pow).then_inc(S[step], 1)
                pool.wait_ge(S[step], count(before + 3))
                pool.sem_inc(S["passed"])

            def norm_x(b, m):
                ln_scale(0, b)
                if not isinstance(b, int) or b >= 1:
                    pool.wait_ge(S["misc_full"], count(xT_use(b - 1) + 1))
                    pool.sem_inc(S["passed"])
                for c in range(2):
                    last = G.tensor_scalar(xn[:, c, :], xin[:, m % 2, c, :], nm[0][:, c:c + 1], rs[0][:, c:c + 1],
                                           ALU.add, ALU.mult)
                last.then_inc(S["xn_ok"], 1)
                pool.wait_ge(S["xn_ok"], count(b + 1))
                G.tensor_tensor(xnb_all[:, bass.ds(b * 2, 2), :], xn[:, :, :],
                                bo_row[:, :].unsqueeze(1).broadcast_to([P, 2, P]), ALU.add).then_inc(S["xnb_ok"], 1)

            def last_parts(b, m):
                pool.wait_ge(S["p2_ok"], count(b + 1))
                G.tensor_tensor(parts[:, m // 2, 2, :, m % 2, :], rest[:, :, :], parts[:, m // 2, 1, :, m % 2, :],
                                ALU.subtract).then_inc(S["p3_ok"], 1)

            def split_max(b, hf):
                src = nmax[:, :, hf * HALF:(hf + 1) * HALF]
                n = 3 * (2 * b + hf)
                pool.wait_ge(S["a_free"], count(16 * b + 8 * hf + 8))
                if not isinstance(b, int) or b + hf > 0:
                    pool.wait_ge(S["misc_full"], count((max_use(b, 0) if hf else max_use(b - 1, 1)) + 1))
                    pool.sem_inc(S["passed"])
                G.tensor_copy(mparts[:, :, 0, :], src).then_inc(S["split_step"], 1)
                pool.wait_ge(S["split_step"], count(n + 1))
                G.tensor_tensor(nmr[:, :, :], src, mparts[:, :, 0, :], ALU.subtract).then_inc(S["split_step"], 1)
                pool.wait_ge(S["split_step"], count(n + 2))
                pool.sem_inc(S["passed"])
                G.tensor_copy(mparts[:, :, 1, :], nmr[:, :, :]).then_inc(S["split_step"], 1)
                pool.wait_ge(S["split_step"], count(n + 3))
                G.tensor_tensor(mparts[:, :, 2, :], nmr[:, :, :], mparts[:, :, 1, :],
                                ALU.subtract).then_inc(S["mp_ok"], 1)

            def add_attention(b):
                ln_scale(1, b)
                for c in range(2):
                    last = G.tensor_scalar(nr[:, c, :], r1[:, c, :], nm[1][:, c:c + 1], rs[1][:, c:c + 1],
                                           ALU.add, ALU.mult)
                last.then_inc(S["ln1_step"], 1)
                pool.wait_ge(S["ln1_step"], count(4 * b + 4))
                G.tensor_tensor(x_all[:, bass.ds(b * 2, 2), :], nr[:, :, :], x_all[:, bass.ds(b * 2, 2), :],
                                ALU.add).then_inc(S["x1_ok"], 1)

            def iteration(i, m):
                if fits(i, 0):
                    split_max(i, 1)
                if fits(i, AHEAD):
                    norm_x(i + AHEAD, m)
                if fits(i, 1):
                    split_max(i + 1, 0)
                if fits(i, AHEAD):
                    last_parts(i + AHEAD, m)
                if fits(i, -2):
                    add_attention(i - 2)

            G.memset(v32[:, :, :, :, C1 + 1:32], 0.0)
            G.memset(v32[:, :, :, :, C1:C1 + 1], 1.0)
            pool.wait_ge(S["ld_b"], 64)
            pool.wait_ge(S["ld_x"], 16)
            norm_x(0, 0)
            for b in range(1, AHEAD):
                norm_x(b, b)
                if b == 1:
                    G.memset(qs[:, :, :, :].rearrange("p h b l -> p (h b l)").bitcast(F32),
                             0.0).then_inc(S["zeroed"], 1)
                last_parts(b - 1, b - 1)
            last_parts(3, 3)
            split_max(0, 0)
            pipeline(pool, iteration)

        @block.sync
        def _(sp):
            def load_x(b, m):
                sp.wait_ge(S["xn_ok"], count(b - 1))
                sp.dma_start(xin[:, m % 2, :, :], x_t[b]).then_inc(S[f"x_in{m % 2}"], 16)

            def stack(b, m):
                sp.wait_ge(S["p3_ok"], count(b + 2))
                if not isinstance(b, int) or b >= 4:
                    sp.wait_ge(S["b_full"], count(8 * (b - 2)))
                for dst, k, which in ((qs, 0, Q_PART), (ks, 1, K_PART)):
                    for j, part in enumerate(which):
                        sp.dma_start(dst[C1 * j:C1 * (j + 1), :, m:m + 2, :].rearrange("c h b l -> c h (b l)"),
                                     parts[:, m // 2, part, k, :, :].rearrange("p b l -> p (b l)")
                                     ).then_inc(S[f"stack{m // 2}"], 16)

            def max_rows(b, m, hf):
                sp.wait_ge(S["misc_free"], count(max_use(b, hf) + 1))
                sp.dma_start(qs[MAX_ROW:MAX_ROW + 3, hf * HALF:(hf + 1) * HALF, m, :],
                             mT[:, :]).then_inc(S[f"mrow{hf}"], 16)

            def iteration(i, m):
                if fits(i, AHEAD):
                    load_x(i + AHEAD, m)
                if fits(i, 0):
                    max_rows(i, m, 1)
                if m % 2 == 0 and fits(i, 2):
                    stack(i + 2, (m + 2) % 4)
                if fits(i, 1):
                    max_rows(i + 1, (m + 1) % 4, 0)
                if not isinstance(i, int):
                    pass
                elif i >= 10:
                    for b in range((0 if i == 10 else i - 3), i - 2):
                        x1_over(b)

            def x1_over(b):
                sp.wait_ge(S["x1_ok"], count(b + 1))
                sp.dma_start(xs[(L1 // 32) * b:(L1 // 32) * (b + 1), :, :].rearrange("p j d -> p (j d)"),
                             x_all[:, 2 * b:2 * b + 2, :].rearrange("p c d -> p (c d)")).then_inc(S["stored"], 16)

            load_x(0, 0)
            load_x(1, 1)
            sp.dma_start(w_nat[:, 0:3, :], w_qkv.rearrange("(k p) d -> p k d", p=P)).then_inc(S["ld_w"], 16)
            sp.dma_start(w_nat[:, 3, :], w_o).then_inc(S["ld_w"], 16)
            for k in range(2):
                sp.dma_start(b_col[:, k:k + 1], b_qkv[k * P:(k + 1) * P].rearrange("(h c o) -> c h o", c=C1, o=1),
                             allow_slow_non_contiguous=True).then_inc(S["ld_b"], 16)
            sp.dma_start(bv_col[:, :], b_qkv[2 * P:3 * P].rearrange("(p o) -> p o", o=1),
                         allow_slow_non_contiguous=True).then_inc(S["ld_b"], 16)
            sp.dma_start(bo_row[:, :], b_o.partition_broadcast(P)).then_inc(S["ld_b"], 16)
            sp.dma_start(x_all[:, :, :].rearrange("p (b c) d -> p b c d", c=2),
                         x.rearrange("b (p c) d -> p b c d", p=P)).then_inc(S["ld_x"], 16)
            load_x(2, 2)
            load_x(3, 3)
            sp.wait_ge(S["zeroed"], 3)
            stack(0, 0)
            max_rows(0, 0, 0)
            pipeline(sp, iteration)
            x1_over(LAST)
            sp.wait_ge(S["stored"], count(16 * B1))


H2, C2 = 4, 32
S2 = B1
SCALE2 = 1.0 / float(C2) ** 0.5
NSTEP = NT // 2
NE, DF = 8, 512


def second_attention(nc, w, ident, identh, minus_half, xs, y_all, logits, loaded, loads, y_sorted):
    Wqkv, bqkv, Wo, bo, g1, be1, Wg = w
    with ExitStack() as ctx:
        def sb(name, shape, dt=F32):
            return ctx.enter_context(nc.sbuf_tensor(name, shape, dt))

        def pb(name):
            return ctx.enter_context(nc.psum_tensor(name, [P, 512], F32))

        u_nat = sb("u_nat", [P, 4, P])
        wg_nat = sb("wg_nat", [NE, P])
        uT = sb("uT", [P, 4, P])
        wgT = sb("wgT", [P, NE])
        u_col = sb("u_col", [P, 3])
        rows = sb("rows", [P, 3, P])
        NZ = NS * P // 3
        zeros = sb("zeros", [P, NZ])
        same = sb("same", [P, 8])
        mask = sb("mask", [P, P], BF16)
        x2n = sb("x2n", [P, 2, 2, P])
        st_x, st_y = sb("st_x", [P, 2, 6]), sb("st_y", [P, 2, 6])
        mv_x, mv_y = sb("mv_x", [P, 2, 2]), sb("mv_y", [P, 2, 2])
        ve_x, ve_y = sb("ve_x", [P, 2]), sb("ve_y", [P, 2])
        nm_x, nm_y = sb("nm_x", [P, 2]), sb("nm_y", [P, 2])
        rs_x, rs_y = sb("rs_x", [P, 2]), sb("rs_y", [P, 2])
        xy = sb("xy", [P, 2, 512])
        qT2 = sb("qT2", [P, 2, H2, L1])
        kT2 = sb("kT2", [P, 2, L1])
        v2 = sb("v2", [P, 4, 2, P])
        nmax2 = sb("nmax2", [P, 2, H2])
        nbias = sb("nbias", [P, 2, H2])
        den = sb("den", [P, 2, 2, H2])
        rden2 = sb("rden2", [P, 2, H2])
        prob = sb("prob", [P, 2, 2, H2, P])
        probT = sb("probT", [P, 2, 512])
        attT = sb("attT", [P, L1])
        r2 = sb("r2", [P, 2, P])
        yn = sb("yn", [P, 2, P])
        yg = sb("yg", [P, 2, P])
        yout = sb("yout", [P, 2, 2, P])
        xs_flat = xs[:, :, :].rearrange("p j d -> p (j d)")
        psXY, psQK, psVO, psAL = pb("psXY"), pb("psQK"), pb("psVO"), pb("psAL")
        psS = [pb("psS0"), pb("psS1")]
        psP = [pb("psP0"), pb("psP1")]

        names = ["passed", "in_w", "in_b", "wT_full", "wT_ok", "same_ok", "zeros_ok", "zeroed", "q_zero", "mask_ok", "xst", "xagg", "xstep", "xrs_ok", "xn2_ok",
                 "xnb2_ok", "xy_full", "xy_read", "qk_full", "q_ok", "k_ok", "vo_full", "v2_ok", "r2_ok", "s_full",
                 "m_step", "max_ok", "p_ok", "rd_ok", "pn_ok", "pt_full", "pt_ok", "al_full", "att_ok", "lg_ok",
                 "yst", "yagg", "ystep", "yln_step", "y_ok", "y_kept"]
        S = {n: ctx.enter_context(nc.semaphore("l2_" + n)) for n in names}

        def has(t, lag):
            return not isinstance(t, int) or 0 <= t - lag < NSTEP

        def pipeline(iteration):
            def run(eng):
                for t in range(8):
                    iteration(t, t)
                with eng.Fori(0, 2) as four:
                    for r in range(4):
                        iteration(four * 4 + (8 + r), r)
                for t in range(16, NSTEP + 8):
                    iteration(t, t % 4)
            return run

        block = ctx.enter_context(nc.Block())

        @block.tensor
        def _(pe):
            T = nc.tensor
            pe.wait_ge(S["in_w"], 48)
            for k in range(4):
                last = T.transpose(psS[0][:, k * P:(k + 1) * P], u_nat[:, k, :], ident[:, :])
            last = T.transpose(psS[1][:, 0:NE], wg_nat[:, :], ident[0:NE, 0:NE])
            last.then_inc(S["wT_full"], 1)
            pe.wait_ge(S["wT_ok"], 2)
            pe.wait_ge(S["mask_ok"], 1)

            def iteration(t, m):
                if has(t, 2):
                    i, n = t - 2, (m - 2) % 2
                    pe.wait_ge(S["q_ok"], count(i + 1))
                    pe.wait_ge(S["k_ok"], count(i + 1))
                    for c in range(2):
                        pe.wait_ge(S["p_ok"], count(8 * (i - 1) + 4 * c + 4))
                        for h in range(H2):
                            at = psS[c][:, h * P:(h + 1) * P]
                            T.matmul(at, identh[:, :], mask[:, :], start=True, stop=False)
                            last = T.matmul(at, qT2[:, n, h, c * P:(c + 1) * P],
                                            kT2[:, n, c * P:(c + 1) * P], start=False, stop=True)
                        last.then_inc(S["s_full"], 1)
                if has(t, 1):
                    pe.wait_ge(S["xy_read"], count(t))
                    pe.wait_ge(S["q_ok"], count(t - 1))
                    pe.wait_ge(S["k_ok"], count(t - 1))
                    for k in range(2):
                        last = T.matmul(psQK[:, k * L1:(k + 1) * L1], uT[:, k, :], xy[:, (m - 1) % 2, 0:L1],
                                        start=True, stop=True)
                    last.then_inc(S["qk_full"], 1)
                if has(t, 1) or has(t, 5):
                    pe.wait_ge(S["v2_ok"], count(min(t - 1, NSTEP) if isinstance(t, int) else t - 1))
                    pe.wait_ge(S["r2_ok"], count(t - 5))
                    if has(t, 1):
                        for c in range(2):
                            last = T.matmul(psVO[:, c * P:(c + 1) * P], xy[:, (m - 1) % 2, c * P:(c + 1) * P],
                                            uT[:, 2, :], start=True, stop=True)
                    if has(t, 5):
                        pe.wait_ge(S["att_ok"], count(t - 4))
                        for c in range(2):
                            last = T.matmul(psVO[:, (2 + c) * P:(3 + c) * P], attT[:, c * P:(c + 1) * P],
                                            uT[:, 3, :], start=True, stop=True)
                    last.then_inc(S["vo_full"], 1)
                if has(t, 4) or has(t, 8):
                    pe.wait_ge(S["att_ok"], count(min(t - 4, NSTEP) if isinstance(t, int) else t - 4))
                    pe.wait_ge(S["lg_ok"], count(t - 8))
                    if has(t, 4):
                        pe.wait_ge(S["pt_ok"], count(2 * (t - 4) + 2))
                        pe.wait_ge(S["v2_ok"], count(t - 3))
                        for c in range(2):
                            for h in range(H2):
                                last = T.matmul(psAL[C2 * h:C2 * h + C2, c * P:(c + 1) * P],
                                                v2[:, m % 4, c, C2 * h:C2 * h + C2],
                                                probT[:, c, h * P:(h + 1) * P], start=True, stop=True,
                                                tile_position=(0, C2 * h))
                    if has(t, 8):
                        pe.wait_ge(S["xy_read"], count(t))
                        for c in range(2):
                            last = T.matmul(psAL[:, L1 + NE * c:L1 + NE * (c + 1)],
                                            xy[:, (m - 1) % 2, (2 + c) * P:(3 + c) * P], wgT[:, :], start=True,
                                            stop=True)
                    last.then_inc(S["al_full"], 1)
                if has(t, 0) or has(t, 7):
                    pe.wait_ge(S["xy_read"], count(t))
                    if has(t, 0):
                        pe.wait_ge(S["xn2_ok"], count(t + 1))
                        for c in range(2):
                            last = T.transpose(psXY[:, c * P:(c + 1) * P], x2n[:, m % 2, c, :], ident[:, :])
                    if has(t, 7):
                        pe.wait_ge(S["y_ok"], count(t - 6))
                        for c in range(2):
                            last = T.transpose(psXY[:, (2 + c) * P:(3 + c) * P], yout[:, (m - 7) % 2, c, :], ident[:, :])
                    last.then_inc(S["xy_full"], 1)
                if has(t, 3):
                    i = t - 3
                    for c in range(2):
                        pe.wait_ge(S["pn_ok"], count(2 * i + c + 1))
                        pe.wait_ge(S["pt_ok"], count(2 * (i - 1) + c + 1))
                        for h in range(H2):
                            last = T.transpose(psP[c][:, h * P:(h + 1) * P], prob[:, (m - 3) % 2, c, h, :],
                                               ident[:, :])
                        last.then_inc(S["pt_full"], 1)

            pipeline(iteration)(pe)

        @block.vector
        def _(dve):
            V = nc.vector
            V.tensor_reduce(same[:, :], ident[:, :].rearrange("p (s r) -> p r s", r=8), AX.X,
                            ALU.add).then_inc(S["same_ok"], 1)
            dve.wait_ge(S["same_ok"], 1)
            V.tensor_scalar(mask[:, :].rearrange("p (s r) -> p s r", r=8),
                            same[:, :].unsqueeze(1).broadcast_to([P, S2, 8]), -1.0, 1e30, ALU.add,
                            ALU.mult).then_inc(S["mask_ok"], 1)
            dve.wait_ge(S["wT_full"], 1)
            V.tensor_copy(uT[:, :, :].rearrange("p k d -> p (k d)"), psS[0][:, :]).then_inc(S["wT_ok"], 1)
            V.tensor_copy(wgT[:, :], psS[1][:, 0:NE]).then_inc(S["wT_ok"], 1)
            dve.wait_ge(S["in_b"], 96)

            def norm_x(i, n):
                dve.wait_ge(S["xn2_ok"], count(i))
                for c in range(2):
                    V.bn_stats(st_x[:, c, :], xs_flat[:, bass.ds(i * L1 + c * P, P)]).then_inc(S["xst"], 1)
                for c in range(2):
                    dve.wait_ge(S["xst"], count(2 * i + c + 1))
                    dve.sem_inc(S["passed"])
                    last = V.bn_aggr(mv_x[:, c, :], st_x[:, c, :])
                last.then_inc(S["xagg"], 1)

            def apply_x(i, n):
                dve.wait_ge(S["xrs_ok"], count(i + 1))
                dve.wait_ge(S["xnb2_ok"], count(i - 1))
                dve.wait_ge(S["xy_full"], count(i - 1))
                for c in range(2):
                    last = V.tensor_scalar(x2n[:, n, c, :], xs_flat[:, bass.ds(i * L1 + c * P, P)], nm_x[:, c:c + 1], rs_x[:, c:c + 1],
                                           ALU.add, ALU.mult)
                last.then_inc(S["xn2_ok"], 1)

            def iteration(t, m):
                if has(t, 0):
                    norm_x(t, m % 2)
                if has(t, 2):
                    i = t - 2
                    for c in range(2):
                        dve.wait_ge(S["s_full"], count(2 * i + c + 1))
                        V.tensor_reduce(nmax2[:, c, :], psS[c][:, :].rearrange("p (h k) -> p h k", h=H2), AX.X,
                                        ALU.max, negate=True).then_inc(S["m_step"], 1)
                        dve.wait_ge(S["m_step"], count(2 * i + c + 1))
                        dve.wait_ge(S["p_ok"], count(8 * (i - 1) + 4 * c + 4))
                        V.tensor_scalar(nbias[:, c, :], nmax2[:, c, :], SCALE2, None,
                                        ALU.mult).then_inc(S["max_ok"], 1)
                if has(t, 0):
                    apply_x(t, m % 2)
                if has(t, 3):
                    i, n = t - 3, (m - 3) % 2
                    for c in range(2):
                        dve.wait_ge(S["p_ok"], count(8 * i + 4 * c + 4))
                        dve.wait_ge(S["pn_ok"], count(2 * (i - 1) + c + 1))
                        V.reciprocal(rden2[:, c, :], den[:, n, c, :]).then_inc(S["rd_ok"], 1)
                        dve.wait_ge(S["rd_ok"], count(2 * i + c + 1))
                        V.tensor_tensor(out=prob[:, n, c, :, :], in0=prob[:, n, c, :, :],
                                        in1=rden2[:, c, :].unsqueeze(2).broadcast_to([P, H2, P]),
                                        op=ALU.mult).then_inc(S["pn_ok"], 1)
                if has(t, 1):
                    dve.wait_ge(S["qk_full"], count(t))
                    dve.wait_ge(S["s_full"], count(2 * (t - 1) - 2))
                    V.tensor_scalar(kT2[:, (m - 1) % 2, :], psQK[:, L1:2 * L1], u_col[:, 1:2], None,
                                    ALU.add).then_inc(S["k_ok"], 1)
                if has(t, 5):
                    dve.wait_ge(S["vo_full"], count(t))
                    dve.wait_ge(S["v2_ok"], count(min(t, NSTEP) if isinstance(t, int) else t))
                    dve.wait_ge(S["y_ok"], count(t - 5))
                    dve.wait_ge(S["xnb2_ok"], count(t - 4))
                    V.tensor_tensor(out=r2[:, :, :], in0=psVO[:, L1:2 * L1].rearrange("p (c d) -> p c d", c=2),
                                    in1=y_all[:, bass.ds((t - 5) * 2, 2), :], op=ALU.add).then_inc(S["r2_ok"], 1)
                    dve.wait_ge(S["r2_ok"], count(t - 4))
                    for c in range(2):
                        V.bn_stats(st_y[:, c, :], r2[:, c, :]).then_inc(S["yst"], 1)
                    for c in range(2):
                        dve.wait_ge(S["yst"], count(2 * (t - 5) + c + 1))
                        dve.sem_inc(S["passed"])
                        last = V.bn_aggr(mv_y[:, c, :], st_y[:, c, :])
                    last.then_inc(S["yagg"], 1)
                if has(t, 8):
                    dve.wait_ge(S["al_full"], count(t - 3))
                    dve.wait_ge(S["att_ok"], count(min(t - 3, NSTEP) if isinstance(t, int) else t - 3))
                    V.tensor_copy(logits[:, bass.ds((t - 8) * 2, 2), :],
                                  psAL[:, L1:L1 + 2 * NE].rearrange("p (c e) -> p c e", c=2)).then_inc(S["lg_ok"], 1)

            pipeline(iteration)(dve)

        @block.scalar
        def _(act):
            A = nc.scalar
            act.wait_ge(S["in_b"], 96)
            act.wait_ge(S["q_zero"], 1)

            def iteration(t, m):
                if has(t, 4):
                    i = t - 4
                    for c in range(2):
                        act.wait_ge(S["pt_full"], count(2 * i + c + 1))
                        act.wait_ge(S["al_full"], count(i))
                        A.activation(probT[:, c, :], psP[c][:, :], ACT.Copy).then_inc(S["pt_ok"], 1)
                if has(t, 2):
                    i, n = t - 2, m % 2
                    for c in range(2):
                        act.wait_ge(S["max_ok"], count(2 * i + c + 1))
                        act.wait_ge(S["pt_full"], count(2 * (i - 2) + c + 1))
                        for h in range(H2):
                            A.activation(prob[:, n, c, h, :], psS[c][:, h * P:(h + 1) * P], ACT.Exp,
                                         bias=nbias[:, c, h:h + 1], scale=SCALE2,
                                         accum_out=den[:, n, c, h:h + 1]).then_inc(S["p_ok"], 1)
                if has(t, 0) or has(t, 7):
                    act.wait_ge(S["xy_full"], count(t + 1))
                    act.wait_ge(S["vo_full"], count(min(t - 1, NSTEP) if isinstance(t, int) else t - 1))
                    act.wait_ge(S["al_full"], count(t - 4))
                    lo, hi = (0 if has(t, 0) else L1), (2 * L1 if has(t, 7) else L1)
                    A.activation(xy[:, m % 2, lo:hi], psXY[:, lo:hi], ACT.Copy).then_inc(S["xy_read"], 1)
                if has(t, 1):
                    act.wait_ge(S["qk_full"], count(t))
                    act.wait_ge(S["s_full"], count(2 * (t - 1) - 2))
                    act.wait_ge(S["k_ok"], count(t))
                    for h in range(H2):
                        mine = slice(C2 * h, C2 * h + C2)
                        last = A.activation(qT2[mine, (m - 1) % 2, h, :], psQK[mine, 0:L1], ACT.Identity,
                                            bias=u_col[mine, 0:1])
                    last.then_inc(S["q_ok"], 1)
                    act.wait_ge(S["vo_full"], count(t))
                    act.wait_ge(S["al_full"], count(t - 4))
                    A.activation(v2[:, (m - 1) % 4, :, :].rearrange("p c d -> p (c d)"), psVO[:, 0:L1],
                                 ACT.Copy).then_inc(S["v2_ok"], 1)
                if has(t, 4):
                    act.wait_ge(S["al_full"], count(t - 3))
                    act.wait_ge(S["vo_full"], count(t))
                    A.activation(attT[:, :], psAL[:, 0:L1], ACT.Identity, bias=u_col[:, 2:3]
                                 ).then_inc(S["att_ok"], 1)

            pipeline(iteration)(act)

        @block.gpsimd
        def _(pool):
            G = nc.gpsimd
            G.memset(zeros[:, :], 0.0).then_inc(S["zeros_ok"], 1)
            G.memset(qT2[:, :, :, :], 0.0).then_inc(S["q_zero"], 1)
            pool.wait_ge(S["in_b"], 96)

            def scale_of(agg, step, i, mv, ve, nm, rs):
                pool.wait_ge(S[agg], count(i + 1))
                pool.sem_inc(S["passed"])
                G.tensor_scalar(ve[:, :], mv[:, :, 1], EPS, None, ALU.add).then_inc(S[step], 1)
                G.tensor_scalar(nm[:, :], mv[:, :, 0], -1.0, None, ALU.mult).then_inc(S[step], 1)
                pool.wait_ge(S[step], count(2 * i + 2))
                return G.tensor_tensor(rs[:, :], ve[:, :], minus_half[:, :], ALU.pow)

            def ready_x(i, n):
                scale_of("xagg", "xstep", i, mv_x, ve_x, nm_x, rs_x).then_inc(S["xrs_ok"], 1)

            def add_bo(i, n):
                pool.wait_ge(S["xn2_ok"], count(i + 1))
                G.tensor_tensor(y_all[:, bass.ds(i * 2, 2), :], x2n[:, n, :, :],
                                rows[:, 0:1, :].broadcast_to([P, 2, P]), ALU.add).then_inc(S["xnb2_ok"], 1)

            def iteration(t, m):
                if has(t, 0):
                    ready_x(t, m % 2)
                if has(t, 5):
                    i = t - 5
                    scale_of("yagg", "ystep", i, mv_y, ve_y, nm_y, rs_y).then_inc(S["yln_step"], 1)
                    pool.wait_ge(S["yln_step"], count(3 * i + 1))
                    pool.sem_inc(S["passed"])
                    for c in range(2):
                        last = G.tensor_scalar(yn[:, c, :], r2[:, c, :], nm_y[:, c:c + 1], rs_y[:, c:c + 1], ALU.add,
                                               ALU.mult)
                    last.then_inc(S["yln_step"], 1)
                    pool.wait_ge(S["yln_step"], count(3 * i + 2))
                    G.tensor_tensor(yg[:, :, :], yn[:, :, :], rows[:, 1:2, :].broadcast_to([P, 2, P]),
                                    ALU.mult).then_inc(S["yln_step"], 1)
                    pool.wait_ge(S["yln_step"], count(3 * i + 3))
                    pool.wait_ge(S["xy_full"], count(t + 1))
                    G.tensor_tensor(yout[:, (m - 5) % 2, :, :], yg[:, :, :], rows[:, 2:3, :].broadcast_to([P, 2, P]),
                                    ALU.add).then_inc(S["y_ok"], 1)
                    pool.wait_ge(S["y_ok"], count(i + 1))
                    pool.sem_inc(S["passed"])
                    G.tensor_copy(y_all[:, bass.ds(i * 2, 2), :], yout[:, (m - 5) % 2, :, :]).then_inc(S["y_kept"], 1)
                if has(t, 0):
                    add_bo(t, m % 2)

            pipeline(iteration)(pool)

        @block.sync
        def _(sp):
            sp.dma_start(u_nat[:, 0:3, :], Wqkv.rearrange("(k p) d -> p k d", p=P)).then_inc(S["in_w"], 16)
            sp.dma_start(u_nat[:, 3, :], Wo).then_inc(S["in_w"], 16)
            sp.dma_start(wg_nat[:, :], Wg).then_inc(S["in_w"], 16)
            for k in range(3):
                sp.dma_start(u_col[:, k:k + 1], bqkv[k * P:(k + 1) * P].rearrange("(p o) -> p o", o=1),
                             allow_slow_non_contiguous=True).then_inc(S["in_b"], 16)
            for k, row in enumerate((bo, g1, be1)):
                sp.dma_start(rows[:, k, :], row.partition_broadcast(P)).then_inc(S["in_b"], 16)
            for to, source in loads:
                sp.dma_start(to, source).then_inc(loaded, 16)
            sp.wait_ge(S["zeros_ok"], 1)
            y_rows = y_sorted.rearrange("(p n) d -> p (n d)", p=P)
            for k in range(3):
                sp.dma_start(y_rows[:, k * NZ:(k + 1) * NZ], zeros[:, :]).then_inc(S["zeroed"], 16)
            sp.wait_ge(S["zeroed"], 48)


NF = DF // P
NS = (B1 * L1 + NE * (P - 1)) // P
RING = 4
NG = NT // 4


def expert_weights(nc, ctx, w):
    W1, b1, W2, b2, g2, be2 = w
    t = {"w1": [P, NE * DF],
         "w2": [P, NE * DF],
         "b1r": [P, NE * DF], "b2r": [P, NE * P], "g2r": [P, P], "be2r": [P, P]}
    t = {name: ctx.enter_context(nc.sbuf_tensor("e_" + name, shape, F32)) for name, shape in t.items()}
    loads = [(t["w1"][:, :].rearrange("d (e f) -> d e f", e=NE), W1.rearrange("e d f -> d e f")),
             (t["w2"][:, :].rearrange("p (c d) -> p c d", d=P), W2.rearrange("e (f p) d -> p (e f) d", p=P)),
             (t["b1r"][:, :], b1.rearrange("e f -> (e f)").partition_broadcast(P)),
             (t["b2r"][:, :], b2.rearrange("e d -> (e d)").partition_broadcast(P)),
             (t["g2r"][:, :], g2.partition_broadcast(P)), (t["be2r"][:, :], be2.partition_broadcast(P))]
    return t, loads


def experts(nc, w, loaded, loads, ident, xs, y_all, logits, y_sorted, moe_sorted, out):
    with ExitStack() as ctx:
        def sb(name, shape, dt=F32):
            return ctx.enter_context(nc.sbuf_tensor(name, shape, dt))

        def pb(name):
            return [ctx.enter_context(nc.psum_tensor(f"{name}{k}", [P, 512], F32)) for k in range(2)]

        before = sb("before", [P, P])
        every = sb("every", [P, P])
        number = sb("number", [P, 40])
        full = sb("full", [P, NT])
        pref = sb("pref", [P, NE])
        best = sb("best", [P, NT])
        hit = sb("hit", [P, NT, NE])
        tmp = sb("tmp", [P, NT, NE])
        mine = sb("mine", [P, NT, NE])
        run = [sb(f"run{k}", [P, NT // 2 + NT, NE]) for k in range(2)]
        more = sb("more", [P, NE, NT])
        ends = [sb(f"ends{k}", [P, NE // 2 + NE]) for k in range(2)]
        base = sb("base", [P, NE])
        place = sb("place", [P, NT, NE])
        slot = sb("slot", [P, NT])
        slot_i = sb("slot_i", [P, NT], I32)
        past = sb("past", [P, NS, NE])
        owner = sb("owner", [P, NS])
        owner_i = sb("owner_i", [P, NS], I32)
        ys = sb("ys", [P, RING, P])
        yT = sb("yT", [P, 2, P])
        hs = sb("hs", [P, 2, DF])
        hT = sb("hT", [P, 2, DF])
        os = sb("os", [P, RING, P])
        moe = sb("moe", [P, NT, P])
        z0 = sb("z0", [P, 2, 4, P])
        z1 = sb("z1", [P, 2, 4, P])
        z2 = sb("z2", [P, 2, 4, P])
        z3 = sb("z3", [P, 2, 4, P])
        st_z = [sb(f"st_z{k}", [P, 4, 6]) for k in range(2)]
        mv_z = [sb(f"mv_z{k}", [P, 4, 2]) for k in range(2)]
        ve_z = [sb(f"ve_z{k}", [P, 4]) for k in range(2)]
        nm_z = [sb(f"nm_z{k}", [P, 4]) for k in range(2)]
        rs_z = [sb(f"rs_z{k}", [P, 4]) for k in range(2)]
        nb_z = [sb(f"nb_z{k}", [P, 4]) for k in range(2)]
        half4 = sb("half4", [P, 4])
        psT, psH, psX, psO = pb("psT"), pb("psH"), pb("psX"), pb("psO")

        names = ["passed", "consts", "sums_full", "route", "slots_ok", "owner_ok", "sorted", "ys0", "ys1", "ys2",
                 "ys3", "t_full", "yT_ok", "h_full", "hs_ok", "x_full", "hT_ok", "o_full", "os_ok", "st0", "st1",
                 "st2", "st3", "got0", "got1", "z0_ok", "z_agg0", "z_agg1", "z_st0", "z_st1", "z_step0", "z_step1",
                 "z_rs0", "z_rs1", "z1_ok", "z2_step", "z2_ok", "z3_ok", "done", "out_ok"]
        S = {n: ctx.enter_context(nc.semaphore("ex_" + n)) for n in names}

        def guarded(lo, t, hi):
            return not isinstance(t, int) or lo <= t < hi

        block = ctx.enter_context(nc.Block())

        def sorted_tiles(eng, iteration):
            for t in range(RING):
                iteration(t, t)
            loops = (NS - 1) // RING - 1
            with eng.Fori(0, loops) as k:
                for r in range(RING):
                    iteration(k * RING + (RING + r), r)
            for t in range(RING * (loops + 1), NS + 2):
                iteration(t, t % RING)

        def groups(eng, iteration):
            iteration(0, 0)
            iteration(1, 1)
            with eng.Fori(0, (NG - 2) // 2) as k:
                iteration(k * 2 + 2, 0)
                iteration(k * 2 + 3, 1)
            iteration(NG, 0)
            iteration(NG + 1, 1)

        @block.tensor
        def _(pe):
            T = nc.tensor
            pe.wait_ge(S["consts"], 2)
            pe.wait_ge(S["route"], 5)
            flat = mine[:, :, :].rearrange("p j e -> p (j e)")
            T.matmul(psT[0][:, 0:NT * NE], before[:, :], flat, start=True, stop=True)
            T.matmul(psT[0][:, NT * NE:2 * NT * NE], every[:, :], flat, start=True,
                     stop=True).then_inc(S["sums_full"], 1)
            pe.wait_ge(loaded, 16 * len(loads))
            pe.wait_ge(S["owner_ok"], 1)

            def turn(t, m):
                pe.wait_ge(S[f"ys{m % 4}"], (t - m % 4) * 4 + 16)
                pe.wait_ge(S["yT_ok"], count(t - 1))
                T.transpose(psT[m % 2][:, 0:P], ys[:, m % 4, :], ident[:, :]).then_inc(S["t_full"], 1)

            def iteration(t, m):
                if guarded(0, t, NS):
                    e = pe.value_load(owner_i[0:1, bass.ds(t, 1)], min_val=0, max_val=NE - 1)
                    pe.wait_ge(S["yT_ok"], t + 1)
                    pe.wait_ge(S["hs_ok"], count(t - 1))
                    T.matmul(psH[m % 2][:, :], yT[:, m % 2, :], w["w1"][:, bass.ds(e * DF, DF)], start=True,
                             stop=True).then_inc(S["h_full"], 1)
                if guarded(0, t - 1, NS):
                    pe.wait_ge(S["hs_ok"], t)
                    pe.wait_ge(S["hT_ok"], count(t - 2))
                    for f in range(NF):
                        last = T.transpose(psX[(m - 1) % 2][:, f * P:(f + 1) * P],
                                           hs[:, (m - 1) % 2, f * P:(f + 1) * P], ident[:, :])
                    last.then_inc(S["x_full"], 1)
                if guarded(0, t - 2, NS):
                    e = pe.value_load(owner_i[0:1, bass.ds(t - 2, 1)], min_val=0, max_val=NE - 1)
                    pe.wait_ge(S["hT_ok"], t - 1)
                    pe.wait_ge(S["os_ok"], count(t - 3))
                    for f in range(NF):
                        last = T.matmul(psO[m % 2][:, 0:P], hT[:, m % 2, f * P:(f + 1) * P],
                                        w["w2"][:, bass.ds(e * DF + f * P, P)], start=(f == 0), stop=(f == NF - 1))
                    last.then_inc(S["o_full"], 1)
                if guarded(0, t + 1, NS):
                    turn(t + 1, (m + 1) % 4)

            turn(0, 0)
            sorted_tiles(pe, iteration)

        @block.vector
        def _(dve):
            V = nc.vector
            steps = [0]

            def step(instruction):
                steps[0] += 1
                instruction.then_inc(S["route"], 1)
                dve.wait_ge(S["route"], steps[0])

            def over(row):
                return row.unsqueeze(1).broadcast_to([P, NT, NE])

            step(V.tensor_reduce(best[:, :], logits[:, :, :], AX.X, ALU.max))
            step(V.tensor_tensor(hit[:, :, :], logits[:, :, :], best[:, :].unsqueeze(2).broadcast_to([P, NT, NE]),
                                 ALU.is_ge))
            dve.wait_ge(S["consts"], 2)
            step(V.tensor_tensor(tmp[:, :, :], hit[:, :, :], over(pref[:, :]), ALU.mult))
            step(V.tensor_reduce(best[:, :], tmp[:, :, :], AX.X, ALU.max))
            step(V.tensor_tensor(mine[:, :, :], tmp[:, :, :], best[:, :].unsqueeze(2).broadcast_to([P, NT, NE]),
                                 ALU.is_equal))
            Z = NT // 2
            V.memset(run[0][:, 0:Z, :], 0.0)
            V.memset(run[1][:, 0:Z, :], 0.0)
            V.memset(ends[0][:, 0:NE // 2], 0.0)
            V.memset(ends[1][:, 0:NE // 2], 0.0)
            dve.wait_ge(S["sums_full"], 1)
            step(V.tensor_copy(run[0][:, Z:, :].rearrange("p j e -> p (j e)"), psT[0][:, NT * NE:2 * NT * NE]))
            for k in range(5):
                a, b = run[k % 2], run[1 - k % 2]
                step(V.tensor_tensor(b[:, Z:, :], a[:, Z:, :], a[:, Z - 2 ** k:Z + NT - 2 ** k, :], ALU.add))
            total = run[1]
            step(V.tensor_tensor(more[:, :, :], total[:, Z + NT - 1, :].unsqueeze(2).broadcast_to([P, NE, NT]),
                                 full[:, :].unsqueeze(1).broadcast_to([P, NE, NT]), ALU.is_gt))
            Y = NE // 2
            step(V.tensor_reduce(ends[0][:, Y:], more[:, :, :], AX.X, ALU.add))
            for k in range(3):
                a, b = ends[k % 2], ends[1 - k % 2]
                step(V.tensor_tensor(b[:, Y:], a[:, Y:], a[:, Y - 2 ** k:Y + NE - 2 ** k], ALU.add))
            end = ends[1]
            step(V.tensor_scalar(base[:, :], end[:, Y - 1:Y - 1 + NE], float(P), None, ALU.mult))
            step(V.tensor_tensor(place[:, :, :], psT[0][:, 0:NT * NE].rearrange("p (j e) -> p j e", e=NE),
                                 total[:, Z - 1:Z - 1 + NT, :], ALU.add))
            step(V.tensor_tensor(place[:, :, :], place[:, :, :], over(base[:, :]), ALU.add))
            step(V.tensor_tensor(place[:, :, :], place[:, :, :], mine[:, :, :], ALU.mult))
            step(V.tensor_reduce(slot[:, :], place[:, :, :], AX.X, ALU.add))
            V.tensor_copy(slot_i[:, :], slot[:, :]).then_inc(S["slots_ok"], 1)
            step(V.tensor_tensor(past[:, :, :], end[:, Y:].unsqueeze(1).broadcast_to([P, NS, NE]),
                                 number[:, 0:NS].unsqueeze(2).broadcast_to([P, NS, NE]), ALU.is_le))
            step(V.tensor_reduce(owner[:, :], past[:, :, :], AX.X, ALU.add))
            V.tensor_scalar(owner_i[:, :], owner[:, :], float(NE - 1), None, ALU.min).then_inc(S["owner_ok"], 1)
            dve.wait_ge(S["owner_ok"], 1)
            dve.wait_ge(loaded, 16 * len(loads))

            def iteration(t, m):
                if guarded(0, t, NS):
                    e = dve.value_load(owner_i[0:1, bass.ds(t, 1)], min_val=0, max_val=NE - 1)
                    dve.wait_ge(S["h_full"], t + 1)
                    dve.wait_ge(S["x_full"], count(t - 1))
                    V.tensor_tensor(hs[:, m % 2, :], psH[m % 2][:, :], w["b1r"][:, bass.ds(e * DF, DF)],
                                    ALU.add).then_inc(S["hs_ok"], 1)
                if guarded(0, t - 2, NS):
                    e = dve.value_load(owner_i[0:1, bass.ds(t - 2, 1)], min_val=0, max_val=NE - 1)
                    dve.wait_ge(S["o_full"], t - 1)
                    dve.wait_ge(S[f"st{(m - 2) % 4}"], count((t - 2 - (m - 2) % 4) * 4))
                    V.tensor_tensor(os[:, (m - 2) % 4, :], psO[m % 2][:, 0:P], w["b2r"][:, bass.ds(e * P, P)],
                                    ALU.add).then_inc(S["os_ok"], 1)

            sorted_tiles(dve, iteration)

            def statistics(k, g, src):
                for c in range(4):
                    V.bn_stats(st_z[k][:, c, :], src[:, c, :]).then_inc(S[f"z_st{k}"], 1)
                for c in range(4):
                    dve.wait_ge(S[f"z_st{k}"], 4 * g + c + 1)
                    dve.sem_inc(S["passed"])
                    last = V.bn_aggr(mv_z[k][:, c, :], st_z[k][:, c, :])
                last.then_inc(S[f"z_agg{k}"], 1)

            def last_step(t, n):
                if guarded(0, t, NG):
                    dve.wait_ge(S[f"got{n}"], (t - n) * 32 + 64)
                    dve.wait_ge(S["z1_ok"], count(t - 1))
                    V.tensor_tensor(z0[:, n, :, :], y_all[:, bass.ds(t * 4, 4), :], moe[:, bass.ds(t * 4, 4), :],
                                    ALU.add).then_inc(S["z0_ok"], 1)
                    dve.wait_ge(S["z0_ok"], t + 1)
                    dve.wait_ge(S["z_rs0"], count(t))
                    statistics(0, t, z0[:, n, :, :])
                if guarded(0, t - 1, NG):
                    i, o = t - 1, 1 - n
                    dve.wait_ge(S["z1_ok"], i + 1)
                    dve.wait_ge(S["z3_ok"], count(i - 1))
                    V.tensor_tensor(z2[:, o, :, :], z1[:, o, :, :],
                                    w["g2r"][:, :].unsqueeze(1).broadcast_to([P, 4, P]),
                                    ALU.mult).then_inc(S["z2_step"], 1)
                    dve.wait_ge(S["z2_step"], i + 1)
                    V.tensor_tensor(z2[:, o, :, :], z2[:, o, :, :],
                                    w["be2r"][:, :].unsqueeze(1).broadcast_to([P, 4, P]),
                                    ALU.add).then_inc(S["z2_ok"], 1)
                    dve.wait_ge(S["z2_ok"], i + 1)
                    dve.wait_ge(S["z_rs1"], count(i))
                    statistics(1, i, z2[:, o, :, :])
                if guarded(0, t - 2, NG):
                    i = t - 2
                    dve.wait_ge(S["z3_ok"], i + 1)
                    V.tensor_tensor(xs[:, bass.ds(i * 4, 4), :], xs[:, bass.ds(i * 4, 4), :], z3[:, n, :, :],
                                    ALU.add).then_inc(S["done"], 1)

            groups(dve, last_step)

        @block.scalar
        def _(act):
            A = nc.scalar

            def turned(t, m):
                act.wait_ge(S["t_full"], t + 1)
                act.wait_ge(S["h_full"], count(t - 1))
                A.activation(yT[:, m % 2, :], psT[m % 2][:, 0:P], ACT.Copy).then_inc(S["yT_ok"], 1)

            def store(t, m):
                act.wait_ge(S["os_ok"], t + 1)
                act.dma_start(moe_sorted[bass.ds(t * P, P), :], os[:, m % 4, :]).then_inc(S[f"st{m % 4}"], 16)

            def iteration(t, m):
                if guarded(0, t - 1, NS):
                    act.wait_ge(S["x_full"], t)
                    act.wait_ge(S["o_full"], count(t - 2))
                    A.activation(hT[:, (m - 1) % 2, :], psX[(m - 1) % 2][:, :], ACT.Relu).then_inc(S["hT_ok"], 1)
                if guarded(0, t + 1, NS):
                    turned(t + 1, (m + 1) % 4)
                if guarded(0, t - 2, NS):
                    store(t - 2, (m - 2) % 4)

            act.wait_ge(S["owner_ok"], 1)
            turned(0, 0)
            sorted_tiles(act, iteration)

            def apply(k, dst, src):
                for c in range(4):
                    last = A.activation(dst[:, c, :], src[:, c, :], ACT.Identity, bias=nb_z[k][:, c:c + 1],
                                        scale=rs_z[k][:, c:c + 1])
                return last

            def last_step(t, n):
                if guarded(0, t, NG):
                    act.wait_ge(S["z_rs0"], t + 1)
                    act.wait_ge(S["z2_step"], count(t - 1))
                    apply(0, z1[:, n, :, :], z0[:, n, :, :]).then_inc(S["z1_ok"], 1)
                if guarded(0, t - 1, NG):
                    act.wait_ge(S["z_rs1"], t)
                    act.wait_ge(S["done"], count(t - 2))
                    apply(1, z3[:, 1 - n, :, :], z2[:, 1 - n, :, :]).then_inc(S["z3_ok"], 1)

            groups(act, last_step)

        @block.gpsimd
        def _(pool):
            G = nc.gpsimd
            G.memset(half4[:, :], -0.5)
            for k in range(40):
                G.memset(number[:, k:k + 1], float(k))
            for k in range(NT):
                G.memset(full[:, k:k + 1], float(P * k))
            for e in range(NE):
                G.memset(pref[:, e:e + 1], float(NE - e))
            G.memset(every[:, :], 1.0).then_inc(S["consts"], 1)
            pool.wait_ge(S["consts"], 1)
            G.affine_select(out=before[:, :], in_=every[:, :], compare_op=ALU.is_gt, fill=0.0, base=0,
                            pattern=[[1, P]], channel_multiplier=-1).then_inc(S["consts"], 1)
            pool.wait_ge(S["slots_ok"], 1)
            for j in range(NT):
                G.indirect_dma_start(y_sorted, bass.IndirectOffsetOnAxis(slot_i[:, j:j + 1], 0), y_all[:, j, :],
                                     None).then_inc(S["sorted"], 16)
            for m in range(RING):
                pool.wait_ge(S[f"st{m}"], 16 * len(range(m, NS, RING)))

            def gather(g, n):
                if isinstance(g, int) and g >= 2:
                    pool.wait_ge(S["z0_ok"], g - 1)
                for c in range(4):
                    G.indirect_dma_start(moe[:, 4 * g + c, :], None, moe_sorted,
                                         bass.IndirectOffsetOnAxis(slot_i[:, 4 * g + c:4 * g + c + 1], 0)
                                         ).then_inc(S[f"got{n}"], 16)

            def scale(k, g):
                pool.wait_ge(S[f"z_agg{k}"], g + 1)
                if g >= 1:
                    pool.wait_ge(S[f"z{2 * k + 1}_ok"], g)
                G.tensor_scalar(ve_z[k][:, :], mv_z[k][:, :, 1], EPS, None, ALU.add).then_inc(S[f"z_step{k}"], 1)
                G.tensor_scalar(nm_z[k][:, :], mv_z[k][:, :, 0], -1.0, None, ALU.mult).then_inc(S[f"z_step{k}"], 1)
                pool.wait_ge(S[f"z_step{k}"], 3 * g + 2)
                G.tensor_tensor(rs_z[k][:, :], ve_z[k][:, :], half4[:, :], ALU.pow).then_inc(S[f"z_step{k}"], 1)
                pool.wait_ge(S[f"z_step{k}"], 3 * g + 3)
                G.tensor_tensor(nb_z[k][:, :], nm_z[k][:, :], rs_z[k][:, :], ALU.mult).then_inc(S[f"z_rs{k}"], 1)

            gather(0, 0)
            gather(1, 1)
            for t in range(NG + 1):
                if t < NG:
                    scale(0, t)
                if t + 2 < NG:
                    gather(t + 2, t % 2)
                if t >= 1:
                    scale(1, t - 1)

        @block.sync
        def _(sp):
            def load(t, m):
                sp.wait_ge(S["t_full"], count(t - (RING - 1)))
                sp.dma_start(ys[:, m % 4, :], y_sorted[bass.ds(t * P, P), :]).then_inc(S[f"ys{m % 4}"], 16)

            sp.wait_ge(S["sorted"], 16 * NT)
            for t in range(RING):
                load(t, t)
            with sp.Fori(0, NS // RING - 1) as k:
                for r in range(RING):
                    load(k * RING + (RING + r), r)
            for t in range(NS // RING * RING, NS):
                load(t, t % RING)
            out_t = out.rearrange("(q r) l d -> q (r l d)", q=B1).rearrange("q (b n) -> (q b) n", b=8)
            for g in range(NG):
                sp.wait_ge(S["done"], g + 1)
                sp.dma_start(out_t[:, 4 * g * P:4 * (g + 1) * P],
                             xs[:, 4 * g:4 * g + 4, :].rearrange("p c d -> p (c d)")).then_inc(S["out_ok"], 16)
            sp.wait_ge(S["out_ok"], 16 * NG)


def build_program(nc, a, out):
    with ExitStack() as ctx:
        ident = ctx.enter_context(nc.sbuf_tensor("ident", [P, P], F32))
        identh = ctx.enter_context(nc.sbuf_tensor("identh", [P, P], BF16))
        minus_half = ctx.enter_context(nc.sbuf_tensor("minus_half", [P, 2], F32))
        xs = ctx.enter_context(nc.sbuf_tensor("xs", [P, NT, P], F32))
        y_sorted = nc.dram_tensor("y_sorted", (NS * P, P), F32).ap()
        moe_sorted = nc.dram_tensor("moe_sorted", (NS * P, P), F32).ap()
        first_layer(nc, a["x"], a["w_qkv"], a["b_qkv"], a["w_o"], a["b_o"], ident, identh, minus_half, xs)
        y_all = ctx.enter_context(nc.sbuf_tensor("y_all", [P, NT, P], F32))
        logits = ctx.enter_context(nc.sbuf_tensor("logits", [P, NT, NE], F32))
        loaded = ctx.enter_context(nc.semaphore("loaded"))
        w, loads = expert_weights(nc, ctx, [a[k] for k in ("W1", "b1", "W2", "b2", "g2", "be2")])
        second_attention(nc, [a[k] for k in ("Wqkv", "bqkv", "Wo", "bo", "g1", "be1", "Wg")], ident, identh,
                         minus_half, xs, y_all, logits, loaded, loads, y_sorted)
        experts(nc, w, loaded, loads, ident, xs, y_all, logits, y_sorted, moe_sorted, out)


def kernel(L0_attn_x, L0_attn_w_qkv, L0_attn_b_qkv, L0_attn_w_o, L0_attn_b_o, L0_ffn_Wqkv, L0_ffn_bqkv, L0_ffn_Wo,
           L0_ffn_bo, L0_ffn_g1, L0_ffn_be1, L0_ffn_g2, L0_ffn_be2, L0_ffn_Wg, L0_ffn_W1, L0_ffn_b1, L0_ffn_W2,
           L0_ffn_b2):
    import numpy as np
    import concourse.bacc as bacc
    from concourse.bass_utils import run_bass_kernel_spmd

    given = {"x": L0_attn_x, "w_qkv": L0_attn_w_qkv, "b_qkv": L0_attn_b_qkv, "w_o": L0_attn_w_o, "b_o": L0_attn_b_o,
             "Wqkv": L0_ffn_Wqkv, "bqkv": L0_ffn_bqkv, "Wo": L0_ffn_Wo, "bo": L0_ffn_bo, "g1": L0_ffn_g1,
             "be1": L0_ffn_be1, "g2": L0_ffn_g2, "be2": L0_ffn_be2, "Wg": L0_ffn_Wg, "W1": L0_ffn_W1,
             "b1": L0_ffn_b1, "W2": L0_ffn_W2, "b2": L0_ffn_b2}
    nc = bacc.Bacc("TRN2", target_bir_lowering=False, num_devices=1)
    arrays, args = {}, {}
    for name, array in given.items():
        arrays[name] = np.ascontiguousarray(array)
        args[name] = nc.dram_tensor(name, arrays[name].shape, mybir.dt.from_np(arrays[name].dtype),
                                    kind="ExternalInput").ap()
    out = nc.dram_tensor("out", (B1, L1, P), F32, kind="ExternalOutput").ap()
    build_program(nc, args, out)
    r = run_bass_kernel_spmd(nc, [arrays], core_ids=[0])
    return r.results[0]["out"]
```

```python
from contextlib import ExitStack

import concourse.bass as bass
from concourse import mybir

F32 = mybir.dt.float32
BF16 = mybir.dt.bfloat16
I32 = mybir.dt.int32
ALU = mybir.AluOpType
ACT = mybir.ActivationFunctionType
AX = mybir.AxisListType

P = 128
B1, L1 = 16, 256
H1, C1 = 16, 8
SCALE1 = 1.0 / float(P) ** 0.5
EPS = 1e-5
NT = B1 * L1 // P
Q_PART = (0, 0, 1, 1, 0, 2)
K_PART = (0, 1, 0, 1, 2, 0)
NPROD = len(Q_PART)
MAX_ROW = 96
HALF = 8
AHEAD = 4
LAST = B1 - 1
PRING = 8


def count(value):
    return max(value, 0) if isinstance(value, int) else value


def first_layer(nc, x, w_qkv, b_qkv, w_o, b_o, ident, identh, minus_half, xs, loads2, loaded2):
    with ExitStack() as ctx:
        def sb(name, shape, dt=F32):
            return ctx.enter_context(nc.sbuf_tensor(name, shape, dt))

        def pb(name, shape, dt=F32):
            return ctx.enter_context(nc.psum_tensor(name, shape, dt))

        def sem(name):
            return ctx.enter_context(nc.semaphore(name))

        w_nat = sb("w_nat", [P, 4, P])
        wT = sb("wT", [P, 4, P])
        b_col = sb("b_col", [P, 2])
        bv_col = sb("bv_col", [P, 1])
        one_pair = sb("one_pair", [P, 1])
        zero = sb("zero", [P, 1])
        bo_row = sb("bo_row", [P, P])
        x_all = sb("x_all", [P, NT, P])
        xnb_all = sb("xnb_all", [P, NT, P])
        xin = sb("xin", [P, 2, 2, P])
        xn = sb("xn", [P, 2, P])
        st = [sb(f"st{k}", [P, 2, 6]) for k in range(2)]
        mv = [sb(f"mv{k}", [P, 2, 2]) for k in range(2)]
        nm = [sb(f"nm{k}", [P, 2]) for k in range(2)]
        ve = [sb(f"ve{k}", [P, 2]) for k in range(2)]
        rs = [sb(f"rs{k}", [P, 2]) for k in range(2)]
        xnT = sb("xnT", [P, L1])
        parts = sb("parts", [P, 2, 3, 2, 2, L1], BF16)
        rest = sb("rest", [P, 2, L1])
        qs = sb("qs", [P, H1, 4, L1], BF16)
        ks = sb("ks", [P, H1, 4, L1], BF16)
        v32 = sb("v32", [P, 4, 2, H1, 32])
        nmax = sb("nmax", [P, 2, H1])
        nmr = sb("nmr", [P, 2, HALF])
        mparts = sb("mparts", [P, 2, 3, HALF], BF16)
        mT = sb("mT", [24, L1], BF16)
        pr = sb("pr", [P, PRING, 2, L1])
        osb = sb("osb", [P, 2, 512])
        rden = sb("rden", [P, 2, 8])
        on = sb("on", [P, 2, P])
        onT = sb("onT", [P, L1])
        r1 = sb("r1", [P, 2, P])
        nr = sb("nr", [P, 2, P])

        psA = pb("psA", [P, 2, 512])
        psB = pb("psB", [P, 3, 512])
        psO = pb("psO", [P, 512])
        misc = [pb(f"misc{k}", [P, 512]) for k in range(2)]
        misch = [bank[:, :].bitcast(BF16) for bank in misc]

        names = ["passed", "ld_w", "ld_b", "ld_x", "consts", "consts_p", "zeroed", "zeroed2", "x_in0",
                 "x_in1", "stats0", "stats1", "aggr0", "aggr1", "ln0_step", "ln1_step", "xn_ok", "xnb_ok", "full0",
                 "full1", "free0", "free1", "p1_ok", "p2_ok", "p3_ok", "stack0", "stack1", "a_full", "a_free",
                 "split_step", "mp_ok", "mrow0", "mrow1", "b_full", "b_free", "av_done", "o_ev", "rden_ok", "r_ok",
                 "x1_ok", "stored", "v_ok"]
        S = {n: sem(n) for n in names}

        x_t = x.rearrange("b (p c) d -> b p c d", p=P)

        BEFORE, EACH = 13, 8

        def has(k, i):
            done, here, ahead = 1 <= i <= LAST + 1, i <= LAST, i + AHEAD <= LAST
            return (done, here, i + 3 <= LAST or 2 <= i <= LAST + 2, ahead, done, i + 1 <= LAST, ahead, done)[k]

        def turn(n):
            return n % 2, n // 2

        def use_no(k, i):
            if isinstance(i, int):
                return turn(BEFORE + sum(has(kk, ii) for ii in range(i) for kk in range(EACH)) + sum(
                    has(kk, i) for kk in range(k)))
            bank, before = use_no(k, 2)
            return bank, i * (EACH // 2) + (before - EACH)

        def xT_use(b):
            return turn(1 + 3 * b) if isinstance(b, int) and b < AHEAD else use_no(3, b - AHEAD)

        def v_use(b):
            return turn(2 + 3 * b) if isinstance(b, int) and b < 3 else use_no(2, b - 3)

        def qk_use(b):
            if isinstance(b, int) and b < AHEAD:
                return turn(3 + 3 * b if b < 3 else 11)
            return use_no(6, b - AHEAD)

        def max_use(b, hf):
            if hf == 0 and isinstance(b, int) and b == 0:
                return turn(12)
            return use_no(1, b) if hf else use_no(5, b - 1)

        def out_use(b, hf):
            return use_no(4 * hf, b + 1)

        def fits(i, d):
            return not isinstance(i, int) or 0 <= i + d <= LAST

        def stack_count(b, m):
            return (b - m) * (4 * NPROD * 2) + 16 * 2 * NPROD

        def pipeline(eng, iteration):
            iteration(0, 0)
            iteration(1, 1)
            with eng.Fori(0, 2) as four:
                for r in range(2, 6):
                    iteration(four * 4 + r, r % 4)
            for i in range(10, LAST + 3):
                iteration(i, i % 4)

        block = ctx.enter_context(nc.Block())

        @block.tensor
        def _(pe):
            T = nc.tensor
            pe.wait_ge(S["ld_w"], 32)
            pe.wait_ge(S["consts_p"], 1)
            for k in range(4):
                last = T.transpose(misc[0][:, k * P:(k + 1) * P], w_nat[:, k, :], ident[:, :])
            last.then_inc(S["full0"], 1)

            def prep_x(b):
                bank, before = xT_use(b)
                pe.wait_ge(S[f"free{bank}"], count(before))
                pe.wait_ge(S["xn_ok"], count(b + 1))
                for c in range(2):
                    last = T.transpose(misc[bank][:, c * P:(c + 1) * P], xn[:, c, :], ident[:, :])
                last.then_inc(S[f"full{bank}"], 1)

            def prep_qk(b):
                made, n = xT_use(b)
                pe.wait_ge(S[f"free{made}"], count(n + 1))
                bank, before = qk_use(b)
                pe.wait_ge(S[f"free{bank}"], count(before))
                for k in range(2):
                    last = T.matmul(misc[bank][:, k * L1:(k + 1) * L1], wT[:, k, :], xnT[:, :], start=True, stop=True)
                last.then_inc(S[f"full{bank}"], 1)

            def token_major(lhs, k, bank, at):
                for c in range(2):
                    last = T.matmul(misc[bank][:, at + c * P:at + (c + 1) * P], lhs[:, c * P:(c + 1) * P], wT[:, k, :],
                                    start=True, stop=True)
                return last

            def scores_for_max(b, m, g):
                if g == 0:
                    if isinstance(b, int) and b == 2:
                        pe.wait_ge(S["zeroed2"], 2)
                    pe.wait_ge(S[f"stack{m // 2}"], count(stack_count(b, m)))
                for c in range(2):
                    pe.wait_ge(S["a_free"], count(16 * b + 2 * g + c - 1))
                    for j in range(2):
                        h = 2 * g + j
                        last = T.matmul(psA[:, c, j * L1:(j + 1) * L1], qs[0:MAX_ROW, h, m, c * P:(c + 1) * P],
                                        ks[0:MAX_ROW, h, m, :], start=True, stop=True)
                    last.then_inc(S["a_full"], 1)

            def scores(b, m, h):
                if h % HALF == 0:
                    pe.wait_ge(S[f"mrow{h // HALF}"], count(16 * (b + 1)))
                pe.wait_ge(S["b_free"], count(16 * b + (0, -2, -1)[h] if h < 3 else 16 * b + h - 2))
                for c in range(2):
                    last = T.matmul(psB[:, h % 3, c * L1:(c + 1) * L1], ks[:, h, m, c * P:(c + 1) * P],
                                    qs[:, h, m, :], start=True, stop=True)
                last.then_inc(S["b_full"], 1)

            def attend(b, m, q):
                pe.wait_ge(S["b_free"], count(16 * b + 4 * q + 4))
                if q % 2 == 0:
                    pe.wait_ge(S["o_ev"], count(2 * b + q // 2))
                for c in range(2):
                    for j in range(4):
                        last = T.matmul(psO[32 * j:32 * j + 32, (q % 2) * L1:(q % 2 + 1) * L1],
                                        v32[:, m, c, 4 * q + j, :], pr[:, (4 * q + j) % PRING, c, :],
                                        start=(c == 0), stop=(c == 1))
                last.then_inc(S["av_done"], 1)

            def max_rows(b, hf):
                bank, before = max_use(b, hf)
                pe.wait_ge(S[f"free{bank}"], count(before))
                pe.wait_ge(S["mp_ok"], count(2 * b + hf + 1))
                for c in range(2):
                    last = T.transpose(misch[bank][0:24, c * P:(c + 1) * P],
                                       mparts[:, c, :, :].rearrange("p a h -> p (a h)"), identh[:, :])
                last.then_inc(S[f"full{bank}"], 1)

            def heads_to_tokens(b, hf):
                bank, before = out_use(b, hf)
                pe.wait_ge(S[f"free{bank}"], count(before))
                pe.wait_ge(S["o_ev"], count(2 * b + hf + 1))
                for c in range(2):
                    for q in range(2):
                        last = T.transpose(misc[bank][:, (2 * c + q) * P:(2 * c + q + 1) * P],
                                           osb[:, hf, q * L1 + c * P:q * L1 + (c + 1) * P], ident[:, :])
                last.then_inc(S[f"full{bank}"], 1)

            def heads_T(i):
                for hf in range(2):
                    made, n = out_use(i - 1, hf)
                    pe.wait_ge(S[f"free{made}"], count(n + 1))
                bank, before = use_no(7, i)
                pe.wait_ge(S[f"free{bank}"], count(before))
                for c in range(2):
                    last = T.transpose(misc[bank][:, c * P:(c + 1) * P], on[:, c, :], ident[:, :])
                last.then_inc(S[f"full{bank}"], 1)

            def iteration(i, m):
                here, next_, done, ahead = fits(i, 0), fits(i, 1), fits(i, -1), fits(i, AHEAD)
                for g in range(8):
                    if here:
                        scores(i, m, 2 * g)
                        scores(i, m, 2 * g + 1)
                    if next_:
                        scores_for_max(i + 1, (m + 1) % 4, g)
                    if here and g in (3, 5, 7):
                        attend(i, m, g // 2 - 1)
                    if g == 1 and done:
                        attend(i - 1, (m - 1) % 4, 3)
                    if g == 0 and done:
                        heads_to_tokens(i - 1, 0)
                    if g == 1 and here:
                        max_rows(i, 1)
                    if g == 2 and (fits(i, 3) or fits(i, -2)):
                        bank, before = use_no(2, i)
                        pe.wait_ge(S[f"free{bank}"], count(before))
                        if fits(i, 3):
                            last = token_major(xnT, 2, bank, 0)
                        if fits(i, -2):
                            made, n = use_no(7, i - 1)
                            pe.wait_ge(S[f"free{made}"], count(n + 1))
                            last = token_major(onT, 3, bank, 2 * P)
                        last.then_inc(S[f"full{bank}"], 1)
                    if g == 3 and ahead:
                        prep_x(i + AHEAD)
                    if g == 4 and done:
                        heads_to_tokens(i - 1, 1)
                    if g == 5 and next_:
                        max_rows(i + 1, 0)
                    if g == 6 and ahead:
                        prep_qk(i + AHEAD)
                    if g == 7 and done:
                        heads_T(i)

            for b in range(AHEAD):
                prep_x(b)
                if b < 3:
                    made, n = xT_use(b)
                    pe.wait_ge(S[f"free{made}"], count(n + 1))
                    bank, before = v_use(b)
                    pe.wait_ge(S[f"free{bank}"], count(before))
                    token_major(xnT, 2, bank, 0).then_inc(S[f"full{bank}"], 1)
                prep_qk(b)
            pe.wait_ge(S["zeroed"], 3)
            for g in range(8):
                scores_for_max(0, 0, g)
                if g == 4:
                    max_rows(0, 0)
            pipeline(pe, iteration)

        @block.vector
        def _(dve):
            V = nc.vector
            V.memset(ks[0:MAX_ROW, :, 0:2, :].rearrange("p h b l -> p h (b l)").bitcast(F32),
                     0.0).then_inc(S["zeroed"], 1)
            dve.wait_ge(S["full0"], 1)
            V.tensor_copy(wT[:, 0:2, :].rearrange("p k (c h) -> p k h c", c=C1),
                          misc[0][:, 0:2 * P].rearrange("p (k h c) -> p k h c", k=2, c=C1))
            V.tensor_copy(wT[:, 2:4, :].rearrange("p a d -> p (a d)"), misc[0][:, 2 * P:4 * P]).then_inc(S["free0"], 1)

            def ln_stats(kind, b, src):
                for c in range(2):
                    V.bn_stats(st[kind][:, c, :], src[:, c, :]).then_inc(S[f"stats{kind}"], 1)
                for c in range(2):
                    dve.wait_ge(S[f"stats{kind}"], count(2 * b + c + 1))
                    dve.sem_inc(S["passed"])
                    last = V.bn_aggr(mv[kind][:, c, :], st[kind][:, c, :])
                last.then_inc(S[f"aggr{kind}"], 1)

            def stats_x(b, m):
                dve.wait_ge(S[f"x_in{m % 2}"], count((b - m % 2) * 8 + 16))
                dve.wait_ge(S["xn_ok"], count(b))
                ln_stats(0, b, xin[:, m % 2, :, :])

            def split_qk(b, m):
                bank, before = qk_use(b)
                dve.wait_ge(S[f"full{bank}"], count(before + 1))
                dve.wait_ge(S["p1_ok"], count(2 * b + 2))
                dve.wait_ge(S["p3_ok"], count(b))
                for k in range(2):
                    last = V.scalar_tensor_tensor(out=rest[:, k, :], in0=misc[bank][:, k * L1:(k + 1) * L1],
                                                  scalar=b_col[:, k:k + 1], in1=parts[:, m // 2, 0, k, m % 2, :],
                                                  op0=ALU.add, op1=ALU.subtract)
                last.then_inc(S[f"free{bank}"], 1)
                dve.wait_ge(S[f"free{bank}"], count(before + 1))
                V.tensor_copy(parts[:, m // 2, 1, :, m % 2, :], rest[:, :, :]).then_inc(S["p2_ok"], 1)

            def residual(i):
                bank, before = use_no(2, i)
                dve.wait_ge(S[f"full{bank}"], count(before + 1))
                if fits(i, 3):
                    dve.wait_ge(S["v_ok"], count(i - 1))
                dve.wait_ge(S["xnb_ok"], count(i - 1))
                dve.wait_ge(S["x1_ok"], count(i - 2))
                V.tensor_tensor(out=r1[:, :, :], in0=misc[bank][:, 2 * P:4 * P].rearrange("p (c d) -> p c d", c=2),
                                in1=xnb_all[:, bass.ds((i - 2) * 2, 2), :], op=ALU.add).then_inc(S[f"free{bank}"], 1)
                dve.wait_ge(S[f"free{bank}"], count(before + 1))
                ln_stats(1, i - 2, r1)

            def maxima(b, g):
                for c in range(2):
                    dve.wait_ge(S["a_full"], count(16 * b + 2 * g + c + 1))
                    if g % 4 == 0 and c == 0:
                        dve.wait_ge(S["mp_ok"], count(2 * b + g // 4 - 1))
                    V.tensor_reduce(nmax[:, c, 2 * g:2 * g + 2], psA[:, c, :].rearrange("p (h m) -> p h m", h=2),
                                    AX.X, ALU.max, negate=True).then_inc(S["a_free"], 1)

            def normalise(b, hf):
                if hf == 0 and (not isinstance(b, int) or b >= 1):
                    made, n = use_no(7, b)
                    dve.wait_ge(S[f"full{made}"], count(n + 1))
                bank, before = out_use(b, hf)
                dve.wait_ge(S[f"full{bank}"], count(before + 1))
                o = misc[bank][:, :].rearrange("p (c k r) -> p c k r", c=2, r=32)
                V.reciprocal(rden[:, :, :], o[:, :, :, C1]).then_inc(S["rden_ok"], 1)
                dve.wait_ge(S["rden_ok"], count(2 * b + hf + 1))
                V.tensor_tensor(out=on[:, :, hf * 64:(hf + 1) * 64].rearrange("p c (k e) -> p c k e", e=C1),
                                in0=o[:, :, :, 0:C1],
                                in1=rden[:, :, :].unsqueeze(3).broadcast_to([P, 2, 8, C1]),
                                op=ALU.mult).then_inc(S[f"free{bank}"], 1)

            def iteration(i, m):
                next_, done = fits(i, 1), fits(i, -1)
                for g in range(8):
                    if next_:
                        maxima(i + 1, g)
                    if g == 0 and done:
                        normalise(i - 1, 0)
                    if g == 1 and fits(i, AHEAD):
                        stats_x(i + AHEAD, m)
                    if g == 2 and fits(i, -2):
                        residual(i)
                    if g == 4 and done:
                        normalise(i - 1, 1)
                    if g == 7 and fits(i, AHEAD):
                        split_qk(i + AHEAD, m)

            for b in range(AHEAD):
                stats_x(b, b)
                if b == 3:
                    V.memset(ks[0:MAX_ROW, :, 2:4, :].rearrange("p h b l -> p h (b l)").bitcast(F32),
                             0.0).then_inc(S["zeroed2"], 1)
                if b >= 1:
                    split_qk(b - 1, b - 1)
            split_qk(3, 3)
            for g in range(8):
                maxima(0, g)
            pipeline(dve, iteration)

        @block.scalar
        def _(act):
            A = nc.scalar

            def first_parts(b, m):
                bank, before = qk_use(b)
                act.wait_ge(S[f"full{bank}"], count(before + 1))
                act.wait_ge(S[f"stack{m // 2}"], count(stack_count(b - 4, m)))
                for k in range(2):
                    A.activation(parts[:, m // 2, 0, k, m % 2, :], misc[bank][:, k * L1:(k + 1) * L1], ACT.Identity,
                                 bias=b_col[:, k:k + 1]).then_inc(S["p1_ok"], 1)

            def copy_out(dst, banks, rows, use):
                bank, before = use
                act.wait_ge(S[f"full{bank}"], count(before + 1))
                A.activation(dst, banks[bank][0:rows, 0:L1], ACT.Copy).then_inc(S[f"free{bank}"], 1)

            def max_rows(b, hf):
                act.wait_ge(S[f"mrow{hf}"], count(16 * b))
                act.wait_ge(S[f"mrow{1 - hf}"], count(16 * (b + hf)))
                copy_out(mT[:, :], misch, 24, max_use(b, hf))

            def out_rows(b, hf):
                act.wait_ge(S["av_done"], count(4 * b + 2 * hf + 2))
                if not isinstance(b, int) or b >= 1:
                    bank, before = out_use(b - 1, hf)
                    act.wait_ge(S[f"full{bank}"], count(before + 1))
                A.activation(osb[:, hf, :], psO[:, :], ACT.Copy).then_inc(S["o_ev"], 1)

            def v_in(b, m, only):
                bank, before = v_use(b)
                act.wait_ge(S[f"full{bank}"], count(before + 1))
                A.activation(v32[:, m, :, :, 0:C1], misc[bank][:, 0:2 * P].rearrange("p (a h c) -> p a h c", a=2, c=C1),
                             ACT.Copy).then_inc(S[f"free{bank}" if only else "v_ok"], 1)

            def exponentials(b, h):
                act.wait_ge(S["b_full"], count(16 * b + h + 1))
                if h % 4 == 0:
                    act.wait_ge(S["av_done"], count(4 * b + h // 4 - 1))
                A.activation(pr[:, h % PRING, :, :].rearrange("p c l -> p (c l)"), psB[:, h % 3, :], ACT.Exp,
                             scale=SCALE1).then_inc(S["b_free"], 1)

            def iteration(i, m):
                here, next_, done, ahead = fits(i, 0), fits(i, 1), fits(i, -1), fits(i, AHEAD)
                for g in range(8):
                    if here:
                        exponentials(i, 2 * g)
                        exponentials(i, 2 * g + 1)
                    if g == 2 and done:
                        out_rows(i - 1, 1)
                    if g == 1 and here:
                        max_rows(i, 1)
                    if g == 2 and fits(i, 3):
                        v_in(i + 3, (m + 3) % 4, isinstance(i, int) and i < 2)
                    if g == 3 and ahead:
                        copy_out(xnT[:, :], misc, P, xT_use(i + AHEAD))
                    if g == 5 and here:
                        out_rows(i, 0)
                    if g == 5 and next_:
                        max_rows(i + 1, 0)
                    if g == 6 and ahead:
                        first_parts(i + AHEAD, m)
                    if g == 7 and done:
                        bank, before = use_no(7, i)
                        act.wait_ge(S[f"full{bank}"], count(before + 1))
                        A.activation(onT[:, :], misc[bank][:, 0:L1], ACT.Identity, bias=bv_col[:, :]
                                     ).then_inc(S[f"free{bank}"], 1)

            act.wait_ge(S["consts"], 1)
            A.activation(ks[MAX_ROW:P, :, :, :].rearrange("p h b l -> p (h b l)").bitcast(F32),
                         one_pair[MAX_ROW:P, :].broadcast_to([P - MAX_ROW, H1 * 2 * L1]),
                         ACT.Copy).then_inc(S["zeroed"], 1)
            A.activation(qs[:, :, 0:2, :].rearrange("p h b l -> p h (b l)").bitcast(F32),
                         zero[:, :].unsqueeze(2).broadcast_to([P, H1, L1]), ACT.Copy).then_inc(S["zeroed"], 1)
            act.wait_ge(S["ld_b"], 64)
            for b in range(AHEAD):
                copy_out(xnT[:, :], misc, P, xT_use(b))
                if b < 3:
                    v_in(b, b, True)
                first_parts(b, b)
            max_rows(0, 0)
            pipeline(act, iteration)

        @block.gpsimd
        def _(pool):
            G = nc.gpsimd
            G.memset(minus_half[:, :], -0.5)
            G.memset(one_pair[:, :].bitcast(BF16), 1.0)
            G.memset(zero[:, :], 0.0)
            G.memset(ident[:, :], 0.0).then_inc(S["consts"], 1)
            pool.wait_ge(S["consts"], 1)
            G.affine_select(out=ident[:, :], in_=ident[:, :], compare_op=ALU.not_equal, fill=1.0, base=0,
                            pattern=[[-1, P]], channel_multiplier=1).then_inc(S["consts"], 1)
            pool.wait_ge(S["consts"], 2)
            pool.sem_inc(S["passed"])
            G.tensor_copy(identh[:, :], ident[:, :]).then_inc(S["consts_p"], 1)

            def ln_scale(kind, b):
                step, before = f"ln{kind}_step", (3 + kind) * b
                pool.wait_ge(S[f"aggr{kind}"], count(b + 1))
                pool.sem_inc(S["passed"])
                G.tensor_scalar(ve[kind][:, :], mv[kind][:, :, 1], EPS, None, ALU.add).then_inc(S[step], 1)
                G.tensor_scalar(nm[kind][:, :], mv[kind][:, :, 0], -1.0, None, ALU.mult).then_inc(S[step], 1)
                pool.wait_ge(S[step], count(before + 1))
                G.tensor_tensor(rs[kind][:, :], ve[kind][:, :], minus_half[:, :], ALU.pow).then_inc(S[step], 1)
                pool.wait_ge(S[step], count(before + 3))
                pool.sem_inc(S["passed"])

            def norm_x(b, m):
                ln_scale(0, b)
                if not isinstance(b, int) or b >= 1:
                    bank, before = xT_use(b - 1)
                    pool.wait_ge(S[f"full{bank}"], count(before + 1))
                    pool.sem_inc(S["passed"])
                for c in range(2):
                    last = G.tensor_scalar(xn[:, c, :], xin[:, m % 2, c, :], nm[0][:, c:c + 1], rs[0][:, c:c + 1],
                                           ALU.add, ALU.mult)
                last.then_inc(S["xn_ok"], 1)
                pool.wait_ge(S["xn_ok"], count(b + 1))
                G.tensor_tensor(xnb_all[:, bass.ds(b * 2, 2), :], xn[:, :, :],
                                bo_row[:, :].unsqueeze(1).broadcast_to([P, 2, P]), ALU.add).then_inc(S["xnb_ok"], 1)

            def last_parts(b, m):
                pool.wait_ge(S["p2_ok"], count(b + 1))
                G.tensor_tensor(parts[:, m // 2, 2, :, m % 2, :], rest[:, :, :], parts[:, m // 2, 1, :, m % 2, :],
                                ALU.subtract).then_inc(S["p3_ok"], 1)

            def split_max(b, hf):
                src = nmax[:, :, hf * HALF:(hf + 1) * HALF]
                n = 3 * (2 * b + hf)
                pool.wait_ge(S["a_free"], count(16 * b + 8 * hf + 8))
                if not isinstance(b, int) or b + hf > 0:
                    bank, before = max_use(b, 0) if hf else max_use(b - 1, 1)
                    pool.wait_ge(S[f"full{bank}"], count(before + 1))
                    pool.sem_inc(S["passed"])
                G.tensor_copy(mparts[:, :, 0, :], src).then_inc(S["split_step"], 1)
                pool.wait_ge(S["split_step"], count(n + 1))
                G.tensor_tensor(nmr[:, :, :], src, mparts[:, :, 0, :], ALU.subtract).then_inc(S["split_step"], 1)
                pool.wait_ge(S["split_step"], count(n + 2))
                pool.sem_inc(S["passed"])
                G.tensor_copy(mparts[:, :, 1, :], nmr[:, :, :]).then_inc(S["split_step"], 1)
                pool.wait_ge(S["split_step"], count(n + 3))
                G.tensor_tensor(mparts[:, :, 2, :], nmr[:, :, :], mparts[:, :, 1, :],
                                ALU.subtract).then_inc(S["mp_ok"], 1)

            def add_attention(b):
                ln_scale(1, b)
                for c in range(2):
                    last = G.tensor_scalar(nr[:, c, :], r1[:, c, :], nm[1][:, c:c + 1], rs[1][:, c:c + 1],
                                           ALU.add, ALU.mult)
                last.then_inc(S["ln1_step"], 1)
                pool.wait_ge(S["ln1_step"], count(4 * b + 4))
                G.tensor_tensor(x_all[:, bass.ds(b * 2, 2), :], nr[:, :, :], x_all[:, bass.ds(b * 2, 2), :],
                                ALU.add).then_inc(S["x1_ok"], 1)

            def iteration(i, m):
                if fits(i, 0):
                    split_max(i, 1)
                if fits(i, 3):
                    last_parts(i + 3, (m + 3) % 4)
                if fits(i, AHEAD):
                    norm_x(i + AHEAD, m)
                if fits(i, 1):
                    split_max(i + 1, 0)
                if fits(i, -2):
                    add_attention(i - 2)
                if isinstance(i, int) and i == 1:
                    pool.wait_ge(S["ld_x"], 16)

            G.memset(v32[:, :, :, :, C1 + 1:32], 0.0)
            G.memset(v32[:, :, :, :, C1:C1 + 1], 1.0)
            pool.wait_ge(S["ld_b"], 64)
            norm_x(0, 0)
            for b in range(1, AHEAD):
                norm_x(b, b)
                last_parts(b - 1, b - 1)
                if b == 2:
                    G.memset(qs[:, :, 2:4, :].rearrange("p h b l -> p h (b l)").bitcast(F32),
                             0.0).then_inc(S["zeroed2"], 1)
            split_max(0, 0)
            pipeline(pool, iteration)

        @block.sync
        def _(sp):
            def load_x(b, m):
                sp.wait_ge(S["xn_ok"], count(b - 1))
                sp.dma_start(xin[:, m % 2, :, :], x_t[b]).then_inc(S[f"x_in{m % 2}"], 16)

            def stack(b, m):
                if isinstance(b, int) and b == 2:
                    sp.wait_ge(S["zeroed2"], 2)
                sp.wait_ge(S["p3_ok"], count(b + 2))
                sp.sem_inc(S["passed"])
                if not isinstance(b, int) or b >= 4:
                    sp.wait_ge(S["b_full"], count(16 * (b - 2)))
                for dst, k, which in ((qs, 0, Q_PART), (ks, 1, K_PART)):
                    for j, part in enumerate(which):
                        sp.dma_start(dst[C1 * j:C1 * (j + 1), :, m:m + 2, :].rearrange("c h b l -> c h (b l)"),
                                     parts[:, m // 2, part, k, :, :].rearrange("p b l -> p (b l)")
                                     ).then_inc(S[f"stack{m // 2}"], 16)

            def max_rows(b, m, hf):
                bank, before = max_use(b, hf)
                sp.wait_ge(S[f"free{bank}"], count(before + 1))
                sp.dma_start(qs[MAX_ROW:MAX_ROW + 3, hf * HALF:(hf + 1) * HALF, m, :],
                             mT[:, :]).then_inc(S[f"mrow{hf}"], 16)

            def iteration(i, m):
                if fits(i, AHEAD):
                    load_x(i + AHEAD, m)
                if fits(i, 0):
                    max_rows(i, m, 1)
                if m % 2 == 0 and fits(i, 2):
                    stack(i + 2, (m + 2) % 4)
                if fits(i, 1):
                    max_rows(i + 1, (m + 1) % 4, 0)
                if not isinstance(i, int):
                    pass
                elif i >= 10:
                    for b in range((0 if i == 10 else i - 3), i - 2):
                        x1_over(b)

            def x1_over(b):
                sp.wait_ge(S["x1_ok"], count(b + 1))
                sp.dma_start(xs[(L1 // 32) * b:(L1 // 32) * (b + 1), :, :].rearrange("p j d -> p (j d)"),
                             x_all[:, 2 * b:2 * b + 2, :].rearrange("p c d -> p (c d)")).then_inc(S["stored"], 16)

            load_x(0, 0)
            load_x(1, 1)
            sp.dma_start(w_nat[:, 0:3, :], w_qkv.rearrange("(k p) d -> p k d", p=P)).then_inc(S["ld_w"], 16)
            sp.dma_start(w_nat[:, 3, :], w_o).then_inc(S["ld_w"], 16)
            for k in range(2):
                sp.dma_start(b_col[:, k:k + 1], b_qkv[k * P:(k + 1) * P].rearrange("(h c o) -> c h o", c=C1, o=1),
                             allow_slow_non_contiguous=True).then_inc(S["ld_b"], 16)
            sp.dma_start(bv_col[:, :], b_qkv[2 * P:3 * P].rearrange("(p o) -> p o", o=1),
                         allow_slow_non_contiguous=True).then_inc(S["ld_b"], 16)
            sp.dma_start(bo_row[:, :], b_o.partition_broadcast(P)).then_inc(S["ld_b"], 16)
            load_x(2, 2)
            load_x(3, 3)
            sp.wait_ge(S["zeroed"], 3)
            stack(0, 0)
            max_rows(0, 0, 0)
            sp.dma_start(x_all[:, :, :].rearrange("p (b c) d -> p b c d", c=2),
                         x.rearrange("b (p c) d -> p b c d", p=P)).then_inc(S["ld_x"], 16)
            for to, source in loads2:
                sp.dma_start(to, source, allow_slow_non_contiguous=True).then_inc(loaded2, 16)
            pipeline(sp, iteration)
            x1_over(LAST)
            sp.wait_ge(S["stored"], count(16 * B1))


H2, C2 = 4, 32
S2 = B1
SCALE2 = 1.0 / float(C2) ** 0.5
NSTEP = NT // 2
NE, DF = 8, 512
NS = (B1 * L1 + NE * (P - 1)) // P
REGION = NT * P + P
LAST_ROW = NE * REGION + (NS - NT) * P
CHUNK = 8
SORT_AT = {16: 0, 17: 1, 20: 2}
SEND_AT = {17: (0, 0), 18: (0, 4), 19: (1, 0), 20: (1, 4), 21: (2, 0), 22: (2, 4)}


def attention_parameters(nc, ctx, w):
    Wqkv, bqkv, Wo, bo, g1, be1, Wg = w
    u_nat = ctx.enter_context(nc.sbuf_tensor("u_nat", [P, 4, P], F32))
    wg_nat = ctx.enter_context(nc.sbuf_tensor("wg_nat", [NE, P], F32))
    u_col = ctx.enter_context(nc.sbuf_tensor("u_col", [P, 3], F32))
    rows = ctx.enter_context(nc.sbuf_tensor("rows", [P, 3, P], F32))
    loads = [(u_nat[:, 0:3, :], Wqkv.rearrange("(k p) d -> p k d", p=P)), (u_nat[:, 3, :], Wo), (wg_nat[:, :], Wg)]
    loads += [(u_col[:, k:k + 1], bqkv[k * P:(k + 1) * P].rearrange("(p o) -> p o", o=1)) for k in range(3)]
    loads += [(rows[:, k, :], row.partition_broadcast(P)) for k, row in enumerate((bo, g1, be1))]
    return (u_nat, wg_nat, u_col, rows), loads


def second_attention(nc, parameters, loaded2, loads2, ident, identh, minus_half, xs, y_all, logits, loaded, loads,
                     y_sorted, slots, slot_i, base, sorting, sent):
    u_nat, wg_nat, u_col, rows = parameters
    with ExitStack() as ctx:
        def sb(name, shape, dt=F32):
            return ctx.enter_context(nc.sbuf_tensor(name, shape, dt))

        def pb(name):
            return ctx.enter_context(nc.psum_tensor(name, [P, 512], F32))

        uT = sb("uT", [P, 4, P])
        wgT = sb("wgT", [P, NE])
        zeros = sb("zeros", [P, (NS - NT) * P])
        before = sb("before", [P, P])
        every = sb("every", [P, P])
        pref = sb("pref", [P, NE])
        best = sb("best", [P, CHUNK])
        hit = sb("hit", [P, CHUNK, NE])
        ranked = sb("ranked", [P, CHUNK, NE])
        mine = sb("mine", [P, CHUNK, NE])
        run = [sb(f"run{k}", [P, CHUNK // 2 + CHUNK, NE]) for k in range(2)]
        place = sb("place", [P, CHUNK, NE])
        pad_i = sb("pad_i", [P, NE], I32)
        number = sb("number", [P, 40])
        full = sb("full", [P, NT])
        start = sb("start", [P, NE])
        total = sb("total", [P, NE])
        more = sb("more", [P, NE, NT])
        ends = [sb(f"ends{k}", [P, NE // 2 + NE]) for k in range(2)]
        hop = sb("hop", [P, NE])
        hops = sb("hops", [P, NS, NE])
        beyond = sb("beyond", [P, NT, NE])
        back = sb("back", [P, NT])
        row = sb("row", [P, NS])
        past = sb("past", [P, NS, NE])
        owner = sb("owner", [P, NS])
        first_i, w2_i, row_i, back_i = sorting
        same = sb("same", [P, 8])
        mask = sb("mask", [P, P], BF16)
        x2n = sb("x2n", [P, 2, 2, P])
        st_x, st_y = sb("st_x", [P, 2, 6]), sb("st_y", [P, 2, 6])
        mv_x, mv_y = sb("mv_x", [P, 2, 2]), sb("mv_y", [P, 2, 2, 2])
        ve_x, ve_y = sb("ve_x", [P, 2]), sb("ve_y", [P, 2])
        nm_x, nm_y = sb("nm_x", [P, 2]), sb("nm_y", [P, 2])
        rs_x, rs_y = sb("rs_x", [P, 2]), sb("rs_y", [P, 2])
        xy = sb("xy", [P, 2, 512])
        qT2 = sb("qT2", [P, 2, H2, L1])
        kT2 = sb("kT2", [P, 2, L1])
        v2 = sb("v2", [P, 4, 2, P])
        nmax2 = sb("nmax2", [P, 2, H2])
        nbias = sb("nbias", [P, 2, H2])
        den = sb("den", [P, 2, 2, H2])
        rden2 = sb("rden2", [P, 2, H2])
        prob = sb("prob", [P, 2, 2, H2, P])
        probT = sb("probT", [P, 2, 512])
        attT = sb("attT", [P, L1])
        r2 = sb("r2", [P, 2, 2, P])
        yn = sb("yn", [P, 2, P])
        yg = sb("yg", [P, 2, P])
        yout = sb("yout", [P, 2, 2, P])
        xs_flat = xs[:, :, :].rearrange("p j d -> p (j d)")
        psXY, psQK, psVO, psAL = pb("psXY"), pb("psQK"), pb("psVO"), pb("psAL")
        psS = [pb("psS0"), pb("psS1")]
        psP = [pb("psP0"), pb("psP1")]

        names = ["passed", "wT_full", "wT_ok", "same_ok", "zeros_ok", "zeroed", "consts", "sorting", "mine_ok",
                 "sums_full", "slots_ok", "pads_ok", "padded", "tail", "start_ok", "owner_ok", "rows_ok", "back_ok",
                 "q_zero", "mask_ok", "xst", "xagg", "xstep", "xrs_ok", "xn2_ok", "xnb2_ok", "xy_full", "xy_read",
                 "qk_full", "q_ok", "k_ok", "vo_full", "v2_ok", "r2_ok", "s_full", "m_step", "max_ok", "p_ok",
                 "rd_ok", "pn_ok", "pt_full", "pt_ok", "al_full", "att_ok", "lg_ok", "yst", "yagg", "ystep",
                 "yln_step", "y_ok", "y_kept"]
        S = {n: ctx.enter_context(nc.semaphore("l2_" + n)) for n in names}

        def has(t, lag):
            return not isinstance(t, int) or 0 <= t - lag < NSTEP

        def pipeline(iteration):
            def run(eng):
                for t in range(8):
                    iteration(t, t)
                with eng.Fori(0, 2) as four:
                    for r in range(4):
                        iteration(four * 4 + (8 + r), r)
                for t in range(16, NSTEP + 8):
                    iteration(t, t % 4)
            return run

        def late(t):
            return isinstance(t, int) and t >= NSTEP

        block = ctx.enter_context(nc.Block())

        @block.tensor
        def _(pe):
            T = nc.tensor
            pe.wait_ge(loaded2, 16 * len(loads2))
            for k in range(4):
                last = T.transpose(psS[0][:, k * P:(k + 1) * P], u_nat[:, k, :], ident[:, :])
            last = T.transpose(psS[1][:, 0:NE], wg_nat[:, :], ident[0:NE, 0:NE])
            last.then_inc(S["wT_full"], 1)
            pe.wait_ge(S["wT_ok"], 2)
            pe.wait_ge(S["mask_ok"], 1)

            def sums(k):
                pe.wait_ge(S["consts"], 2)
                pe.wait_ge(S["mine_ok"], k + 1)
                pe.wait_ge(S["q_ok"], NSTEP)
                pe.wait_ge(S["k_ok"], NSTEP)
                pe.wait_ge(S["slots_ok"], k)
                flat = mine[:, :, :].rearrange("p j e -> p (j e)")
                T.matmul(psQK[:, 0:CHUNK * NE], before[:, :], flat, start=True, stop=True)
                T.matmul(psQK[:, CHUNK * NE:2 * CHUNK * NE], every[:, :], flat, start=True,
                         stop=True).then_inc(S["sums_full"], 1)

            def iteration(t, m):
                if has(t, 1):
                    pe.wait_ge(S["xy_read"], count(t))
                    pe.wait_ge(S["q_ok"], count(t - 1))
                    pe.wait_ge(S["k_ok"], count(t - 1))
                    for k in range(2):
                        last = T.matmul(psQK[:, k * L1:(k + 1) * L1], uT[:, k, :], xy[:, (m - 1) % 2, 0:L1],
                                        start=True, stop=True)
                    last.then_inc(S["qk_full"], 1)
                if has(t, 1) or has(t, 5):
                    pe.wait_ge(S["v2_ok"], count(min(t - 1, NSTEP) if isinstance(t, int) else t - 1))
                    pe.wait_ge(S["r2_ok"], count(t - 5))
                    if has(t, 1):
                        for c in range(2):
                            last = T.matmul(psVO[:, c * P:(c + 1) * P], xy[:, (m - 1) % 2, c * P:(c + 1) * P],
                                            uT[:, 2, :], start=True, stop=True)
                    if has(t, 5):
                        pe.wait_ge(S["att_ok"], count(t - 4))
                        for c in range(2):
                            last = T.matmul(psVO[:, (2 + c) * P:(3 + c) * P], attT[:, c * P:(c + 1) * P],
                                            uT[:, 3, :], start=True, stop=True)
                    last.then_inc(S["vo_full"], 1)
                if has(t, 2):
                    i, n = t - 2, (m - 2) % 2
                    pe.wait_ge(S["q_ok"], count(i + 1))
                    pe.wait_ge(S["k_ok"], count(i + 1))
                    for c in range(2):
                        pe.wait_ge(S["p_ok"], count(8 * (i - 1) + 4 * c + 4))
                        for h in range(H2):
                            at = psS[c][:, h * P:(h + 1) * P]
                            T.matmul(at, identh[:, :], mask[:, :], start=True, stop=False)
                            last = T.matmul(at, qT2[:, n, h, c * P:(c + 1) * P],
                                            kT2[:, n, c * P:(c + 1) * P], start=False, stop=True)
                        last.then_inc(S["s_full"], 1)
                if has(t, 0) or has(t, 7):
                    pe.wait_ge(S["xy_read"], count(t))
                    if has(t, 0):
                        pe.wait_ge(S["xn2_ok"], count(t + 1))
                        for c in range(2):
                            last = T.transpose(psXY[:, c * P:(c + 1) * P], x2n[:, m % 2, c, :], ident[:, :])
                    if has(t, 7):
                        pe.wait_ge(S["y_ok"], count(t - 6))
                        for c in range(2):
                            last = T.transpose(psXY[:, (2 + c) * P:(3 + c) * P], yout[:, (m - 7) % 2, c, :],
                                               ident[:, :])
                    last.then_inc(S["xy_full"], 1)
                if has(t, 4) or has(t, 8):
                    pe.wait_ge(S["att_ok"], count(min(t - 4, NSTEP) if isinstance(t, int) else t - 4))
                    pe.wait_ge(S["lg_ok"], count(t - 8))
                    if has(t, 4):
                        pe.wait_ge(S["pt_ok"], count(2 * (t - 4) + 2))
                        pe.wait_ge(S["v2_ok"], count(t - 3))
                        for c in range(2):
                            for h in range(H2):
                                last = T.matmul(psAL[C2 * h:C2 * h + C2, c * P:(c + 1) * P],
                                                v2[:, m % 4, c, C2 * h:C2 * h + C2],
                                                probT[:, c, h * P:(h + 1) * P], start=True, stop=True,
                                                tile_position=(0, C2 * h))
                    if has(t, 8):
                        pe.wait_ge(S["xy_read"], count(t))
                        for c in range(2):
                            last = T.matmul(psAL[:, L1 + NE * c:L1 + NE * (c + 1)],
                                            xy[:, (m - 1) % 2, (2 + c) * P:(3 + c) * P], wgT[:, :], start=True,
                                            stop=True)
                    last.then_inc(S["al_full"], 1)
                if has(t, 3):
                    i = t - 3
                    for c in range(2):
                        pe.wait_ge(S["pn_ok"], count(2 * i + c + 1))
                        pe.wait_ge(S["pt_ok"], count(2 * (i - 1) + c + 1))
                        for h in range(H2):
                            last = T.transpose(psP[c][:, h * P:(h + 1) * P], prob[:, (m - 3) % 2, c, h, :],
                                               ident[:, :])
                        last.then_inc(S["pt_full"], 1)
                if isinstance(t, int) and t in SORT_AT:
                    sums(SORT_AT[t])

            pipeline(iteration)(pe)
            sums(NT // CHUNK - 1)

        @block.vector
        def _(dve):
            V = nc.vector
            V.tensor_reduce(same[:, :], ident[:, :].rearrange("p (s r) -> p r s", r=8), AX.X,
                            ALU.add).then_inc(S["same_ok"], 1)
            dve.wait_ge(S["same_ok"], 1)
            V.tensor_scalar(mask[:, :].rearrange("p (s r) -> p s r", r=8),
                            same[:, :].unsqueeze(1).broadcast_to([P, S2, 8]), -1.0, 1e30, ALU.add,
                            ALU.mult).then_inc(S["mask_ok"], 1)
            dve.wait_ge(S["wT_full"], 1)
            V.tensor_copy(uT[:, :, :].rearrange("p k d -> p (k d)"), psS[0][:, :]).then_inc(S["wT_ok"], 1)
            V.tensor_copy(wgT[:, :], psS[1][:, 0:NE]).then_inc(S["wT_ok"], 1)
            dve.wait_ge(loaded2, 16 * len(loads2))

            def norm_x(i, n):
                dve.wait_ge(S["xn2_ok"], count(i))
                for c in range(2):
                    V.bn_stats(st_x[:, c, :], xs_flat[:, bass.ds(i * L1 + c * P, P)]).then_inc(S["xst"], 1)
                for c in range(2):
                    dve.wait_ge(S["xst"], count(2 * i + c + 1))
                    dve.sem_inc(S["passed"])
                    last = V.bn_aggr(mv_x[:, c, :], st_x[:, c, :])
                last.then_inc(S["xagg"], 1)

            def apply_x(i, n):
                dve.wait_ge(S["xrs_ok"], count(i + 1))
                dve.wait_ge(S["xnb2_ok"], count(i - 1))
                dve.wait_ge(S["xy_full"], count(i - 1))
                for c in range(2):
                    last = V.tensor_scalar(x2n[:, n, c, :], xs_flat[:, bass.ds(i * L1 + c * P, P)],
                                           nm_x[:, c:c + 1], rs_x[:, c:c + 1], ALU.add, ALU.mult)
                last.then_inc(S["xn2_ok"], 1)

            def maxima(i, c):
                dve.wait_ge(S["s_full"], count(2 * i + c + 1))
                V.tensor_reduce(nmax2[:, c, :], psS[c][:, :].rearrange("p (h k) -> p h k", h=H2), AX.X,
                                ALU.max, negate=True).then_inc(S["m_step"], 1)
                dve.wait_ge(S["m_step"], count(2 * i + c + 1))
                dve.wait_ge(S["p_ok"], count(8 * (i - 1) + 4 * c + 4))
                V.tensor_scalar(nbias[:, c, :], nmax2[:, c, :], SCALE2, None,
                                ALU.mult).then_inc(S["max_ok"], 1)

            Z = CHUNK // 2
            SORT_STEPS = 13

            def mark(k):
                mine_of = logits[:, k * CHUNK:(k + 1) * CHUNK, :]
                n = SORT_STEPS * k
                dve.wait_ge(S["lg_ok"], (k + 1) * CHUNK // 2)
                dve.wait_ge(S["consts"], 2)
                V.tensor_reduce(best[:, :], mine_of, AX.X, ALU.max).then_inc(S["sorting"], 1)
                dve.wait_ge(S["sorting"], n + 1)
                V.tensor_tensor(hit[:, :, :], mine_of, best[:, :].unsqueeze(2).broadcast_to([P, CHUNK, NE]),
                                ALU.is_ge).then_inc(S["sorting"], 1)
                dve.wait_ge(S["sorting"], n + 2)
                V.tensor_tensor(ranked[:, :, :], hit[:, :, :],
                                pref[:, :].unsqueeze(1).broadcast_to([P, CHUNK, NE]), ALU.mult
                                ).then_inc(S["sorting"], 1)
                dve.wait_ge(S["sorting"], n + 3)
                V.tensor_reduce(best[:, :], ranked[:, :, :], AX.X, ALU.max).then_inc(S["sorting"], 1)
                dve.wait_ge(S["sorting"], n + 4)
                V.tensor_tensor(mine[:, :, :], ranked[:, :, :],
                                best[:, :].unsqueeze(2).broadcast_to([P, CHUNK, NE]), ALU.is_equal
                                ).then_inc(S["mine_ok"], 1)

            def find(k):
                n = SORT_STEPS * k + 4
                dve.wait_ge(S["sums_full"], k + 1)
                V.tensor_copy(run[0][:, Z:, :].rearrange("p j e -> p (j e)"),
                              psQK[:, CHUNK * NE:2 * CHUNK * NE]).then_inc(S["sorting"], 1)
                dve.wait_ge(S["sorting"], n + 1)
                for step in range(3):
                    a, b = run[step % 2], run[1 - step % 2]
                    V.tensor_tensor(b[:, Z:, :], a[:, Z:, :], a[:, Z - 2 ** step:Z + CHUNK - 2 ** step, :],
                                    ALU.add).then_inc(S["sorting"], 1)
                    dve.wait_ge(S["sorting"], n + 2 + step)
                V.tensor_tensor(place[:, :, :], psQK[:, 0:CHUNK * NE].rearrange("p (j e) -> p j e", e=NE),
                                run[1][:, Z - 1:Z - 1 + CHUNK, :], ALU.add).then_inc(S["sorting"], 1)
                dve.wait_ge(S["sorting"], n + 5)
                V.tensor_tensor(place[:, :, :], place[:, :, :],
                                base[:, :].unsqueeze(1).broadcast_to([P, CHUNK, NE]), ALU.add
                                ).then_inc(S["sorting"], 1)
                dve.wait_ge(S["sorting"], n + 6)
                V.tensor_tensor(base[:, :], base[:, :], run[1][:, Z + CHUNK - 1, :], ALU.add
                                ).then_inc(S["sorting"], 1)
                V.tensor_tensor(place[:, :, :], place[:, :, :], mine[:, :, :], ALU.mult
                                ).then_inc(S["sorting"], 1)
                dve.wait_ge(S["sorting"], n + 8)
                these = slice(k * CHUNK, (k + 1) * CHUNK)
                V.tensor_reduce(slots[:, these], place[:, :, :], AX.X, ALU.add).then_inc(S["sorting"], 1)
                dve.wait_ge(S["sorting"], n + 9)
                V.tensor_copy(slot_i[:, these], slots[:, these]).then_inc(S["slots_ok"], 1)

            def finish_y(i, n, t):
                dve.wait_ge(S["yln_step"], 3 * i + 2)
                V.tensor_tensor(yg[:, :, :], yn[:, :, :], rows[:, 1:2, :].broadcast_to([P, 2, P]),
                                ALU.mult).then_inc(S["yln_step"], 1)
                dve.wait_ge(S["yln_step"], 3 * i + 3)
                dve.wait_ge(S["xy_full"], t)
                dve.wait_ge(S["y_kept"], count(i - 1))
                V.tensor_tensor(yout[:, n, :, :], yg[:, :, :], rows[:, 2:3, :].broadcast_to([P, 2, P]),
                                ALU.add).then_inc(S["y_ok"], 1)

            def iteration(t, m):
                if isinstance(t, int) and t in SORT_AT:
                    mark(SORT_AT[t])
                if has(t, 0):
                    norm_x(t, m % 2)
                if has(t, 1):
                    dve.wait_ge(S["qk_full"], count(t))
                    dve.wait_ge(S["s_full"], count(2 * (t - 1) - 2))
                    V.tensor_scalar(kT2[:, (m - 1) % 2, :], psQK[:, L1:2 * L1], u_col[:, 1:2], None,
                                    ALU.add).then_inc(S["k_ok"], 1)
                if has(t, 0):
                    apply_x(t, m % 2)
                if has(t, 3):
                    i, n = t - 3, (m - 3) % 2
                    for c in range(2):
                        dve.wait_ge(S["p_ok"], count(8 * i + 4 * c + 4))
                        dve.wait_ge(S["pn_ok"], count(2 * (i - 1) + c + 1))
                        V.reciprocal(rden2[:, c, :], den[:, n, c, :]).then_inc(S["rd_ok"], 1)
                        dve.wait_ge(S["rd_ok"], count(2 * i + c + 1))
                        V.tensor_tensor(out=prob[:, n, c, :, :], in0=prob[:, n, c, :, :],
                                        in1=rden2[:, c, :].unsqueeze(2).broadcast_to([P, H2, P]),
                                        op=ALU.mult).then_inc(S["pn_ok"], 1)
                if has(t, 2):
                    maxima(t - 2, 0)
                if has(t, 2):
                    maxima(t - 2, 1)
                if has(t, 7):
                    i, n = t - 7, (m - 7) % 2
                    dve.wait_ge(S["y_ok"], count(i + 1))
                    dve.sem_inc(S["passed"])
                    V.tensor_copy(y_all[:, bass.ds(i * 2, 2), :], yout[:, n, :, :]).then_inc(S["y_kept"], 1)
                if late(t) and has(t, 6):
                    finish_y(t - 6, m % 2, t)
                if has(t, 5):
                    i, n = t - 5, (m - 5) % 2
                    dve.wait_ge(S["vo_full"], count(t))
                    if has(t, 1):
                        dve.wait_ge(S["v2_ok"], count(t))
                    dve.wait_ge(S["y_ok"], count(i - 1))
                    dve.wait_ge(S["xnb2_ok"], count(i + 1))
                    V.tensor_tensor(out=r2[:, n, :, :], in0=psVO[:, L1:2 * L1].rearrange("p (c d) -> p c d", c=2),
                                    in1=y_all[:, bass.ds(i * 2, 2), :], op=ALU.add).then_inc(S["r2_ok"], 1)
                    dve.wait_ge(S["r2_ok"], count(i + 1))
                    for c in range(2):
                        V.bn_stats(st_y[:, c, :], r2[:, n, c, :]).then_inc(S["yst"], 1)
                    for c in range(2):
                        dve.wait_ge(S["yst"], count(2 * i + c + 1))
                        dve.sem_inc(S["passed"])
                        last = V.bn_aggr(mv_y[:, n, c, :], st_y[:, c, :])
                    last.then_inc(S["yagg"], 1)
                if has(t, 8):
                    dve.wait_ge(S["al_full"], count(t - 3))
                    if has(t, 4):
                        dve.wait_ge(S["att_ok"], count(t - 3))
                    dve.sem_inc(S["passed"])
                    V.tensor_copy(logits[:, bass.ds((t - 8) * 2, 2), :],
                                  psAL[:, L1:L1 + 2 * NE].rearrange("p (c e) -> p c e", c=2)).then_inc(S["lg_ok"], 1)
                if isinstance(t, int) and t in SORT_AT:
                    find(SORT_AT[t])

            pipeline(iteration)(dve)
            mark(NT // CHUNK - 1)
            find(NT // CHUNK - 1)
            dve.wait_ge(S["slots_ok"], NT // CHUNK)
            done = SORT_STEPS * (NT // CHUNK)
            dve.wait_ge(S["sorting"], done)
            V.tensor_copy(pad_i[:, :], base[:, :]).then_inc(S["pads_ok"], 1)
            steps = [0]

            def step(instruction):
                steps[0] += 1
                instruction.then_inc(S["tail"], 1)
                dve.wait_ge(S["tail"], steps[0])

            Y = NE // 2
            V.memset(ends[0][:, 0:Y], 0.0)
            V.memset(ends[1][:, 0:Y], 0.0)
            dve.wait_ge(S["start_ok"], 1)
            V.tensor_scalar(full[:, :], number[:, 0:NT], float(P), None, ALU.mult)
            step(V.tensor_tensor(total[:, :], base[:, :], start[:, :], ALU.subtract))
            step(V.tensor_tensor(more[:, :, :], total[:, :].unsqueeze(2).broadcast_to([P, NE, NT]),
                                 full[:, :].unsqueeze(1).broadcast_to([P, NE, NT]), ALU.is_gt))
            step(V.tensor_reduce(ends[0][:, Y:], more[:, :, :], AX.X, ALU.add))
            V.tensor_scalar(hop[:, :], ends[0][:, Y:], -float(P), float(REGION), ALU.mult, ALU.add)
            for k in range(3):
                a, b = ends[k % 2], ends[1 - k % 2]
                step(V.tensor_tensor(b[:, Y:], a[:, Y:], a[:, Y - 2 ** k:Y + NE - 2 ** k], ALU.add))
            end = ends[1]
            step(V.tensor_tensor(past[:, :, :], end[:, Y:].unsqueeze(1).broadcast_to([P, NS, NE]),
                                 number[:, 0:NS].unsqueeze(2).broadcast_to([P, NS, NE]), ALU.is_le))
            step(V.tensor_tensor(hops[:, :, :], past[:, :, :], hop[:, :].unsqueeze(1).broadcast_to([P, NS, NE]),
                                 ALU.mult))
            step(V.tensor_reduce(row[:, :], hops[:, :, :], AX.X, ALU.add))
            step(V.scalar_tensor_tensor(out=row[:, :], in0=number[:, 0:NS], scalar=float(P), in1=row[:, :],
                                        op0=ALU.mult, op1=ALU.add))
            V.tensor_copy(row_i[:, :], row[:, :]).then_inc(S["rows_ok"], 1)
            step(V.tensor_reduce(owner[:, :], past[:, :, :], AX.X, ALU.add))
            step(V.tensor_scalar(owner[:, :], owner[:, :], float(NE - 1), None, ALU.min))
            V.tensor_scalar(first_i[:, :], owner[:, :], float(PACK), None, ALU.mult).then_inc(S["owner_ok"], 1)
            V.tensor_scalar(w2_i[:, :], owner[:, :], float(DF), None, ALU.mult).then_inc(S["owner_ok"], 1)
            dve.wait_ge(S["owner_ok"], 2)
            step(V.tensor_scalar(start[:, :], start[:, :], float(REGION), None, ALU.add))
            step(V.tensor_tensor(beyond[:, :, :], slots[:, :].unsqueeze(2).broadcast_to([P, NT, NE]),
                                 start[:, :].unsqueeze(1).broadcast_to([P, NT, NE]), ALU.is_ge))
            step(V.tensor_tensor(beyond[:, :, :], beyond[:, :, :],
                                 hop[:, :].unsqueeze(1).broadcast_to([P, NT, NE]), ALU.mult))
            step(V.tensor_reduce(back[:, :], beyond[:, :, :], AX.X, ALU.add))
            V.tensor_tensor(back_i[:, :], slots[:, :], back[:, :], ALU.subtract).then_inc(S["back_ok"], 1)


        @block.scalar
        def _(act):
            A = nc.scalar
            act.wait_ge(loaded2, 16 * len(loads2))
            act.wait_ge(S["q_zero"], 1)

            def exponentials(i, n, c):
                act.wait_ge(S["max_ok"], count(2 * i + c + 1))
                act.wait_ge(S["pt_full"], count(2 * (i - 2) + c + 1))
                for h in range(H2):
                    A.activation(prob[:, n, c, h, :], psS[c][:, h * P:(h + 1) * P], ACT.Exp,
                                 bias=nbias[:, c, h:h + 1], scale=SCALE2,
                                 accum_out=den[:, n, c, h:h + 1]).then_inc(S["p_ok"], 1)

            def iteration(t, m):
                if has(t, 1):
                    act.wait_ge(S["qk_full"], count(t))
                    act.wait_ge(S["s_full"], count(2 * (t - 1) - 2))
                    act.wait_ge(S["k_ok"], count(t))
                    for h in range(H2):
                        mine = slice(C2 * h, C2 * h + C2)
                        last = A.activation(qT2[mine, (m - 1) % 2, h, :], psQK[mine, 0:L1], ACT.Identity,
                                            bias=u_col[mine, 0:1])
                    last.then_inc(S["q_ok"], 1)
                if has(t, 4):
                    i = t - 4
                    for c in range(2):
                        act.wait_ge(S["pt_full"], count(2 * i + c + 1))
                        act.wait_ge(S["al_full"], count(i))
                        A.activation(probT[:, c, :], psP[c][:, :], ACT.Copy).then_inc(S["pt_ok"], 1)
                if has(t, 0) or has(t, 7):
                    act.wait_ge(S["xy_full"], count(t + 1))
                    act.wait_ge(S["vo_full"], count(min(t - 1, NSTEP) if isinstance(t, int) else t - 1))
                    act.wait_ge(S["al_full"], count(t - 4))
                    lo, hi = (0 if has(t, 0) else L1), (2 * L1 if has(t, 7) else L1)
                    A.activation(xy[:, m % 2, lo:hi], psXY[:, lo:hi], ACT.Copy).then_inc(S["xy_read"], 1)
                if has(t, 1):
                    act.wait_ge(S["vo_full"], count(t))
                    act.wait_ge(S["al_full"], count(t - 4))
                    A.activation(v2[:, (m - 1) % 4, :, :].rearrange("p c d -> p (c d)"), psVO[:, 0:L1],
                                 ACT.Copy).then_inc(S["v2_ok"], 1)
                if has(t, 2):
                    exponentials(t - 2, m % 2, 0)
                if has(t, 4):
                    act.wait_ge(S["al_full"], count(t - 3))
                    act.wait_ge(S["vo_full"], count(t))
                    A.activation(attT[:, :], psAL[:, 0:L1], ACT.Identity, bias=u_col[:, 2:3]
                                 ).then_inc(S["att_ok"], 1)
                if has(t, 2):
                    exponentials(t - 2, m % 2, 1)

            pipeline(iteration)(act)

        @block.gpsimd
        def _(pool):
            G = nc.gpsimd
            G.memset(zeros[:, :], 0.0).then_inc(S["zeros_ok"], 1)
            for e in range(NE):
                G.memset(pref[:, e:e + 1], float(NE - e))
                G.memset(base[:, e:e + 1], float(e * REGION))
            for k in range(2):
                G.memset(run[k][:, 0:CHUNK // 2, :], 0.0)
            G.memset(every[:, :], 1.0).then_inc(S["consts"], 1)
            pool.wait_ge(S["consts"], 1)
            G.affine_select(out=before[:, :], in_=every[:, :], compare_op=ALU.is_gt, fill=0.0, base=0,
                            pattern=[[1, P]], channel_multiplier=-1).then_inc(S["consts"], 1)
            G.memset(qT2[:, :, :, :], 0.0).then_inc(S["q_zero"], 1)
            pool.wait_ge(loaded2, 16 * len(loads2))

            def scale_of(agg, step, i, mv, ve, nm, rs):
                pool.wait_ge(S[agg], count(i + 1))
                pool.sem_inc(S["passed"])
                G.tensor_scalar(ve[:, :], mv[:, :, 1], EPS, None, ALU.add).then_inc(S[step], 1)
                G.tensor_scalar(nm[:, :], mv[:, :, 0], -1.0, None, ALU.mult).then_inc(S[step], 1)
                pool.wait_ge(S[step], count(2 * i + 2))
                return G.tensor_tensor(rs[:, :], ve[:, :], minus_half[:, :], ALU.pow)

            def ready_x(i, n):
                scale_of("xagg", "xstep", i, mv_x, ve_x, nm_x, rs_x).then_inc(S["xrs_ok"], 1)

            def add_bo(i, n):
                pool.wait_ge(S["xn2_ok"], count(i + 1))
                G.tensor_tensor(y_all[:, bass.ds(i * 2, 2), :], x2n[:, n, :, :],
                                rows[:, 0:1, :].broadcast_to([P, 2, P]), ALU.add).then_inc(S["xnb2_ok"], 1)

            def send(k, first):
                pool.wait_ge(S["slots_ok"], k + 1)
                pool.wait_ge(S["y_kept"], (k + 1) * CHUNK // 2)
                for j in range(k * CHUNK + first, k * CHUNK + first + 4):
                    G.indirect_dma_start(y_sorted, bass.IndirectOffsetOnAxis(slot_i[:, j:j + 1], 0), y_all[:, j, :],
                                         None).then_inc(sent, 16)

            def finish_y(i, n, t):
                pool.wait_ge(S["yln_step"], 3 * i + 2)
                G.tensor_tensor(yg[:, :, :], yn[:, :, :], rows[:, 1:2, :].broadcast_to([P, 2, P]),
                                ALU.mult).then_inc(S["yln_step"], 1)
                pool.wait_ge(S["yln_step"], 3 * i + 3)
                pool.wait_ge(S["xy_full"], t)
                pool.wait_ge(S["y_kept"], count(i - 1))
                G.tensor_tensor(yout[:, n, :, :], yg[:, :, :], rows[:, 2:3, :].broadcast_to([P, 2, P]),
                                ALU.add).then_inc(S["y_ok"], 1)

            def iteration(t, m):
                if has(t, 0):
                    ready_x(t, m % 2)
                if has(t, 0):
                    add_bo(t, m % 2)
                if isinstance(t, int) and t == 17:
                    for k in range(40):
                        G.memset(number[:, k:k + 1], float(k))
                    for e in range(NE):
                        last = G.memset(start[:, e:e + 1], float(e * REGION))
                    last.then_inc(S["start_ok"], 1)
                if has(t, 6):
                    i, n = t - 6, m % 2
                    if late(t):
                        pool.wait_ge(S["yln_step"], 3 * i)
                    scale_of("yagg", "ystep", i, mv_y[:, n, :, :], ve_y, nm_y, rs_y).then_inc(S["yln_step"], 1)
                    pool.wait_ge(S["yln_step"], 3 * i + 1)
                    pool.sem_inc(S["passed"])
                    for c in range(2):
                        last = G.tensor_scalar(yn[:, c, :], r2[:, n, c, :], nm_y[:, c:c + 1], rs_y[:, c:c + 1],
                                               ALU.add, ALU.mult)
                    last.then_inc(S["yln_step"], 1)
                    if not late(t):
                        finish_y(i, n, t)
                if isinstance(t, int) and t in SEND_AT:
                    send(*SEND_AT[t])

            pipeline(iteration)(pool)
            send(NT // CHUNK - 1, 0)
            send(NT // CHUNK - 1, 4)

        @block.sync
        def _(sp):
            for to, source in loads:
                sp.dma_start(to, source).then_inc(loaded, 16)
            sp.wait_ge(S["zeros_ok"], 1)
            sp.dma_start(y_sorted[NE * REGION:LAST_ROW, :].rearrange("(p n) d -> p (n d)", p=P),
                         zeros[:, :]).then_inc(S["zeroed"], 16)
            sp.wait_ge(S["pads_ok"], 1)
            for e in range(NE):
                r = sp.value_load(pad_i[0:1, e:e + 1], min_val=0, max_val=LAST_ROW - P)
                sp.dma_start(y_sorted[bass.ds(r, P), :], zeros[:, 0:P]).then_inc(S["padded"], 16)
            sp.wait_ge(S["zeroed"], 16)
            sp.wait_ge(S["padded"], 16 * NE)


NF = DF // P
PACK = 2 * DF + P
RING = 4
NG = NT // 4


def expert_weights(nc, ctx, w):
    W1, b1, W2, b2, g2, be2 = w
    t = {"first": [P, NE, PACK],
         "w2": [P, NE * DF],
         "g2r": [P, P], "be2r": [P, P]}
    t = {name: ctx.enter_context(nc.sbuf_tensor("e_" + name, shape, F32)) for name, shape in t.items()}
    loads = [(t["first"][:, :, 0:DF], W1.rearrange("e d f -> d e f")),
             (t["w2"][:, :].rearrange("p (c d) -> p c d", d=P), W2.rearrange("e (f p) d -> p (e f) d", p=P)),
             (t["first"][:, :, DF:2 * DF], b1.partition_broadcast(P)),
             (t["first"][:, :, 2 * DF:PACK], b2.partition_broadcast(P)),
             (t["g2r"][:, :], g2.partition_broadcast(P)), (t["be2r"][:, :], be2.partition_broadcast(P))]
    return t, loads


def experts(nc, w, loaded, loads, ident, xs, y_all, sorting, sent, y_sorted, moe_sorted, out):
    with ExitStack() as ctx:
        def sb(name, shape, dt=F32):
            return ctx.enter_context(nc.sbuf_tensor(name, shape, dt))

        def pb(name):
            return [ctx.enter_context(nc.psum_tensor(f"{name}{k}", [P, 512], F32)) for k in range(2)]

        ys = sb("ys", [P, RING, P])
        yT = sb("yT", [P, 2, P])
        hs = sb("hs", [P, 2, DF])
        hT = sb("hT", [P, 2, DF])
        os = sb("os", [P, RING, P])
        own = sb("own", [P, RING, PACK])
        w2s = sb("w2s", [P, 2, DF])
        first_flat = w["first"][:, :, :].rearrange("p e n -> p (e n)")
        moe = sb("moe", [P, NT, P])
        z0 = sb("z0", [P, 2, 4, P])
        z1 = sb("z1", [P, 2, 4, P])
        z2 = sb("z2", [P, 2, 4, P])
        z3 = sb("z3", [P, 2, 4, P])
        st_z = [sb(f"st_z{k}", [P, 4, 6]) for k in range(2)]
        mv_z = [sb(f"mv_z{k}", [P, 4, 2]) for k in range(2)]
        ve_z = [sb(f"ve_z{k}", [P, 4]) for k in range(2)]
        nm_z = [sb(f"nm_z{k}", [P, 4]) for k in range(2)]
        rs_z = [sb(f"rs_z{k}", [P, 4]) for k in range(2)]
        nb_z = [sb(f"nb_z{k}", [P, 4]) for k in range(2)]
        half4 = sb("half4", [P, 4])
        psT, psH, psX, psO = pb("psT"), pb("psH"), pb("psX"), pb("psO")

        names = ["passed", "consts", "ys0", "ys1", "ys2", "ys3", "t_full", "yT_ok", "h_full", "hs_ok", "w1_ok",
                 "w2_ok", "x_full", "hT_ok", "o_full", "os_ok", "st0", "st1", "st2", "st3", "got0", "got1", "z0_ok",
                 "z_mv0", "z_mv1", "z_agg0", "z_agg1", "z_st0", "z_st1", "z_step0", "z_step1", "z_rs0", "z_rs1",
                 "z1_ok", "z2_step", "z2_ok", "z3_ok", "done", "out_ok"]
        S = {n: ctx.enter_context(nc.semaphore("ex_" + n)) for n in names}

        first_i, w2_i, row_i, back_i = sorting

        def guarded(lo, t, hi):
            return not isinstance(t, int) or lo <= t < hi

        block = ctx.enter_context(nc.Block())

        def sorted_tiles(eng, iteration):
            for t in range(RING):
                iteration(t, t)
            loops = (NS - 2) // RING - 1
            with eng.Fori(0, loops) as k:
                for r in range(RING):
                    iteration(k * RING + (RING + r), r)
            for t in range(RING * (loops + 1), NS + 2):
                iteration(t, t % RING)

        def groups(eng, iteration):
            iteration(0, 0)
            iteration(1, 1)
            with eng.Fori(0, (NG - 2) // 2) as k:
                iteration(k * 2 + 2, 0)
                iteration(k * 2 + 3, 1)
            iteration(NG, 0)
            iteration(NG + 1, 1)

        @block.tensor
        def _(pe):
            T = nc.tensor
            pe.wait_ge(loaded, 16 * len(loads))

            def turn(t, m):
                pe.wait_ge(S[f"ys{m % 4}"], (t - m % 4) * 4 + 16)
                pe.wait_ge(S["yT_ok"], count(t - 1))
                T.transpose(psT[m % 2][:, 0:P], ys[:, m % 4, :], ident[:, :]).then_inc(S["t_full"], 1)

            def iteration(t, m):
                if guarded(0, t, NS):
                    pe.wait_ge(S["w1_ok"], t + 1)
                    pe.wait_ge(S["yT_ok"], t + 1)
                    pe.wait_ge(S["hs_ok"], count(t - 1))
                    T.matmul(psH[m % 2][:, :], yT[:, m % 2, :], own[:, m % 4, 0:DF], start=True,
                             stop=True).then_inc(S["h_full"], 1)
                if guarded(0, t + 1, NS):
                    turn(t + 1, (m + 1) % 4)
                if guarded(0, t - 1, NS):
                    pe.wait_ge(S["hs_ok"], t)
                    pe.wait_ge(S["hT_ok"], count(t - 2))
                    for f in range(NF):
                        last = T.transpose(psX[(m - 1) % 2][:, f * P:(f + 1) * P],
                                           hs[:, (m - 1) % 2, f * P:(f + 1) * P], ident[:, :])
                    last.then_inc(S["x_full"], 1)
                if guarded(0, t - 2, NS):
                    pe.wait_ge(S["w2_ok"], t - 1)
                    pe.wait_ge(S["hT_ok"], t - 1)
                    pe.wait_ge(S["os_ok"], count(t - 3))
                    for f in range(NF):
                        last = T.matmul(psO[m % 2][:, 0:P], hT[:, m % 2, f * P:(f + 1) * P],
                                        w2s[:, m % 2, f * P:(f + 1) * P], start=(f == 0), stop=(f == NF - 1))
                    last.then_inc(S["o_full"], 1)

            turn(0, 0)
            sorted_tiles(pe, iteration)

        @block.vector
        def _(dve):
            V = nc.vector
            dve.wait_ge(loaded, 16 * len(loads))

            def pick(t, m):
                e = dve.value_load(first_i[0:1, bass.ds(t, 1)], min_val=0, max_val=(NE - 1) * PACK)
                dve.wait_ge(S["h_full"], count(t - 3))
                dve.wait_ge(S["os_ok"], count(t - 3))
                dve.sem_inc(S["passed"])
                V.tensor_copy(own[:, m % 4, :], first_flat[:, bass.ds(e, PACK)]).then_inc(S["w1_ok"], 1)

            def iteration(t, m):
                if guarded(0, t + 1, NS):
                    pick(t + 1, m + 1)
                if guarded(0, t, NS):
                    dve.wait_ge(S["w1_ok"], t + 1)
                    dve.wait_ge(S["h_full"], t + 1)
                    dve.wait_ge(S["x_full"], count(t - 1))
                    V.tensor_tensor(hs[:, m % 2, :], psH[m % 2][:, :], own[:, m % 4, DF:2 * DF],
                                    ALU.add).then_inc(S["hs_ok"], 1)
                if guarded(0, t - 2, NS):
                    dve.wait_ge(S["o_full"], t - 1)
                    dve.wait_ge(S[f"st{(m - 2) % 4}"], count((t - 2 - (m - 2) % 4) * 4))
                    V.tensor_tensor(os[:, (m - 2) % 4, :], psO[m % 2][:, 0:P], own[:, (m - 2) % 4, 2 * DF:PACK],
                                    ALU.add).then_inc(S["os_ok"], 1)

            pick(0, 0)
            sorted_tiles(dve, iteration)

            def statistics(k, g, src):
                for c in range(4):
                    V.bn_stats(st_z[k][:, c, :], src[:, c, :]).then_inc(S[f"z_st{k}"], 1)
                dve.wait_ge(S[f"z_st{k}"], 4 * g + 4)
                dve.sem_inc(S["passed"])
                for c in range(4):
                    last = V.bn_aggr(mv_z[k][:, c, :], st_z[k][:, c, :])
                last.then_inc(S[f"z_mv{k}"], 1)
                dve.wait_ge(S[f"z_mv{k}"], g + 1)
                V.tensor_scalar(nm_z[k][:, :], mv_z[k][:, :, 0], -1.0, None, ALU.mult)
                V.tensor_scalar(ve_z[k][:, :], mv_z[k][:, :, 1], EPS, None, ALU.add).then_inc(S[f"z_agg{k}"], 1)

            def last_step(t, n):
                if guarded(0, t, NG):
                    dve.wait_ge(S[f"got{n}"], (t - n) * 32 + 64)
                    dve.wait_ge(S["z1_ok"], count(t - 1))
                    V.tensor_tensor(z0[:, n, :, :], y_all[:, bass.ds(t * 4, 4), :], moe[:, bass.ds(t * 4, 4), :],
                                    ALU.add).then_inc(S["z0_ok"], 1)
                    dve.wait_ge(S["z0_ok"], t + 1)
                    dve.wait_ge(S["z_rs0"], count(t))
                    statistics(0, t, z0[:, n, :, :])
                if guarded(0, t - 1, NG):
                    i, o = t - 1, 1 - n
                    dve.wait_ge(S["z1_ok"], i + 1)
                    dve.wait_ge(S["z3_ok"], count(i - 1))
                    V.tensor_tensor(z2[:, o, :, :], z1[:, o, :, :],
                                    w["g2r"][:, :].unsqueeze(1).broadcast_to([P, 4, P]),
                                    ALU.mult).then_inc(S["z2_step"], 1)
                    dve.wait_ge(S["z2_step"], i + 1)
                    V.tensor_tensor(z2[:, o, :, :], z2[:, o, :, :],
                                    w["be2r"][:, :].unsqueeze(1).broadcast_to([P, 4, P]),
                                    ALU.add).then_inc(S["z2_ok"], 1)
                    dve.wait_ge(S["z2_ok"], i + 1)
                    dve.wait_ge(S["z_rs1"], count(i))
                    statistics(1, i, z2[:, o, :, :])
                if guarded(0, t - 2, NG):
                    i = t - 2
                    dve.wait_ge(S["z3_ok"], i + 1)
                    V.tensor_tensor(xs[:, bass.ds(i * 4, 4), :], xs[:, bass.ds(i * 4, 4), :], z3[:, n, :, :],
                                    ALU.add).then_inc(S["done"], 1)

            groups(dve, last_step)

        @block.scalar
        def _(act):
            A = nc.scalar

            def turned(t, m):
                act.wait_ge(S["t_full"], t + 1)
                act.wait_ge(S["h_full"], count(t - 1))
                A.activation(yT[:, m % 2, :], psT[m % 2][:, 0:P], ACT.Copy).then_inc(S["yT_ok"], 1)

            def store(t, m):
                act.wait_ge(S["os_ok"], t + 1)
                act.dma_start(moe_sorted[bass.ds(t * P, P), :], os[:, m % 4, :]).then_inc(S[f"st{m % 4}"], 16)

            def iteration(t, m):
                if guarded(0, t + 1, NS):
                    turned(t + 1, (m + 1) % 4)
                if guarded(0, t - 1, NS):
                    act.wait_ge(S["x_full"], t)
                    act.wait_ge(S["o_full"], count(t - 2))
                    A.activation(hT[:, (m - 1) % 2, :], psX[(m - 1) % 2][:, :], ACT.Relu).then_inc(S["hT_ok"], 1)
                    e = act.value_load(w2_i[0:1, bass.ds(t - 1, 1)], min_val=0, max_val=(NE - 1) * DF)
                    A.activation(w2s[:, (m - 1) % 2, :], w["w2"][:, bass.ds(e, DF)],
                                 ACT.Copy).then_inc(S["w2_ok"], 1)
                if guarded(0, t - 2, NS):
                    store(t - 2, (m - 2) % 4)

            act.wait_ge(loaded, 16 * len(loads))
            turned(0, 0)
            sorted_tiles(act, iteration)

            def apply(k, dst, src):
                for c in range(4):
                    last = A.activation(dst[:, c, :], src[:, c, :], ACT.Identity, bias=nb_z[k][:, c:c + 1],
                                        scale=rs_z[k][:, c:c + 1])
                return last

            def last_step(t, n):
                if guarded(0, t, NG):
                    act.wait_ge(S["z_rs0"], t + 1)
                    act.wait_ge(S["z2_step"], count(t - 1))
                    apply(0, z1[:, n, :, :], z0[:, n, :, :]).then_inc(S["z1_ok"], 1)
                if guarded(0, t - 1, NG):
                    act.wait_ge(S["z_rs1"], t)
                    act.wait_ge(S["done"], count(t - 2))
                    apply(1, z3[:, 1 - n, :, :], z2[:, 1 - n, :, :]).then_inc(S["z3_ok"], 1)

            groups(act, last_step)

        @block.gpsimd
        def _(pool):
            G = nc.gpsimd
            G.memset(half4[:, :], -0.5).then_inc(S["consts"], 1)
            pool.wait_ge(S["consts"], 1)
            for m in range(RING):
                pool.wait_ge(S[f"st{m}"], 16 * len(range(m, NS, RING)))

            def gather(g, n):
                if isinstance(g, int) and g >= 2:
                    pool.wait_ge(S["z0_ok"], g - 1)
                for c in range(4):
                    G.indirect_dma_start(moe[:, 4 * g + c, :], None, moe_sorted,
                                         bass.IndirectOffsetOnAxis(back_i[:, 4 * g + c:4 * g + c + 1], 0)
                                         ).then_inc(S[f"got{n}"], 16)

            def scale(k, g):
                pool.wait_ge(S[f"z_agg{k}"], g + 1)
                if g >= 1:
                    pool.wait_ge(S[f"z{2 * k + 1}_ok"], g)
                G.tensor_tensor(rs_z[k][:, :], ve_z[k][:, :], half4[:, :], ALU.pow).then_inc(S[f"z_step{k}"], 1)
                pool.wait_ge(S[f"z_step{k}"], g + 1)
                G.tensor_tensor(nb_z[k][:, :], nm_z[k][:, :], rs_z[k][:, :], ALU.mult).then_inc(S[f"z_rs{k}"], 1)

            gather(0, 0)
            gather(1, 1)
            for t in range(NG + 1):
                if t < NG:
                    scale(0, t)
                if t + 2 < NG:
                    gather(t + 2, t % 2)
                if t >= 1:
                    scale(1, t - 1)

        @block.sync
        def _(sp):
            def load(t, m):
                sp.wait_ge(S["t_full"], count(t - (RING - 1)))
                r = sp.value_load(row_i[0:1, bass.ds(t, 1)], min_val=0, max_val=LAST_ROW - P)
                sp.dma_start(ys[:, m % 4, :], y_sorted[bass.ds(r, P), :]).then_inc(S[f"ys{m % 4}"], 16)

            sp.wait_ge(sent, 16 * NT)
            for t in range(RING):
                load(t, t)
            with sp.Fori(0, NS // RING - 1) as k:
                for r in range(RING):
                    load(k * RING + (RING + r), r)
            for t in range(NS // RING * RING, NS):
                load(t, t % RING)
            out_t = out.rearrange("(q r) l d -> q (r l d)", q=B1).rearrange("q (b n) -> (q b) n", b=8)
            for g in range(NG):
                sp.wait_ge(S["done"], g + 1)
                sp.dma_start(out_t[:, 4 * g * P:4 * (g + 1) * P],
                             xs[:, 4 * g:4 * g + 4, :].rearrange("p c d -> p (c d)")).then_inc(S["out_ok"], 16)
            sp.wait_ge(S["out_ok"], 16 * NG)


def build_program(nc, a, out):
    with ExitStack() as ctx:
        ident = ctx.enter_context(nc.sbuf_tensor("ident", [P, P], F32))
        identh = ctx.enter_context(nc.sbuf_tensor("identh", [P, P], BF16))
        minus_half = ctx.enter_context(nc.sbuf_tensor("minus_half", [P, 2], F32))
        xs = ctx.enter_context(nc.sbuf_tensor("xs", [P, NT, P], F32))
        y_sorted = nc.dram_tensor("y_sorted", (LAST_ROW, P), F32).ap()
        moe_sorted = nc.dram_tensor("moe_sorted", (NS * P, P), F32).ap()
        loaded2 = ctx.enter_context(nc.semaphore("loaded2"))
        parameters, loads2 = attention_parameters(nc, ctx, [a[k] for k in ("Wqkv", "bqkv", "Wo", "bo", "g1", "be1",
                                                                           "Wg")])
        first_layer(nc, a["x"], a["w_qkv"], a["b_qkv"], a["w_o"], a["b_o"], ident, identh, minus_half, xs, loads2,
                    loaded2)
        y_all = ctx.enter_context(nc.sbuf_tensor("y_all", [P, NT, P], F32))
        logits = ctx.enter_context(nc.sbuf_tensor("logits", [P, NT, NE], F32))
        slots = ctx.enter_context(nc.sbuf_tensor("slots", [P, NT], F32))
        slot_i = ctx.enter_context(nc.sbuf_tensor("slot_i", [P, NT], I32))
        base = ctx.enter_context(nc.sbuf_tensor("base", [P, NE], F32))
        sorting = [ctx.enter_context(nc.sbuf_tensor(name, [P, n], I32))
                   for name, n in (("first_i", NS), ("w2_i", NS), ("row_i", NS), ("back_i", NT))]
        sent = ctx.enter_context(nc.semaphore("sent"))
        loaded = ctx.enter_context(nc.semaphore("loaded"))
        w, loads = expert_weights(nc, ctx, [a[k] for k in ("W1", "b1", "W2", "b2", "g2", "be2")])
        second_attention(nc, parameters, loaded2, loads2, ident, identh,
                         minus_half, xs, y_all, logits, loaded, loads, y_sorted, slots, slot_i, base, sorting, sent)
        experts(nc, w, loaded, loads, ident, xs, y_all, sorting, sent, y_sorted, moe_sorted, out)


def kernel(L0_attn_x, L0_attn_w_qkv, L0_attn_b_qkv, L0_attn_w_o, L0_attn_b_o, L0_ffn_Wqkv, L0_ffn_bqkv, L0_ffn_Wo,
           L0_ffn_bo, L0_ffn_g1, L0_ffn_be1, L0_ffn_g2, L0_ffn_be2, L0_ffn_Wg, L0_ffn_W1, L0_ffn_b1, L0_ffn_W2,
           L0_ffn_b2):
    import numpy as np
    import concourse.bacc as bacc
    from concourse.bass_utils import run_bass_kernel_spmd

    given = {"x": L0_attn_x, "w_qkv": L0_attn_w_qkv, "b_qkv": L0_attn_b_qkv, "w_o": L0_attn_w_o, "b_o": L0_attn_b_o,
             "Wqkv": L0_ffn_Wqkv, "bqkv": L0_ffn_bqkv, "Wo": L0_ffn_Wo, "bo": L0_ffn_bo, "g1": L0_ffn_g1,
             "be1": L0_ffn_be1, "g2": L0_ffn_g2, "be2": L0_ffn_be2, "Wg": L0_ffn_Wg, "W1": L0_ffn_W1,
             "b1": L0_ffn_b1, "W2": L0_ffn_W2, "b2": L0_ffn_b2}
    nc = bacc.Bacc("TRN2", target_bir_lowering=False, num_devices=1)
    arrays, args = {}, {}
    for name, array in given.items():
        arrays[name] = np.ascontiguousarray(array)
        args[name] = nc.dram_tensor(name, arrays[name].shape, mybir.dt.from_np(arrays[name].dtype),
                                    kind="ExternalInput").ap()
    out = nc.dram_tensor("out", (B1, L1, P), F32, kind="ExternalOutput").ap()
    build_program(nc, args, out)
    r = run_bass_kernel_spmd(nc, [arrays], core_ids=[0])
    return r.results[0]["out"]
```
